# Optimizing a Trainium2 kernel written in Bass

```python
import numpy as np
import jax
import jax.numpy as jnp

def _softmax(x, axis=-1):
    return jax.nn.softmax(x, axis=axis)

def _gelu(x):
    return jax.nn.gelu(x, approximate=True)

def _silu(x):
    return jax.nn.silu(x)

def _sigmoid(x):
    return jax.nn.sigmoid(x)

def _layernorm(x, axis=-1, eps=1e-05):
    m = jnp.mean(x, axis=axis, keepdims=True)
    v = jnp.var(x, axis=axis, keepdims=True)
    return (x - m) / jnp.sqrt(v + eps)

def _scatter_add(tgt, idx, src, axis=0):
    return tgt.at[idx].add(src)

def _segment_sum(src, seg, n):
    return jax.ops.segment_sum(src, seg, n)
kernel_name = 'mk_xattn_ffn_d4_seqx_r4_135bb7'

def setup_inputs(seed: int=0):
    np.random.seed(seed)
    _w = jnp.asarray

    def _rec_inputs():
        import jax
        import jax.numpy as jnp
        _rk = jax.random.key(seed)
        x = -1.394e-06 + 0.9999 * jax.random.normal(jax.random.fold_in(_rk, 1), (16, 112, 256), jnp.float32)
        _lenS = 112 - jax.random.randint(jax.random.fold_in(_rk, 7), (16,), 0, max(1, 112 // 4) + 1, jnp.int32)
        _lenS2 = 375 - jax.random.randint(jax.random.fold_in(_rk, 8), (16,), 0, max(1, 375 // 4) + 1, jnp.int32)
        _ctx_1024P = jax.random.normal(jax.random.fold_in(_rk, 11), (16, 16, 256), jnp.float32)
        _ctx_1024c = jax.random.dirichlet(jax.random.fold_in(_rk, 511), 0.3 * jnp.ones((16,), jnp.float32), (16, 375))
        _ctx_1024t = jnp.einsum('bsk,bkd->bsd', _ctx_1024c, _ctx_1024P)
        _ctx_1024t = _ctx_1024t * jax.lax.rsqrt(jnp.mean(jnp.square(_ctx_1024t)) + 1e-12) * 0.953939
        ctx_1024 = -0.000292821 + 1.00034 * (_ctx_1024t + 0.3 * jax.random.normal(jax.random.fold_in(_rk, 611), (16, 375, 256), jnp.float32))
        _validS = jnp.arange(112)[None, :] < _lenS[:, None]
        _validS2 = jnp.arange(375)[None, :] < _lenS2[:, None]
        _causal = jnp.tril(jnp.ones((112, 112), dtype=bool))
        mask_BxSxS2_bk1 = jnp.broadcast_to(_validS2[:, None, :], (16, 112, 375))
        mask_Bx1xS2_ik0 = jnp.where(jnp.broadcast_to(_validS2[:, None, :], (16, 1, 375)), 0, 1).astype(jnp.int32)
        return (x, ctx_1024, mask_BxSxS2_bk1, mask_Bx1xS2_ik0)
    x, ctx_1024, mask_BxSxS2_bk1, mask_Bx1xS2_ik0 = _rec_inputs()

    def _L0_xattn_setup():
        import jax, jax.numpy as jnp
        import numpy as np
        D_MODEL = 256
        N_HEAD = 16
        HEAD_DIM = D_MODEL // N_HEAD
        key = jax.random.key(seed)
        ks = jax.random.split(key, 9)
        B, T = (2, 512)
        s = 0.02
        return {'k': jax.random.normal(ks[0], (B, T, D_MODEL), jnp.float32), 'q': jax.random.normal(ks[1], (B, T, D_MODEL), jnp.float32), 'v': jax.random.normal(ks[2], (B, T, D_MODEL), jnp.float32), 'Wk': jax.random.normal(ks[3], (D_MODEL, D_MODEL), jnp.float32) * s, 'bk': jnp.zeros((D_MODEL,), jnp.float32), 'Wq': jax.random.normal(ks[4], (D_MODEL, D_MODEL), jnp.float32) * s, 'bq': jnp.zeros((D_MODEL,), jnp.float32), 'Wc': jax.random.normal(ks[5], (D_MODEL, D_MODEL), jnp.float32) * s, 'bc': jnp.zeros((D_MODEL,), jnp.float32)}
    _L0_xattn_all = _L0_xattn_setup()
    _L0_xattn_in = {k: v for k, v in _L0_xattn_all.items() if k in ('Wk', 'bk', 'Wq', 'bq', 'Wc', 'bc')}
    del _L0_xattn_all

    def _L0_ffn_setup():
        import jax, jax.numpy as jnp
        import numpy as np
        B, S, D, E, F = (2, 512, 256, 8, 1024)
        key = jax.random.key(seed)
        ks = jax.random.split(key, 4)
        return {'hidden_states': jax.random.normal(ks[0], (B, S, D), dtype=jnp.float32), 'Wr': jax.random.normal(ks[1], (D, E), dtype=jnp.float32) * (1.0 / np.sqrt(D)), 'W1': jax.random.normal(ks[2], (E, D, F), dtype=jnp.float32) * (1.0 / np.sqrt(D)), 'b1': jnp.zeros((E, F), dtype=jnp.float32), 'W2': jax.random.normal(ks[3], (E, F, D), dtype=jnp.float32) * (1.0 / np.sqrt(F)), 'b2': jnp.zeros((E, D), dtype=jnp.float32)}
    _L0_ffn_all = _L0_ffn_setup()
    _L0_ffn_in = {k: v for k, v in _L0_ffn_all.items() if k in ('Wr', 'W1', 'b1', 'W2', 'b2')}
    del _L0_ffn_all

    def _L1_xattn_setup():
        import jax, jax.numpy as jnp
        import numpy as np
        B, L, HID, H, DH, M = (4, 1024, 256, 16, 64, 128)
        EPS = 0.001

        def _relu_kernel(x, proj):
            ratio = 1.0 / float(np.sqrt(proj.shape[0]))
            return jax.nn.relu(ratio * jnp.einsum('blhd,md->blhm', x, proj)) + EPS
        key = jax.random.key(seed)
        ks = jax.random.split(key, 7)
        lim = float(np.sqrt(6.0 / (HID + HID)))
        return {'query_input': jax.random.normal(ks[0], (B, L, HID), jnp.float32), 'source_input': jax.random.normal(ks[1], (B, L, HID), jnp.float32), 'Wq': jax.random.uniform(ks[2], (HID, H, DH), jnp.float32, -lim, lim), 'Wk': jax.random.uniform(ks[3], (HID, H, DH), jnp.float32, -lim, lim), 'Wv': jax.random.uniform(ks[4], (HID, H, DH), jnp.float32, -lim, lim), 'Wo': jax.random.uniform(ks[5], (H, DH, HID), jnp.float32, -lim, lim), 'proj': jax.random.normal(ks[6], (M, DH), jnp.float32), 'training': 0}
    _L1_xattn_all = _L1_xattn_setup()
    _L1_xattn_in = {k: v for k, v in _L1_xattn_all.items() if k in ('Wq', 'Wk', 'Wv', 'Wo', 'proj')}
    del _L1_xattn_all

    def _L1_ffn_setup():
        import jax, jax.numpy as jnp
        import numpy as np
        D_MODEL = 256
        D_FF = 1024
        N_EXPERTS = 8
        D_EXPERT = D_FF // N_EXPERTS
        TOP_K = 2
        LB_WEIGHT = 0.01
        B, S = (4, 512)

        def _top_k_softmax(logits, k):
            vals, _ = jax.lax.top_k(logits, k)
            thresh = vals[..., -1:]
            masked = jnp.where(logits >= thresh, logits, -jnp.inf)
            return jax.nn.softmax(masked, axis=-1)
        key = jax.random.key(seed)
        ks = jax.random.split(key, 8)
        x = jax.random.normal(ks[0], (B, S, D_MODEL), dtype=jnp.float32)
        w1 = jax.random.normal(ks[1], (N_EXPERTS, D_MODEL, D_EXPERT), dtype=jnp.float32) * (1.0 / np.sqrt(D_MODEL))
        b1 = jnp.zeros((N_EXPERTS, D_EXPERT), dtype=jnp.float32)
        w2 = jax.random.normal(ks[2], (N_EXPERTS, D_EXPERT, D_MODEL), dtype=jnp.float32) * (1.0 / np.sqrt(D_EXPERT))
        b2 = jnp.zeros((N_EXPERTS, D_MODEL), dtype=jnp.float32)
        centroids = jax.random.normal(ks[3], (N_EXPERTS, D_MODEL), dtype=jnp.float32) * 0.02
        w_route = jax.random.normal(ks[4], (N_EXPERTS, D_MODEL), dtype=jnp.float32) * (1.0 / np.sqrt(D_MODEL))
        return {'x': x, 'w1': w1, 'b1': b1, 'w2': w2, 'b2': b2, 'centroids': centroids, 'w_route': w_route}
    _L1_ffn_all = _L1_ffn_setup()
    _L1_ffn_in = {k: v for k, v in _L1_ffn_all.items() if k in ('w1', 'b1', 'w2', 'b2', 'centroids', 'w_route')}
    del _L1_ffn_all

    def _L2_xattn_setup():
        import jax, jax.numpy as jnp
        import numpy as np
        DIM = 256
        HEADS = 16
        DIM_HEAD = 64
        INNER = HEADS * DIM_HEAD
        B, N = (2, 512)
        key = jax.random.key(seed)
        ks = jax.random.split(key, 8)
        q = jax.random.normal(ks[0], (B, N, DIM), dtype=jnp.float32)
        k = jax.random.normal(ks[1], (B, N, DIM), dtype=jnp.float32)
        v = jax.random.normal(ks[2], (B, N, DIM), dtype=jnp.float32)
        causal = jnp.triu(jnp.ones((N, N), dtype=jnp.bool_), k=1)
        mask = jnp.broadcast_to(causal, (B, N, N))
        s = 0.02
        Wq = jax.random.normal(ks[3], (DIM, INNER), dtype=jnp.float32) * s
        Wk = jax.random.normal(ks[4], (DIM, INNER), dtype=jnp.float32) * s
        Wv = jax.random.normal(ks[5], (DIM, INNER), dtype=jnp.float32) * s
        Wo = jax.random.normal(ks[6], (INNER, DIM), dtype=jnp.float32) * s
        bo = jnp.zeros((DIM,), dtype=jnp.float32)
        return {'q': q, 'k': k, 'v': v, 'mask': mask, 'Wq': Wq, 'Wk': Wk, 'Wv': Wv, 'Wo': Wo, 'bo': bo}
    _L2_xattn_all = _L2_xattn_setup()
    _L2_xattn_in = {k: v for k, v in _L2_xattn_all.items() if k in ('Wq', 'Wk', 'Wv', 'Wo', 'bo')}
    del _L2_xattn_all

    def _L2_ffn_setup():
        import jax, jax.numpy as jnp
        import numpy as np
        B, F, D, H, E, K = (4, 512, 256, 512, 8, 2)
        key = jax.random.key(seed)
        ks = jax.random.split(key, 9)
        sc = lambda k, shape, fan_in: jax.random.normal(k, shape, jnp.float32) * fan_in ** (-0.5)
        return {'x': jax.random.normal(ks[0], (B, F, D), jnp.float32), 'rw1': sc(ks[1], (D, D), D), 'rb1': jnp.zeros((D,), jnp.float32), 'rw2': sc(ks[2], (D, E), D), 'rb2': jnp.zeros((E,), jnp.float32), 'ew1': sc(ks[3], (E, D, H), D), 'eb1': jnp.zeros((E, H), jnp.float32), 'ew2': sc(ks[4], (E, H, D), H), 'eb2': jnp.zeros((E, D), jnp.float32)}
    _L2_ffn_all = _L2_ffn_setup()
    _L2_ffn_in = {k: v for k, v in _L2_ffn_all.items() if k in ('rw1', 'rb1', 'rw2', 'rb2', 'ew1', 'eb1', 'ew2', 'eb2')}
    del _L2_ffn_all

    def _L3_xattn_setup():
        import jax, jax.numpy as jnp
        import numpy as np
        B, SQ, SK = (2, 512, 512)
        DQ = DK = DV = DM = DOUT = 256
        H = 16
        DHEAD = DM // H
        key = jax.random.key(seed)
        ks = jax.random.split(key, 12)
        s = 0.02
        return {'Q': jax.random.normal(ks[0], (B, SQ, DQ), jnp.float32), 'K': jax.random.normal(ks[1], (B, SK, DK), jnp.float32), 'V': jax.random.normal(ks[2], (B, SK, DV), jnp.float32), 'mask': jax.random.randint(ks[3], (B, 1, SK), 0, 2, jnp.int32), 'Wq': jax.random.normal(ks[4], (DQ, DM), jnp.float32) * s, 'bq': jnp.zeros((DM,), jnp.float32), 'Wk': jax.random.normal(ks[5], (DK, DM), jnp.float32) * s, 'bk': jnp.zeros((DM,), jnp.float32), 'Wv': jax.random.normal(ks[6], (DV, DM), jnp.float32) * s, 'bv': jnp.zeros((DM,), jnp.float32), 'Wo': jax.random.normal(ks[7], (DM, DOUT), jnp.float32) * s, 'bo': jnp.zeros((DOUT,), jnp.float32)}
    _L3_xattn_all = _L3_xattn_setup()
    _L3_xattn_in = {k: v for k, v in _L3_xattn_all.items() if k in ('Wq', 'bq', 'Wk', 'bk', 'Wv', 'bv', 'Wo', 'bo')}
    del _L3_xattn_all

    def _L3_ffn_setup():
        import jax, jax.numpy as jnp
        import numpy as np
        H = 256
        I = 256
        E = 8
        key = jax.random.key(seed)
        ks = jax.random.split(key, 8)
        s = 0.02
        x = jax.random.normal(ks[0], (4, 512, H), dtype=jnp.float32)
        Wg = jax.random.normal(ks[1], (H, E), dtype=jnp.float32) * s
        bg = jnp.zeros((E,), dtype=jnp.float32)
        W1 = jax.random.normal(ks[2], (E, H, I), dtype=jnp.float32) * s
        b1 = jnp.zeros((E, I), dtype=jnp.float32)
        W2 = jax.random.normal(ks[3], (E, I, H), dtype=jnp.float32) * s
        b2 = jnp.zeros((E, H), dtype=jnp.float32)
        return {'x': x, 'Wg': Wg, 'bg': bg, 'W1': W1, 'b1': b1, 'W2': W2, 'b2': b2}
    _L3_ffn_all = _L3_ffn_setup()
    _L3_ffn_in = {k: v for k, v in _L3_ffn_all.items() if k in ('Wg', 'bg', 'W1', 'b1', 'W2', 'b2')}
    del _L3_ffn_all
    return {'x': x, 'ctx_1024': ctx_1024, 'mask_BxSxS2_bk1': mask_BxSxS2_bk1, 'mask_Bx1xS2_ik0': mask_Bx1xS2_ik0, 'L0_xattn_Wk': _L0_xattn_in['Wk'], 'L0_xattn_bk': _L0_xattn_in['bk'], 'L0_xattn_Wq': _L0_xattn_in['Wq'], 'L0_xattn_bq': _L0_xattn_in['bq'], 'L0_xattn_Wc': _L0_xattn_in['Wc'], 'L0_xattn_bc': _L0_xattn_in['bc'], 'L0_ffn_Wr': _L0_ffn_in['Wr'], 'L0_ffn_W1': _L0_ffn_in['W1'], 'L0_ffn_b1': _L0_ffn_in['b1'], 'L0_ffn_W2': _L0_ffn_in['W2'], 'L0_ffn_b2': _L0_ffn_in['b2'], 'L1_xattn_Wq': _L1_xattn_in['Wq'], 'L1_xattn_Wk': _L1_xattn_in['Wk'], 'L1_xattn_Wv': _L1_xattn_in['Wv'], 'L1_xattn_Wo': _L1_xattn_in['Wo'], 'L1_xattn_proj': _L1_xattn_in['proj'], 'L1_ffn_w1': _L1_ffn_in['w1'], 'L1_ffn_b1': _L1_ffn_in['b1'], 'L1_ffn_w2': _L1_ffn_in['w2'], 'L1_ffn_b2': _L1_ffn_in['b2'], 'L1_ffn_centroids': _L1_ffn_in['centroids'], 'L1_ffn_w_route': _L1_ffn_in['w_route'], 'L2_xattn_Wq': _L2_xattn_in['Wq'], 'L2_xattn_Wk': _L2_xattn_in['Wk'], 'L2_xattn_Wv': _L2_xattn_in['Wv'], 'L2_xattn_Wo': _L2_xattn_in['Wo'], 'L2_xattn_bo': _L2_xattn_in['bo'], 'L2_ffn_rw1': _L2_ffn_in['rw1'], 'L2_ffn_rb1': _L2_ffn_in['rb1'], 'L2_ffn_rw2': _L2_ffn_in['rw2'], 'L2_ffn_rb2': _L2_ffn_in['rb2'], 'L2_ffn_ew1': _L2_ffn_in['ew1'], 'L2_ffn_eb1': _L2_ffn_in['eb1'], 'L2_ffn_ew2': _L2_ffn_in['ew2'], 'L2_ffn_eb2': _L2_ffn_in['eb2'], 'L3_xattn_Wq': _L3_xattn_in['Wq'], 'L3_xattn_bq': _L3_xattn_in['bq'], 'L3_xattn_Wk': _L3_xattn_in['Wk'], 'L3_xattn_bk': _L3_xattn_in['bk'], 'L3_xattn_Wv': _L3_xattn_in['Wv'], 'L3_xattn_bv': _L3_xattn_in['bv'], 'L3_xattn_Wo': _L3_xattn_in['Wo'], 'L3_xattn_bo': _L3_xattn_in['bo'], 'L3_ffn_Wg': _L3_ffn_in['Wg'], 'L3_ffn_bg': _L3_ffn_in['bg'], 'L3_ffn_W1': _L3_ffn_in['W1'], 'L3_ffn_b1': _L3_ffn_in['b1'], 'L3_ffn_W2': _L3_ffn_in['W2'], 'L3_ffn_b2': _L3_ffn_in['b2']}

def reference(x, ctx_1024, mask_BxSxS2_bk1, mask_Bx1xS2_ik0, L0_xattn_Wk, L0_xattn_bk, L0_xattn_Wq, L0_xattn_bq, L0_xattn_Wc, L0_xattn_bc, L0_ffn_Wr, L0_ffn_W1, L0_ffn_b1, L0_ffn_W2, L0_ffn_b2, L1_xattn_Wq, L1_xattn_Wk, L1_xattn_Wv, L1_xattn_Wo, L1_xattn_proj, L1_ffn_w1, L1_ffn_b1, L1_ffn_w2, L1_ffn_b2, L1_ffn_centroids, L1_ffn_w_route, L2_xattn_Wq, L2_xattn_Wk, L2_xattn_Wv, L2_xattn_Wo, L2_xattn_bo, L2_ffn_rw1, L2_ffn_rb1, L2_ffn_rw2, L2_ffn_rb2, L2_ffn_ew1, L2_ffn_eb1, L2_ffn_ew2, L2_ffn_eb2, L3_xattn_Wq, L3_xattn_bq, L3_xattn_Wk, L3_xattn_bk, L3_xattn_Wv, L3_xattn_bv, L3_xattn_Wo, L3_xattn_bo, L3_ffn_Wg, L3_ffn_bg, L3_ffn_W1, L3_ffn_b1, L3_ffn_W2, L3_ffn_b2):
    import jax
    import jax.numpy as jnp

    def _L0_xattn_ref(k, q, v, Wk, bk, Wq, bq, Wc, bc):
        import jax, jax.numpy as jnp
        import numpy as np
        D_MODEL = 256
        N_HEAD = 16
        HEAD_DIM = D_MODEL // N_HEAD
        B, T_v, C = v.shape
        T_q = q.shape[1]
        H, hd = (N_HEAD, C // N_HEAD)
        kp = k @ Wk.T + bk
        qp = q @ Wq.T + bq
        kh = kp.reshape(B, T_v, H, hd).transpose(0, 2, 1, 3)
        qh = qp.reshape(B, T_q, H, hd).transpose(0, 2, 1, 3)
        vh = v.reshape(B, T_v, H, hd).transpose(0, 2, 1, 3)
        scale = 1.0 / jnp.sqrt(jnp.asarray(hd, kh.dtype))
        att = jnp.einsum('bhqd,bhkd->bhqk', qh, kh) * scale
        att = jax.nn.softmax(att, axis=-1)
        y = jnp.einsum('bhqk,bhkd->bhqd', att, vh)
        y = y.transpose(0, 2, 1, 3).reshape(B, T_q, C)
        return y @ Wc.T + bc

    def _L0_ffn_ref(hidden_states, Wr, W1, b1, W2, b2):
        import jax, jax.numpy as jnp
        import numpy as np
        B, S, D, E, F = (2, 512, 256, 8, 1024)
        b, s, d = hidden_states.shape
        e = Wr.shape[1]
        x = hidden_states.reshape(b * s, d)
        router_logits = x @ Wr
        router_probs = jax.nn.softmax(router_logits, axis=-1)
        expert_idx = jnp.argmax(router_probs, axis=-1)
        p_max = jnp.max(router_probs, axis=-1, keepdims=True)

        def expert_mlp(w1, bb1, w2, bb2):
            h = jax.nn.gelu(x @ w1 + bb1, approximate=False)
            return h @ w2 + bb2
        outs = jax.vmap(expert_mlp)(W1, b1, W2, b2)
        onehot = jax.nn.one_hot(expert_idx, e, dtype=x.dtype)
        next_states = jnp.einsum('te,etd->td', onehot, outs)
        out = p_max * next_states
        return out.reshape(b, s, d)

    def _L1_xattn_ref(query_input, source_input, Wq, Wk, Wv, Wo, proj, training):
        import jax, jax.numpy as jnp
        import numpy as np
        B, L, HID, H, DH, M = (4, 1024, 256, 16, 64, 128)
        EPS = 0.001

        def _relu_kernel(x, proj):
            ratio = 1.0 / float(np.sqrt(proj.shape[0]))
            return jax.nn.relu(ratio * jnp.einsum('blhd,md->blhm', x, proj)) + EPS
        q = jnp.einsum('bld,dhk->blhk', query_input, Wq)
        k = jnp.einsum('bld,dhk->blhk', source_input, Wk)
        v = jnp.einsum('bld,dhk->blhk', source_input, Wv)
        qp = _relu_kernel(q, proj)
        kp = _relu_kernel(k, proj)
        kvs = jnp.einsum('blhm,blhd->bhmd', kp, v)
        num = jnp.einsum('blhm,bhmd->blhd', qp, kvs)
        ks_sum = jnp.sum(kp, axis=1)
        den = jnp.einsum('blhm,bhm->blh', qp, ks_sum)
        att = num / den[..., None]
        return jnp.einsum('blhd,hdk->blk', att, Wo)

    def _L1_ffn_ref(x, w1, b1, w2, b2, centroids, w_route):
        import jax, jax.numpy as jnp
        import numpy as np
        D_MODEL = 256
        D_FF = 1024
        N_EXPERTS = 8
        D_EXPERT = D_FF // N_EXPERTS
        TOP_K = 2
        LB_WEIGHT = 0.01
        B, S = (4, 512)

        def _top_k_softmax(logits, k):
            vals, _ = jax.lax.top_k(logits, k)
            thresh = vals[..., -1:]
            masked = jnp.where(logits >= thresh, logits, -jnp.inf)
            return jax.nn.softmax(masked, axis=-1)
        eps = 1e-12
        x_norm = x / jnp.maximum(jnp.linalg.norm(x, axis=-1, keepdims=True), eps)
        c_norm = centroids / jnp.maximum(jnp.linalg.norm(centroids, axis=-1, keepdims=True), eps)
        cos_scores = jnp.einsum('bsd,ed->bse', x_norm, c_norm)
        route_scores = jnp.einsum('bsd,ed->bse', x, w_route)
        logits = cos_scores + route_scores
        gates = _top_k_softmax(logits, TOP_K)
        h = jax.nn.gelu(jnp.einsum('bsd,edh->bseh', x, w1) + b1, approximate=False)
        expert_out = jnp.einsum('bseh,ehd->bsed', h, w2) + b2
        out = jnp.einsum('bse,bsed->bsd', gates, expert_out)
        return out

    def _L2_xattn_ref(q, k, v, mask, Wq, Wk, Wv, Wo, bo):
        import jax, jax.numpy as jnp
        import numpy as np
        DIM = 256
        HEADS = 16
        DIM_HEAD = 64
        INNER = HEADS * DIM_HEAD
        B, N = (2, 512)
        h, d = (HEADS, DIM_HEAD)
        scale = d ** (-0.5)
        b, n, _ = q.shape

        def heads_split(x):
            return x.reshape(b, -1, h, d).transpose(0, 2, 1, 3)
        qh = heads_split(q @ Wq)
        kh = heads_split(k @ Wk)
        vh = heads_split(v @ Wv)
        dots = jnp.einsum('bhid,bhjd->bhij', qh, kh) * scale
        mask_value = -jnp.finfo(dots.dtype).max
        dots = jnp.where(mask[:, None, :, :], mask_value, dots)
        attn = jax.nn.softmax(dots, axis=-1)
        out = jnp.einsum('bhij,bhjd->bhid', attn, vh)
        out = out.transpose(0, 2, 1, 3).reshape(b, n, h * d)
        out = out @ Wo + bo
        return out

    def _L2_ffn_ref(x, rw1, rb1, rw2, rb2, ew1, eb1, ew2, eb2):
        import jax, jax.numpy as jnp
        import numpy as np
        B, F, D, H, E, K = (4, 512, 256, 512, 8, 2)
        b, f, d = x.shape
        t = x.reshape(b * f, d)
        logits = jax.nn.silu(t @ rw1 + rb1) @ rw2 + rb2
        vals, idx = jax.lax.top_k(logits, K)
        rows = jnp.arange(t.shape[0])[:, None]
        masked = jnp.full_like(logits, -jnp.inf).at[rows, idx].set(vals)
        w = jax.nn.softmax(masked, axis=1)
        eh = jax.nn.silu(jnp.einsum('td,edh->teh', t, ew1) + eb1[None])
        eo = jnp.einsum('teh,ehd->ted', eh, ew2) + eb2[None]
        y = t + jnp.einsum('te,ted->td', w, eo)
        return y.reshape(b, f, d)

    def _L3_xattn_ref(Q, K, V, mask, Wq, bq, Wk, bk, Wv, bv, Wo, bo):
        import jax, jax.numpy as jnp
        import numpy as np
        B, SQ, SK = (2, 512, 512)
        DQ = DK = DV = DM = DOUT = 256
        H = 16
        DHEAD = DM // H
        b, sq, _ = Q.shape
        q = (Q @ Wq + bq).reshape(b, sq, H, DHEAD).transpose(0, 2, 1, 3)
        k = (K @ Wk + bk).reshape(b, -1, H, DHEAD).transpose(0, 2, 1, 3)
        v = (V @ Wv + bv).reshape(b, -1, H, DHEAD).transpose(0, 2, 1, 3)
        scores = jnp.einsum('bhqd,bhkd->bhqk', q, k) / np.sqrt(DHEAD).astype(np.float32)
        m = mask[:, None]
        scores = jnp.where(m == 0, -jnp.inf, scores)
        attn = jax.nn.softmax(scores, axis=-1)
        out = jnp.einsum('bhqk,bhkd->bhqd', attn, v)
        out = out.transpose(0, 2, 1, 3).reshape(b, sq, DM)
        return out @ Wo + bo

    def _L3_ffn_ref(x, Wg, bg, W1, b1, W2, b2):
        import jax, jax.numpy as jnp
        import numpy as np
        H = 256
        I = 256
        E = 8
        B, S, Hd = x.shape
        xf = x.reshape(-1, Hd)
        logits = xf @ Wg + bg
        gates = jax.nn.softmax(logits, axis=-1)
        idx = jnp.argmax(gates, axis=-1)
        h = jax.nn.gelu(jnp.einsum('th,ehi->tei', xf, W1) + b1, approximate=False)
        y = jnp.einsum('tei,eih->teh', h, W2) + b2
        out = jnp.take_along_axis(y, idx[:, None, None], axis=1)[:, 0, :]
        return out.reshape(B, S, Hd)
    x = x + _L0_xattn_ref(ctx_1024, _layernorm(x, axis=-1), ctx_1024, L0_xattn_Wk, L0_xattn_bk, L0_xattn_Wq, L0_xattn_bq, L0_xattn_Wc, L0_xattn_bc)
    x = x + _L0_ffn_ref(_layernorm(x, axis=-1), L0_ffn_Wr, L0_ffn_W1, L0_ffn_b1, L0_ffn_W2, L0_ffn_b2)
    x = x + _L1_xattn_ref(_layernorm(x, axis=-1), ctx_1024, L1_xattn_Wq, L1_xattn_Wk, L1_xattn_Wv, L1_xattn_Wo, L1_xattn_proj, 0)
    x = x + _L1_ffn_ref(_layernorm(x, axis=-1), L1_ffn_w1, L1_ffn_b1, L1_ffn_w2, L1_ffn_b2, L1_ffn_centroids, L1_ffn_w_route)
    x = x + _L2_xattn_ref(_layernorm(x, axis=-1), ctx_1024, ctx_1024, mask_BxSxS2_bk1, L2_xattn_Wq, L2_xattn_Wk, L2_xattn_Wv, L2_xattn_Wo, L2_xattn_bo)
    x = x + _L2_ffn_ref(_layernorm(x, axis=-1), L2_ffn_rw1, L2_ffn_rb1, L2_ffn_rw2, L2_ffn_rb2, L2_ffn_ew1, L2_ffn_eb1, L2_ffn_ew2, L2_ffn_eb2)
    x = x + _L3_xattn_ref(_layernorm(x, axis=-1), ctx_1024, ctx_1024, mask_Bx1xS2_ik0, L3_xattn_Wq, L3_xattn_bq, L3_xattn_Wk, L3_xattn_bk, L3_xattn_Wv, L3_xattn_bv, L3_xattn_Wo, L3_xattn_bo)
    x = x + _L3_ffn_ref(_layernorm(x, axis=-1), L3_ffn_Wg, L3_ffn_bg, L3_ffn_W1, L3_ffn_b1, L3_ffn_W2, L3_ffn_b2)
    return x

_drawn_inputs = setup_inputs


def setup_inputs(seed=0):
    import zlib

    import numpy as np

    out = dict(_drawn_inputs(seed))
    spreads = {'L0_xattn_bk': (0.0, 2.0),
     'L0_xattn_bq': (0.0, 0.643),
     'L0_xattn_bc': (0.0, 0.1),
     'L0_ffn_b1': (0.0, 0.1),
     'L0_ffn_b2': (0.0, 0.1),
     'L1_ffn_b1': (0.0, 0.1),
     'L1_ffn_b2': (0.0, 0.1),
     'L2_xattn_bo': (0.0, 0.1),
     'L2_ffn_rb1': (0.0, 0.1),
     'L2_ffn_rb2': (0.0, 0.1),
     'L2_ffn_eb1': (0.0, 0.432),
     'L2_ffn_eb2': (0.0, 0.274),
     'L3_xattn_bq': (0.0, 2.0),
     'L3_xattn_bk': (0.0, 2.0),
     'L3_xattn_bv': (0.0, 0.574),
     'L3_xattn_bo': (0.0, 0.1),
     'L3_ffn_bg': (0.0, 0.1),
     'L3_ffn_b1': (0.0, 0.8),
     'L3_ffn_b2': (0.0, 0.1)}
    factors = {'L2_xattn_Wq': 7.998,
     'L2_xattn_Wk': 7.892,
     'L3_xattn_Wq': 8.0,
     'L3_xattn_Wk': 8.0,
     'L3_ffn_W1': 2.674}
    for name, (base, spread) in spreads.items():
        noise = np.random.default_rng([zlib.crc32(name.encode()), seed]).standard_normal(out[name].shape)
        drawn = base * np.exp(spread * noise) if base else spread * noise
        out[name] = jnp.asarray(drawn.astype(out[name].dtype))
    for name, factor in factors.items():
        out[name] = (out[name] * factor).astype(out[name].dtype)
    return out
```

```python
from contextlib import ExitStack

import numpy as np
import concourse.bass as bass
from concourse import mybir

F32 = mybir.dt.float32
U32 = mybir.dt.uint32
ALU = mybir.AluOpType
ACT = mybir.ActivationFunctionType
AX = mybir.AxisListType

B, S, D = 16, 112, 256
SK, KT, KP = 375, 3, 125
DC = D // 128
H = 16
E = 8
GT = 4
G = B // GT
GW = GT * S
NT = 21
LN_EPS = 1e-5
BIG = 1e30


class Mem:

    def __init__(self, nc, stack, tag):
        self.nc, self.stack, self.tag = nc, stack, tag
        self.sems = []
        stack.callback(self.clear)

    def clear(self):
        if self.sems:
            self.nc.clear_and_free_semaphores(self.sems)
            self.nc.all_engine_barrier()

    def sb(self, name, shape, dt=F32):
        return self.stack.enter_context(self.nc.sbuf_tensor(f"{self.tag}_{name}", shape, dt))

    def bank(self, name):
        return self.stack.enter_context(self.nc.psum_tensor(f"{self.tag}_{name}", [128, 512], F32))

    def sem(self, name):
        self.sems.append(self.nc.alloc_semaphore(f"{self.tag}_{name}"))
        return self.sems[-1]


def wait_for(eng, sem, value):
    if not isinstance(value, int) or value > 0:
        eng.wait_ge(sem, value)


def chunked(w):
    return w.rearrange("(c p) m -> p c m", p=128)


def load_phase(nc, x, X, ident, iota8):
    with ExitStack() as st:
        m = Mem(nc, st, "load")
        x_in, zeroed, made = m.sem("x_in"), m.sem("zeroed"), m.sem("made")
        with nc.Block() as block:
            @block.sync
            def _(sp):
                sp.dma_start(X[:, :, :], x.rearrange("b s d -> s b d")).then_inc(x_in, 16)
                sp.wait_ge(x_in, 16)

            @block.gpsimd
            def _(pool):
                pool.memset(ident[:, :], 0.0).then_inc(zeroed, 1)
                pool.wait_ge(zeroed, 1)
                pool.affine_select(out=ident[:, :], in_=ident[:, :], compare_op=ALU.not_equal, fill=1.0,
                                   base=0, pattern=[[-1, 128]], channel_multiplier=1).then_inc(made, 1)
                pool.iota(iota8[:, :], pattern=[[1, E]], base=0, channel_multiplier=0,
                          allow_small_or_imprecise_dtypes=True).then_inc(made, 1)


def clear_rows_phase(nc, xg):
    with ExitStack() as st:
        m = Mem(nc, st, "clear")
        zero = m.sb("zero", [128, xg.shape[0] // 128 // 3 * D])
        zeroed, cleared = m.sem("zeroed"), m.sem("cleared")
        with nc.Block() as block:
            @block.vector
            def _(dve):
                dve.memset(zero[:, :], 0.0).then_inc(zeroed, 1)

            @block.sync
            def _(sp):
                sp.wait_ge(zeroed, 1)
                for i in range(3):
                    sp.dma_start(xg.rearrange("(i p j) d -> i p (j d)", i=3, p=128)[i], zero[:, :]).then_inc(cleared, 16)
                sp.wait_ge(cleared, 48)


def layernorm_phase(nc, tag, X, XT, ident, bias=None, add_xn=False, xn=None):
    with ExitStack() as st:
        m = Mem(nc, st, tag)
        stats = m.sb("stats", [S, B, 6])
        mean_var = m.sb("mean_var", [S, B, 2])
        eps = m.sb("eps", [S, 1])
        std = m.sb("std", [S, B])
        rstd = m.sb("rstd", [S, B])
        xn = m.sb("xn", [S, B, D]) if xn is None else xn
        banks = [m.bank(f"b{i}") for i in range(8)]
        stats_done, mv_done, std_done, rstd_done = (m.sem(n) for n in ("stats", "mv", "std", "rstd"))
        xn_done, turned, evacuated, eps_done, bias_in, added = (
            m.sem(n) for n in ("xn", "turned", "evac", "eps", "bias_in", "added"))
        if bias is not None:
            bias_bc = m.sb("bias_bc", [S, D])
        with nc.Block() as block:
            if bias is not None:
                @block.sync
                def _(sp):
                    sp.dma_start(bias_bc[:, :], bias.unsqueeze(0).to_broadcast([S, D])).then_inc(bias_in, 16)
                    sp.wait_ge(bias_in, 16)

            @block.vector
            def _(dve):
                dve.memset(eps[:, :], LN_EPS).then_inc(eps_done, 1)
                with dve.Fori(0, B) as b:
                    dve.bn_stats(stats[:, b, :], X[:, b, :]).then_inc(stats_done, 1)
                dve.wait_ge(stats_done, B)
                for b in range(B):
                    dve.bn_aggr(mean_var[:, b, :], stats[:, b, :]).then_inc(mv_done, 1)
                dve.wait_ge(std_done, 1)
                dve.reciprocal(rstd[:, :], std[:, :]).then_inc(rstd_done, 1)
                dve.wait_ge(rstd_done, 1)
                with dve.Fori(0, B) as b:
                    dve.tensor_scalar(xn[:, b, :], X[:, b, :], mean_var[:, b, 0:1], rstd[:, bass.ds(b, 1)],
                                      ALU.subtract, ALU.mult).then_inc(xn_done, 1)

            @block.scalar
            def _(act):
                act.wait_ge(eps_done, 1)
                act.wait_ge(mv_done, B)
                act.activation(std[:, :], mean_var[:, :, 1], ACT.Sqrt, bias=eps[:, 0:1]).then_inc(std_done, 1)
                for g in range(G):
                    for c in range(DC):
                        act.wait_ge(turned, g * DC + c + 1)
                        act.copy(XT[:, c, g * GW:(g + 1) * GW], banks[g * DC + c][:, 0:GW]).then_inc(evacuated, 1)
                act.wait_ge(evacuated, G * DC)

            @block.tensor
            def _(pe):
                for g in range(G):
                    pe.wait_ge(xn_done, (g + 1) * GT)
                    for c in range(DC):
                        for t in range(GT):
                            mm = pe.transpose(banks[g * DC + c][:, t * S:(t + 1) * S],
                                              xn[:, g * GT + t, c * 128:(c + 1) * 128], ident[0:S, 0:S])
                        mm.then_inc(turned, 1)

            if bias is not None or add_xn:
                @block.gpsimd
                def _(pool):
                    if bias is not None:
                        pool.wait_ge(bias_in, 16)
                    with pool.Fori(0, B) as b:
                        pool.wait_ge(xn_done, b + 1)
                        pool.tensor_tensor(X[:, b, :], X[:, b, :], bias_bc[:, :] if bias is not None else xn[:, b, :],
                                           ALU.add).then_inc(added, 1)
                    pool.wait_ge(added, B)


def attention_phase(nc, tag, X, XT, ident, ctxT, Wq, Wk, Wo, bq=None, bk=None, Wv=None, bv=None,
                    ctx=None, hd=16, mask=None, mask_kind=None):
    C = H * hd // 128
    HC = H // C
    step = 32 if hd == 16 else 64
    HB = 128 // step
    NB = H // HB
    VW = H * hd
    VN = min(VW, 512)
    kv = [("q", c, 0) for c in range(C)] + [("k", c, 0) for c in range(C)]
    if Wv is not None:
        kv += [("v", j, n) for j in range(KT) for n in range(VW // VN)]
    NP = len(kv)
    per_step = -(-NP // 11)
    scale = -float(hd) ** -0.5
    NQ = C
    with ExitStack() as st:
        m = Mem(nc, st, tag)
        wq = m.sb("wq", [128, DC, H * hd])
        wk = m.sb("wk", [128, DC, H * hd])
        wv = m.sb("wv", [128, DC, VW]) if Wv is not None else None
        wo = m.sb("wo", [128, NB, D])
        bqT = m.sb("bqT", [128, C]) if bq is not None else None
        bkT = m.sb("bkT", [128, C]) if bk is not None else None
        bv_bc = m.sb("bv_bc", [128, VW]) if bv is not None else None
        kc = m.sb("kc", [128, 2, DC, SK])
        q_raw = m.sb("q_raw", [128, 2, C, S]) if hd == 16 else None
        head_of = m.sb("head_of", [128, HC]) if hd == 16 else None
        q = m.sb("q", [128, 2, H, S])
        k = m.sb("k", [128, 2, C, SK])
        v = m.sb("v", [KP, 2, KT, VW])
        least = m.sb("least", [S, 2, H])
        total = m.sb("total", [S, 2, H])
        inv = m.sb("inv", [S, 2, H])
        P = m.sb("P", [S, 4, SK])
        PT = m.sb("PT", [KP, 2, KT, S])
        yT = m.sb("yT", [128, 2, NB, S])
        if mask is not None:
            mask_raw = m.sb("mask_raw", [S, 2, SK], mask.dtype)
            mask_add = m.sb("mask_add", [S, 2, SK])
            masked = m.sb("masked", [S, 2, SK])
        s_bank = [m.bank("s0"), m.bank("s1")]
        t_bank = [m.bank("t0"), m.bank("t1")]
        y_bank = [m.bank("y0"), m.bank("y1")]
        p_bank = [m.bank("p0"), m.bank("p1")]

        weights_in, zeroed, heads_made = m.sem("weights_in"), m.sem("zeroed"), m.sem("heads_made")
        kc_in = [m.sem("kc_in0"), m.sem("kc_in1")]
        v_in = [m.sem("v_in0"), m.sem("v_in1")]
        mask_in = [m.sem("mask_in0"), m.sem("mask_in1")]
        mask_made = m.sem("mask_made")
        projected, evacuated, q_made = m.sem("projected"), m.sem("evacuated"), m.sem("q_made")
        scored, least_done, exp_done, inv_done, P_done = (
            m.sem(n) for n in ("scored", "least", "exp", "inv", "P_done"))
        turned, PT_done, av_done, y_done, out_done, x_done = (
            m.sem(n) for n in ("turned", "PT_done", "av", "y", "out", "x_done"))
        pool_waited, dve_waited = m.sem("pool_waited"), m.sem("dve_waited")
        half = NB // 2
        n_weights = 3 + (Wv is not None) + (bq is not None) + (bk is not None) + (bv is not None)
        if hd == 16:
            n_weights += 3

        def bodies(eng, body):
            body(0, 0)
            with eng.Fori(0, (B - 2) // 2) as i:
                body(i * 2 + 1, 1)
                body(i * 2 + 2, 0)
            body(B - 1, 1)

        first = lambda b: isinstance(b, int) and b == 0
        last = lambda b: isinstance(b, int) and b == B - 1

        def units(h):
            return range(h * per_step, min((h + 1) * per_step, NP)) if h < 12 else ()

        with nc.Block() as block:
            @block.sync
            def _(sp):
                sp.dma_start(wq[:, :, :], chunked(Wq)).then_inc(weights_in, 16)
                sp.dma_start(wk[:, :, :], chunked(Wk)).then_inc(weights_in, 16)
                if hd == 16:
                    for a in range(4):
                        sp.wait_ge(zeroed, 1)
                        sp.dma_start(wo[32 * a:32 * a + 16, :, :],
                                     Wo.rearrange("(n a d) m -> a d n m", a=4, d=16)[a]).then_inc(weights_in, 16)
                else:
                    sp.dma_start(wo[:, :, :], chunked(Wo)).then_inc(weights_in, 16)
                if Wv is not None:
                    sp.dma_start(wv[:, :, :], chunked(Wv)).then_inc(weights_in, 16)
                if bq is not None:
                    sp.dma_start(bqT[:, :], bq).then_inc(weights_in, 16)
                if bk is not None:
                    sp.dma_start(bkT[:, :], bk).then_inc(weights_in, 16)
                if bv is not None:
                    sp.dma_start(bv_bc[:, :], bv.unsqueeze(0).to_broadcast([128, VW])).then_inc(weights_in, 16)

                def load(b, u):
                    sp.dma_start(kc[:, u, :, :], ctxT[b].rearrange("(c p) s -> p c s", p=128)).then_inc(kc_in[u], 16)
                    if ctx is not None:
                        if not (isinstance(b, int) and b < 2):
                            sp.wait_ge(av_done, H * (b - 1))
                        sp.dma_start(v[:, u, :, :], ctx[b].rearrange("(j p) d -> p j d", p=KP)).then_inc(v_in[u], 16)
                    if mask is not None:
                        src = mask[b] if mask_kind == "per_query" else mask[b].to_broadcast([S, SK])
                        sp.dma_start(mask_raw[:, u, :], src).then_inc(mask_in[u], 16)

                load(0, 0)
                load(1, 1)

                def body(b, u):
                    sp.wait_ge(projected, NP * (b - 1))
                    if mask is not None:
                        sp.wait_ge(mask_made, b - 1)
                    load(b, u)

                with sp.Fori(1, B // 2) as i:
                    body(i * 2, 0)
                    body(i * 2 + 1, 1)

            @block.gpsimd
            def _(pool):
                pool.memset(q[:, :, :, :], 0.0).then_inc(zeroed, 1) if hd == 64 else \
                    pool.memset(wo[:, :, :], 0.0).then_inc(zeroed, 1)
                if hd == 16:
                    pool.memset(head_of[:, :], scale).then_inc(heads_made, 1)
                    pool.wait_ge(heads_made, 1)
                    pool.affine_select(out=head_of[:, :], in_=head_of[:, :], compare_op=ALU.is_ge, fill=0.0,
                                       base=0, pattern=[[-hd, HC]], channel_multiplier=1).then_inc(heads_made, 1)
                    pool.wait_ge(heads_made, 2)
                    pool.affine_select(out=head_of[:, :], in_=head_of[:, :], compare_op=ALU.is_ge, fill=0.0,
                                       base=hd - 1, pattern=[[hd, HC]], channel_multiplier=-1).then_inc(heads_made, 1)
                    pool.wait_ge(heads_made, 3)

                def spread_q(b, u, c):
                    pool.wait_ge(evacuated, NP * b + c + 1)
                    pool.tensor_tensor(q[:, u, c * HC:(c + 1) * HC, :],
                                       q_raw[:, u, c, :].unsqueeze(1).to_broadcast([128, HC, S]),
                                       head_of[:, :].unsqueeze(2).to_broadcast([128, HC, S]),
                                       ALU.mult).then_inc(q_made, 1)

                def scale_P(b, u, h):
                    pool.wait_ge(inv_done, H * b + h + 1)
                    pool.sem_inc(pool_waited, 1)
                    pool.tensor_scalar(P[:, h % 4, :], P[:, h % 4, :], inv[:, u, h:h + 1], 1.0,
                                       ALU.mult, ALU.mult).then_inc(P_done, 1)

                def body(b, u):
                    for h in range(H):
                        for n in units(h):
                            if hd == 16 and kv[n][0] == "q" and not last(b):
                                spread_q(b + 1, 1 - u, kv[n][1])
                        if h < H - 1:
                            scale_P(b, u, h + 1)
                        elif not last(b):
                            scale_P(b + 1, 1 - u, 0)

                if hd == 16:
                    for c in range(C):
                        spread_q(0, 0, c)
                scale_P(0, 0, 0)
                bodies(pool, body)

            @block.scalar
            def _(act):
                def evacuate(b, u, n):
                    kind, c, w = kv[n]
                    act.wait_ge(projected, NP * b + n + 1)
                    src = p_bank[n % 2]
                    if kind == "q" and hd == 16:
                        if not first(b):
                            act.wait_ge(q_made, NQ * b)
                        act.activation(q_raw[:, u, c, :], src[:, 0:S], ACT.Identity,
                                       bias=bqT[:, c:c + 1]).then_inc(evacuated, 1)
                    elif kind == "q":
                        act.mul(q[0:64, u, 2 * c, :], src[0:64, 0:S], scale)
                        act.mul(q[64:128, u, 2 * c + 1, :], src[64:128, 0:S], scale).then_inc(evacuated, 1)
                    elif kind == "k" and bk is not None:
                        act.activation(k[:, u, c, :], src[:, 0:SK], ACT.Identity,
                                       bias=bkT[:, c:c + 1]).then_inc(evacuated, 1)
                    elif kind == "k":
                        act.copy(k[:, u, c, :], src[:, 0:SK]).then_inc(evacuated, 1)
                    elif bv is None:
                        act.copy(v[:, u, c, w * VN:(w + 1) * VN], src[0:KP, 0:VN]).then_inc(evacuated, 1)

                def exp(b, u, h):
                    act.wait_ge(least_done, H * b + h + 1)
                    if not (first(b) and h < 4):
                        act.wait_ge(turned, H * b + h - 3)
                    src = s_bank[h % 2][0:S, 0:SK] if mask is None else masked[:, h % 2, :]
                    act.activation(P[:, h % 4, :], src, ACT.Exp, bias=least[:, u, h:h + 1], scale=-1.0,
                                   accum_out=total[:, u, h:h + 1]).then_inc(exp_done, 1)

                def take_y(b, u, hf):
                    act.wait_ge(av_done, H * b + 8 * hf + 8)
                    if not (first(b) or (isinstance(b, int) and b == 1)) and hf == 0:
                        act.wait_ge(out_done, b - 1)
                    act.copy(yT[:, u, hf * half:(hf + 1) * half, :],
                             y_bank[hf][:, 0:half * S].rearrange("p (n s) -> p n s", n=half)).then_inc(y_done, 1)

                def body(b, u):
                    for h in range(H):
                        if h < H - 3:
                            exp(b, u, h + 3)
                        elif not last(b):
                            exp(b + 1, 1 - u, h + 3 - H)
                        if not last(b):
                            for n in units(h):
                                if not (kv[n][0] == "v" and bv is not None):
                                    evacuate(b + 1, 1 - u, n)
                        if h == 1 and not first(b):
                            take_y(b - 1, 1 - u, 1)
                        if h == 9:
                            take_y(b, u, 0)

                if hd == 64:
                    act.wait_ge(zeroed, 1)
                act.wait_ge(weights_in, 16 * n_weights)
                for n in range(NP):
                    if not (kv[n][0] == "v" and bv is not None):
                        evacuate(0, 0, n)
                for h in range(3):
                    exp(0, 0, h)
                bodies(act, body)
                take_y(B - 1, 1, 1)

            @block.vector
            def _(dve):
                def make_mask(b, u):
                    dve.wait_ge(mask_in[u], 16 * (b // 2) + 16 if isinstance(b, int) else (b - u) * 8 + 16)
                    if mask_kind == "per_query":
                        dve.tensor_scalar(mask_add[:, u, :], mask_raw[:, u, :], BIG, None, ALU.mult).then_inc(mask_made, 1)
                    else:
                        dve.tensor_scalar(mask_add[:, u, :], mask_raw[:, u, :], 0, BIG, ALU.is_equal,
                                          ALU.mult).then_inc(mask_made, 1)

                def value_bias(b, u, n):
                    _, j, w = kv[n]
                    dve.wait_ge(projected, NP * b + n + 1)
                    dve.tensor_tensor(v[:, u, j, w * VN:(w + 1) * VN], p_bank[n % 2][0:KP, 0:VN],
                                      bv_bc[0:KP, w * VN:(w + 1) * VN], ALU.add).then_inc(evacuated, 1)

                def least_of(b, u, h):
                    dve.wait_ge(scored, H * b + h + 1)
                    if mask is None:
                        dve.tensor_reduce(least[:, u, h:h + 1], s_bank[h % 2][0:S, 0:SK], AX.X,
                                          ALU.min).then_inc(least_done, 1)
                        return
                    if h == 0:
                        dve.wait_ge(mask_made, b + 1)
                    if not (first(b) and h < 2):
                        dve.wait_ge(exp_done, H * b + h - 1)
                    dve.sem_inc(dve_waited, 1)
                    dve.tensor_tensor_reduce(masked[:, h % 2, :], s_bank[h % 2][0:S, 0:SK], mask_add[:, u, :], 1.0,
                                             3e38, ALU.add, ALU.min, least[:, u, h:h + 1]).then_inc(least_done, 1)

                def invert(b, u, h):
                    dve.wait_ge(exp_done, H * b + h + 1)
                    dve.reciprocal(inv[:, u, h:h + 1], total[:, u, h:h + 1]).then_inc(inv_done, 1)

                def take_PT(b, u, h):
                    dve.wait_ge(turned, H * b + h + 1)
                    if not (first(b) and h < 2):
                        dve.wait_ge(av_done, H * b + h - 1)
                    dve.tensor_copy(PT[:, h % 2, :, :],
                                    t_bank[h % 2][0:KP, 0:KT * S].rearrange("p (j s) -> p j s", j=KT)).then_inc(PT_done, 1)

                def add_out(b, u):
                    dve.wait_ge(out_done, b + 1)
                    dve.tensor_tensor(X[:, b, :], p_bank[1][0:S, 0:D], X[:, b, :], ALU.add).then_inc(x_done, 1)

                def body(b, u):
                    for h in range(H):
                        if mask is not None and h == 2 and not last(b):
                            make_mask(b + 1, 1 - u)
                        if h < H - 3:
                            least_of(b, u, h + 3)
                        elif not last(b):
                            least_of(b + 1, 1 - u, h + 3 - H)
                        if h < H - 1:
                            invert(b, u, h + 1)
                        elif not last(b):
                            invert(b + 1, 1 - u, 0)
                        if not last(b):
                            for n in units(h):
                                if kv[n][0] == "v" and bv is not None:
                                    value_bias(b + 1, 1 - u, n)
                        take_PT(b, u, h)
                        if h == 13 and not first(b):
                            add_out(b - 1, 1 - u)

                dve.memset(y_bank[0][:, :], 0.0).then_inc(x_done, 1)
                dve.memset(y_bank[1][:, :], 0.0).then_inc(x_done, 1)
                if mask is not None:
                    make_mask(0, 0)
                for n in range(NP):
                    if kv[n][0] == "v" and bv is not None:
                        value_bias(0, 0, n)
                for h in range(3):
                    least_of(0, 0, h)
                invert(0, 0, 0)
                bodies(dve, body)
                add_out(B - 1, 1)
                dve.wait_ge(x_done, 2 + B)

            @block.tensor
            def _(pe):
                def project(b, u, n):
                    kind, c, w = kv[n]
                    out = p_bank[n % 2]
                    if n == 0:
                        pe.wait_ge(kc_in[u], 16 * (b // 2) + 16 if isinstance(b, int) else (b - u) * 8 + 16)
                        if not first(b):
                            pe.wait_ge(evacuated, NP * b)
                        if not first(b) and not (isinstance(b, int) and b == 1):
                            pe.wait_ge(x_done, b)
                    elif kind == "v" and bv is not None and kv[n - 1][0] == "k":
                        pe.wait_ge(evacuated, NP * b + n)
                    elif n >= 2:
                        pe.wait_ge(evacuated, NP * b + n - 1)
                    for i in range(DC):
                        if kind == "q":
                            mm = pe.matmul(out[:, 0:S], wq[:, i, c * 128:(c + 1) * 128],
                                           XT[:, i, bass.ds(b * S, S)], start=i == 0, stop=i == DC - 1)
                        elif kind == "k":
                            mm = pe.matmul(out[:, 0:SK], wk[:, i, c * 128:(c + 1) * 128], kc[:, u, i, :],
                                           start=i == 0, stop=i == DC - 1)
                        else:
                            mm = pe.matmul(out[0:KP, 0:VN], kc[:, u, i, c * KP:(c + 1) * KP],
                                           wv[:, i, w * VN:(w + 1) * VN], start=i == 0, stop=i == DC - 1)
                    mm.then_inc(projected, 1)

                def score(b, u, h):
                    if h == 0:
                        pe.wait_ge(evacuated, NP * (b + 1))
                        if hd == 16:
                            pe.wait_ge(q_made, NQ * (b + 1))
                    if not (first(b) and h < 2):
                        pe.wait_ge(exp_done if mask is None else least_done, H * b + h - 1)
                    pe.matmul(s_bank[h % 2][0:S, 0:SK], q[:, u, h, :], k[:, u, h // HC, :],
                              start=True, stop=True).then_inc(scored, 1)

                def turn(b, u, h):
                    pe.wait_ge(P_done, H * b + h + 1)
                    if not (first(b) and h < 2):
                        pe.wait_ge(PT_done, H * b + h - 1)
                    for j in range(KT):
                        mm = pe.transpose(t_bank[h % 2][0:KP, j * S:(j + 1) * S],
                                          P[:, h % 4, j * KP:(j + 1) * KP], ident[0:S, 0:S])
                    mm.then_inc(turned, 1)

                def weigh(b, u, h):
                    pe.wait_ge(PT_done, H * b + h + 1)
                    if h == 0 and ctx is not None:
                        pe.wait_ge(v_in[u], 16 * (b // 2) + 16 if isinstance(b, int) else (b - u) * 8 + 16)
                    if h % 8 == 0 and not first(b):
                        pe.wait_ge(y_done, 2 * b - 1 + h // 8)
                    p0, blk = step * (h % HB), (h % 8) // HB
                    for j in range(KT):
                        mm = pe.matmul(y_bank[h // 8][p0:p0 + hd, blk * S:(blk + 1) * S],
                                       v[:, u, j, h * hd:(h + 1) * hd], PT[:, h % 2, j, :],
                                       start=j == 0, stop=j == KT - 1)
                    mm.then_inc(av_done, 1)

                def out_product(b, u):
                    pe.wait_ge(y_done, 2 * b + 2)
                    if last(b):
                        pe.wait_ge(x_done, 2 + B - 1)
                    else:
                        pe.wait_ge(evacuated, NP * B if isinstance(b, int) and b == B - 2 else NP * (b + 3))
                    for n in range(NB):
                        mm = pe.matmul(p_bank[1][0:S, 0:D], yT[:, u, n, :], wo[:, n, :], start=n == 0, stop=n == NB - 1)
                    mm.then_inc(out_done, 1)

                def body(b, u):
                    for h in range(H):
                        if h < H - 3:
                            score(b, u, h + 3)
                        elif not last(b):
                            score(b + 1, 1 - u, h + 3 - H)
                        todo = list(units(h)) if not last(b) else []
                        if todo:
                            project(b + 1, 1 - u, todo.pop(0))
                        turn(b, u, h)
                        if h > 0:
                            weigh(b, u, h - 1)
                        elif not first(b):
                            weigh(b - 1, 1 - u, H - 1)
                        for n in todo:
                            project(b + 1, 1 - u, n)
                        if h == 13 and not first(b):
                            out_product(b - 1, 1 - u)

                pe.wait_ge(weights_in, 16 * n_weights)
                pe.wait_ge(x_done, 2)
                for n in range(NP):
                    project(0, 0, n)
                for h in range(3):
                    score(0, 0, h)
                bodies(pe, body)
                weigh(B - 1, 1, H - 1)
                out_product(B - 1, 1)


def linear_attention_phase(nc, tag, X, XT, ctxT, WqT, WkT, projT, Wv, Wo):
    DH, M, EPS = 64, 128, 1e-3
    RATIO = 1.0 / float(np.sqrt(M))
    NPAIR = H // 2
    KN = H * M // 512
    VN = H * DH // 512
    VC = DH + 1
    units = [("k", j, n) for j in range(KT) for n in range(KN)] + \
            [("v", j, n) for j in range(KT) for n in range(VN)] + [("q", g, 0) for g in range(H // 4)]
    NU, NK, NV = len(units), KT * KN, KT * VN
    with ExitStack() as st:
        m = Mem(nc, st, tag)
        wkf = m.sb("wkf", [128, DC, H * M])
        wqf = m.sb("wqf", [128, DC, H * M])
        wv = m.sb("wv", [128, DC, H * DH])
        wo = m.sb("wo", [128, NPAIR, D])
        kc = m.sb("kc", [128, 2, DC, SK])
        kvs = m.sb("kvs", [128, H, VC])
        rden = m.sb("rden", [128, 4 * S])
        attT = m.sb("attT", [128, NPAIR, S])
        u_bank = [m.bank(f"u{i}") for i in range(4)]
        kvs_bank = [m.bank("kvs0"), m.bank("kvs1")]
        num_bank, den_bank = m.bank("num"), m.bank("den")
        fold_in, proj_zero, proj_in, folded, fold_evac = (
            m.sem(n) for n in ("fold_in", "proj_zero", "proj_in", "folded", "fold_evac"))
        weights_in = m.sem("weights_in")
        kc_in = [m.sem("kc_in0"), m.sem("kc_in1")]
        ones_made, unit_done, k_evac, v_evac, q_evac = (
            m.sem(n) for n in ("ones", "unit", "k_evac", "v_evac", "q_evac"))
        kvs_done, kvs_evac, nd_done, rden_done, att_done, out_done, x_done = (
            m.sem(n) for n in ("kvs_done", "kvs_evac", "nd", "rden", "att", "out", "x_done"))

        with ExitStack() as st2:
            m2 = Mem(nc, st2, tag + "_fold")
            wT = m2.sb("wT", [128, 2, NPAIR, D])
            pp = m2.sb("pp", [128, 2 * M])
            with nc.Block() as block:
                @block.sync
                def _(sp):
                    sp.dma_start(wT[:, 0, :, :], chunked(WkT)).then_inc(fold_in, 16)
                    sp.dma_start(wT[:, 1, :, :], chunked(WqT)).then_inc(fold_in, 16)
                    sp.wait_ge(proj_zero, 1)
                    sp.dma_start(pp[0:DH, 0:M], projT).then_inc(proj_in, 16)
                    sp.dma_start(pp[DH:2 * DH, M:2 * M], projT).then_inc(proj_in, 16)
                    sp.dma_start(wv[:, :, :], chunked(Wv)).then_inc(weights_in, 16)
                    sp.dma_start(wo[:, :, :], chunked(Wo)).then_inc(weights_in, 16)
                    sp.dma_start(kc[:, 0, :, :], ctxT[0].rearrange("(c p) s -> p c s", p=128)).then_inc(kc_in[0], 16)
                    sp.dma_start(kc[:, 1, :, :], ctxT[1].rearrange("(c p) s -> p c s", p=128)).then_inc(kc_in[1], 16)

                @block.gpsimd
                def _(pool):
                    pool.memset(pp[:, :], 0.0).then_inc(proj_zero, 1)

                @block.tensor
                def _(pe):
                    pe.wait_ge(fold_in, 32)
                    pe.wait_ge(proj_in, 32)
                    n = 0
                    for w in range(2):
                        for pr in range(NPAIR):
                            for c in range(DC):
                                if n >= 4:
                                    pe.wait_ge(fold_evac, n - 3)
                                pe.matmul(u_bank[n % 4][:, 0:2 * M], wT[:, w, pr, c * 128:(c + 1) * 128], pp[:, :],
                                          start=True, stop=True).then_inc(folded, 1)
                                n += 1

                @block.scalar
                def _(act):
                    n = 0
                    for w in range(2):
                        for pr in range(NPAIR):
                            for c in range(DC):
                                act.wait_ge(folded, n + 1)
                                act.mul((wkf, wqf)[w][:, c, pr * 2 * M:(pr + 1) * 2 * M], u_bank[n % 4][:, 0:2 * M],
                                        RATIO).then_inc(fold_evac, 1)
                                n += 1
                    act.wait_ge(fold_evac, n)

        kp = m.sb("kp", [KP, KT, H * M])
        v = m.sb("v", [KP, 2, KT, H, VC])
        qp = m.sb("qp", [128, 2, H, S])

        def bodies(eng, body):
            body(0, 0)
            with eng.Fori(0, (B - 2) // 2) as i:
                body(i * 2 + 1, 1)
                body(i * 2 + 2, 0)
            body(B - 1, 1)

        first = lambda b: isinstance(b, int) and b == 0
        last = lambda b: isinstance(b, int) and b == B - 1

        with nc.Block() as block:
            @block.sync
            def _(sp):
                def body(b, u):
                    sp.wait_ge(unit_done, NU * (b - 2) + NK + NV)
                    sp.dma_start(kc[:, u, :, :], ctxT[b].rearrange("(c p) s -> p c s", p=128)).then_inc(kc_in[u], 16)
                with sp.Fori(1, B // 2) as i:
                    body(i * 2, 0)
                    body(i * 2 + 1, 1)

            @block.gpsimd
            def _(pool):
                pool.memset(v[:, :, :, :, DH:VC], 1.0).then_inc(ones_made, 1)

            @block.scalar
            def _(act):
                def body(b, u):
                    for n in range(NK, NK + NV):
                        _, j, w = units[n]
                        act.wait_ge(unit_done, NU * b + n + 1)
                        act.copy(v[:, u, j, w * 8:(w + 1) * 8, 0:DH],
                                 u_bank[(u * NU + n) % 4][0:KP, 0:512].rearrange("p (h d) -> p h d", d=DH)).then_inc(v_evac, 1)
                    for g in range(H // 4):
                        act.wait_ge(kvs_done, 4 * b + g + 1)
                        act.copy(kvs[:, 4 * g:4 * g + 4, :],
                                 kvs_bank[g % 2][:, 0:4 * VC].rearrange("p (h d) -> p h d", d=VC)).then_inc(kvs_evac, 1)
                bodies(act, body)

            @block.vector
            def _(dve):
                def take(b, u, n, dst, rows, cols, sem):
                    dve.wait_ge(unit_done, NU * b + n + 1)
                    dve.tensor_scalar(dst, u_bank[(u * NU + n) % 4][0:rows, 0:cols], 0.0, EPS, ALU.max,
                                      ALU.add).then_inc(sem, 1)

                def divide(b, u, hf):
                    dve.wait_ge(nd_done, 2 * b + hf + 1)
                    if not (first(b) and hf == 0):
                        dve.wait_ge(att_done, 2 * b + hf)
                    dve.reciprocal(rden[:, :], den_bank[:, 0:4 * S]).then_inc(rden_done, 1)
                    dve.wait_ge(rden_done, 2 * b + hf + 1)
                    dve.tensor_tensor(attT[:, 4 * hf:4 * hf + 4, :], num_bank[:, 0:4 * S].rearrange("p (n s) -> p n s", s=S),
                                      rden[:, :].rearrange("p (n s) -> p n s", s=S), ALU.mult).then_inc(att_done, 1)

                def add_out(b):
                    dve.wait_ge(out_done, b + 1)
                    dve.tensor_tensor(X[:, b, :], num_bank[0:S, 0:D], X[:, b, :], ALU.add).then_inc(x_done, 1)

                def body(b, u):
                    for n in range(NK):
                        _, j, w = units[n]
                        if n == NK // 2 and not first(b):
                            divide(b - 1, 1 - u, 0)
                        take(b, u, n, kp[:, j, w * 512:(w + 1) * 512], KP, 512, k_evac)
                    if not first(b):
                        divide(b - 1, 1 - u, 1)
                        add_out(b - 1)
                    for g in range(H // 4):
                        take(b, u, NK + NV + g, qp[:, u, 4 * g:4 * g + 4, :].rearrange("p n s -> p (n s)"),
                             128, 4 * S, q_evac)
                bodies(dve, body)
                divide(B - 1, 1, 0)
                divide(B - 1, 1, 1)
                add_out(B - 1)
                dve.wait_ge(x_done, B)

            @block.tensor
            def _(pe):
                def evacuated(b, n):
                    if n < 0:
                        b, n = b - 1, n + NU
                    kind = units[n][0]
                    if kind == "k":
                        pe.wait_ge(k_evac, NK * b + n + 1)
                    elif kind == "v":
                        pe.wait_ge(v_evac, NV * b + n - NK + 1)
                    else:
                        pe.wait_ge(q_evac, (H // 4) * b + n - NK - NV + 1)

                def unit(b, u, n):
                    kind, j, w = units[n]
                    if n == 0:
                        pe.wait_ge(kc_in[u], 16 * (b // 2) + 16 if isinstance(b, int) else (b - u) * 8 + 16)
                    if not (first(b) and n < 4):
                        evacuated(b, n - 4)
                    out = u_bank[(u * NU + n) % 4]
                    if kind == "q":
                        for hh in range(4):
                            h = 4 * j + hh
                            for c in range(DC):
                                mm = pe.matmul(out[:, hh * S:(hh + 1) * S], wqf[:, c, h * M:(h + 1) * M],
                                               XT[:, c, bass.ds(b * S, S)], start=c == 0, stop=c == DC - 1)
                    else:
                        wt = wkf if kind == "k" else wv
                        for c in range(DC):
                            mm = pe.matmul(out[0:KP, 0:512], kc[:, u, c, j * KP:(j + 1) * KP],
                                           wt[:, c, w * 512:(w + 1) * 512], start=c == 0, stop=c == DC - 1)
                    mm.then_inc(unit_done, 1)

                def sum_keys(b, u):
                    pe.wait_ge(k_evac, NK * (b + 1))
                    pe.wait_ge(v_evac, NV * (b + 1))
                    for g in range(H // 4):
                        if g >= 2:
                            pe.wait_ge(kvs_evac, 4 * b + g - 1)
                        elif not first(b):
                            pe.wait_ge(kvs_evac, 4 * b + g - 1)
                        for hh in range(4):
                            h = 4 * g + hh
                            for j in range(KT):
                                mm = pe.matmul(kvs_bank[g % 2][:, hh * VC:(hh + 1) * VC], kp[:, j, h * M:(h + 1) * M],
                                               v[:, u, j, h, :], start=j == 0, stop=j == KT - 1)
                        mm.then_inc(kvs_done, 1)

                def num_den(b, u, hf):
                    pe.wait_ge(kvs_evac, 4 * b + 2 * hf + 2)
                    pe.wait_ge(q_evac, 4 * b + 2 * hf + 2)
                    if not first(b) or hf == 1:
                        pe.wait_ge(att_done, 2 * b + hf)
                    if hf == 0 and not first(b):
                        pe.wait_ge(x_done, b)
                    for pr in range(4):
                        for which in range(2):
                            for side in range(2):
                                h = 8 * hf + 2 * pr + side
                                lhs = kvs[:, h, 0:DH] if which == 0 else kvs[:, h, DH:VC].to_broadcast([128, DH])
                                mm = pe.matmul((num_bank, den_bank)[which][side * DH:(side + 1) * DH, pr * S:(pr + 1) * S],
                                               lhs, qp[:, u, h, :], start=True, stop=True)
                    mm.then_inc(nd_done, 1)

                def out_product(b):
                    pe.wait_ge(att_done, 2 * b + 2)
                    for n in range(NPAIR):
                        mm = pe.matmul(num_bank[0:S, 0:D], attT[:, n, :], wo[:, n, :], start=n == 0, stop=n == NPAIR - 1)
                    mm.then_inc(out_done, 1)

                def body(b, u):
                    for n in range(NK):
                        if n == NK // 2 and not first(b):
                            num_den(b - 1, 1 - u, 0)
                        unit(b, u, n)
                    if not first(b):
                        num_den(b - 1, 1 - u, 1)
                    for n in range(NK, NK + NV):
                        unit(b, u, n)
                    if not first(b):
                        out_product(b - 1)
                    for n in range(NK + NV, NU):
                        unit(b, u, n)
                    sum_keys(b, u)

                pe.wait_ge(weights_in, 32)
                pe.wait_ge(ones_made, 1)
                bodies(pe, body)
                num_den(B - 1, 1, 0)
                num_den(B - 1, 1, 1)
                out_product(B - 1)


def router_phase(nc, tag, X, XT, gates, ident, iota8, kind, b2, Wr=None, bias=None, cent=None,
                 rw1=None, rb1=None, hots=None, weights=None):
    LW = 2 * E if kind == "cos" else E
    with ExitStack() as st:
        m = Mem(nc, st, tag)
        wr = m.sb("wr", [128, DC, LW])
        b2s = m.sb("b2s", [E, D])
        logits = m.sb("logits", [S, B, E])
        best = m.sb("best", [S, B, 8])
        where = m.sb("where", [S, B, 8], U32)
        wheref = m.sb("wheref", [S, B, 8])
        hot = m.sb("hot", [S, B, E])
        hot1 = m.sb("hot1", [S, B, E]) if hots is None else hots[0]
        hot2 = m.sb("hot2", [S, B, E]) if hots is None or kind != "two" else hots[1]
        ex = m.sb("ex", [S, B, E])
        total = m.sb("total", [S, B])
        gT = m.sb("gT", [E, B, S])
        bank = m.bank("logits_ps")
        gt_bank = [m.bank(f"gt{i}") for i in range(4)]
        ob = [m.bank(f"ob{i}") for i in range(2)]
        extra = m.bank("extra")
        weights_in, logits_done, link, exp_done, sub_done, gates_done = (
            m.sem(n) for n in ("weights_in", "logits", "link", "exp", "sub", "gates"))
        gt_turned, gt_evac, out_done, x_done = (m.sem(n) for n in ("gt", "gt_evac", "out", "x_done"))
        c_sq, c_norm, c_scaled, c_turned, c_in, x_sq, x_norm = (
            m.sem(n) for n in ("c_sq", "c_norm", "c_scaled", "c_turned", "c_in", "x_sq", "x_norm"))
        hid, hid_evac = m.sem("hid"), m.sem("hid_evac")
        n_in = 2
        if bias is not None:
            bias_bc = m.sb("bias_bc", [S, E])
            n_in += 1
        if kind == "cos":
            cn = m.sb("cn", [E, D])
            cjunk = m.sb("cjunk", [E, D])
            cstat = m.sb("cstat", [E, 3])
            xjunk = m.sb("xjunk", [S, 2, D])
            xstat = m.sb("xstat", [S, 3, B])
            both = m.sb("both", [S, B, LW])
            n_in += 1
        if kind == "two":
            w1 = m.sb("w1", [128, DC, D])
            b1 = m.sb("b1", [128, DC])
            hidden = m.sb("hidden", [128, DC, B * S])
            n_in += 2
        with nc.Block() as block:
            @block.sync
            def _(sp):
                sp.dma_start(b2s[:, :], b2).then_inc(weights_in, 16)
                sp.dma_start(wr[:, :, LW - E:LW], chunked(Wr)).then_inc(weights_in, 16)
                if bias is not None:
                    sp.dma_start(bias_bc[:, :], bias.unsqueeze(0).to_broadcast([S, E])).then_inc(weights_in, 16)
                if kind == "cos":
                    sp.dma_start(cn[:, :], cent).then_inc(weights_in, 16)
                if kind == "two":
                    sp.dma_start(w1[:, :, :], chunked(rw1)).then_inc(weights_in, 16)
                    sp.dma_start(b1[:, :], rb1).then_inc(weights_in, 16)
                sp.wait_ge(weights_in, 16 * n_in)

            @block.tensor
            def _(pe):
                pe.wait_ge(weights_in, 16 * n_in)
                if kind == "cos":
                    pe.wait_ge(c_scaled, 1)
                    for c in range(DC):
                        mm = pe.transpose(extra[:, c * E:(c + 1) * E], cn[:, c * 128:(c + 1) * 128], ident[0:E, 0:E])
                    mm.then_inc(c_turned, 1)
                    pe.wait_ge(c_in, 1)
                    for t in range(B):
                        if t >= 2:
                            pe.wait_ge(x_sq, t - 1)
                        for c in range(DC):
                            mm = pe.transpose(ob[t % 2][0:S, c * 128:(c + 1) * 128], XT[:, c, t * S:(t + 1) * S], ident[:, :])
                        mm.then_inc(out_done, 1)
                src = XT
                if kind == "two":
                    src = hidden
                    n = 0
                    for g in range(G):
                        for f in range(DC):
                            if n >= 4:
                                pe.wait_ge(hid_evac, n - 3)
                            for c in range(DC):
                                mm = pe.matmul(gt_bank[n % 4][:, 0:GW], w1[:, c, f * 128:(f + 1) * 128],
                                               XT[:, c, g * GW:(g + 1) * GW], start=c == 0, stop=c == DC - 1)
                            mm.then_inc(hid, 1)
                            n += 1
                    pe.wait_ge(hid_evac, n)
                for t in range(B):
                    for c in range(DC):
                        mm = pe.matmul(bank[0:S, t * LW:(t + 1) * LW], src[:, c, t * S:(t + 1) * S], wr[:, c, :],
                                       start=c == 0, stop=c == DC - 1)
                mm.then_inc(logits_done, 1)
                pe.wait_ge(gates_done, 1)
                for g in range(G):
                    for t in range(GT):
                        mm = pe.transpose(gt_bank[g][0:E, t * S:(t + 1) * S], gates[:, :, g * GT + t], ident[0:S, 0:S])
                    mm.then_inc(gt_turned, 1)
                if kind == "cos":
                    pe.wait_ge(x_sq, B)
                for t in range(B):
                    if t % GT == 0:
                        pe.wait_ge(gt_evac, t // GT + 1)
                    if t >= 2:
                        pe.wait_ge(x_done, t - 1)
                    pe.matmul(ob[t % 2][0:S, 0:D], gT[:, t, :], b2s[:, :], start=True, stop=True).then_inc(out_done, 1)

            @block.scalar
            def _(act):
                if kind == "cos":
                    act.wait_ge(c_sq, 1)
                    act.activation(cstat[:, 1:2], cstat[:, 0:1], ACT.Sqrt).then_inc(c_norm, 1)
                    act.wait_ge(c_turned, 1)
                    act.copy(wr[:, :, 0:E], extra[:, 0:DC * E].rearrange("p (c e) -> p c e", e=E)).then_inc(c_in, 1)
                    for t in range(B):
                        act.wait_ge(out_done, t + 1)
                        act.activation(xjunk[:, t % 2, :], ob[t % 2][0:S, 0:D], ACT.Square,
                                       accum_out=xstat[:, 0, t:t + 1]).then_inc(x_sq, 1)
                    act.wait_ge(x_sq, B)
                    act.activation(xstat[:, 1, :], xstat[:, 0, :], ACT.Sqrt).then_inc(x_norm, 1)
                if kind == "two":
                    act.wait_ge(weights_in, 16 * n_in)
                    for n in range(G * DC):
                        g, f = divmod(n, DC)
                        act.wait_ge(hid, n + 1)
                        act.activation(hidden[:, f, g * GW:(g + 1) * GW], gt_bank[n % 4][:, 0:GW], ACT.Silu,
                                       bias=b1[:, f:f + 1]).then_inc(hid_evac, 1)
                if kind != "one":
                    act.wait_ge(sub_done, 1)
                    act.activation(ex[:, :, :], ex[:, :, :], ACT.Exp).then_inc(exp_done, 1)
                for g in range(G):
                    act.wait_ge(gt_turned, g + 1)
                    act.copy(gT[:, g * GT:(g + 1) * GT, :],
                             gt_bank[g][0:E, 0:GW].rearrange("p (t s) -> p t s", t=GT)).then_inc(gt_evac, 1)

            @block.vector
            def _(dve):
                count = [0]

                def step(ins):
                    count[0] += 1
                    ins.then_inc(link, 1)
                    dve.wait_ge(link, count[0])

                def wide(a):
                    return a.to_broadcast([S, B, E])

                dve.wait_ge(weights_in, 16 * n_in)
                if kind == "cos":
                    dve.tensor_tensor_reduce(cjunk[:, :], cn[:, :], cn[:, :], 1.0, 0.0, ALU.mult, ALU.add,
                                             cstat[:, 0:1]).then_inc(c_sq, 1)
                    dve.wait_ge(c_norm, 1)
                    step(dve.tensor_scalar(cstat[:, 1:2], cstat[:, 1:2], 1e-12, None, ALU.max))
                    step(dve.reciprocal(cstat[:, 2:3], cstat[:, 1:2]))
                    dve.tensor_scalar(cn[:, :], cn[:, :], cstat[:, 2:3], None, ALU.mult).then_inc(c_scaled, 1)
                    dve.wait_ge(x_norm, 1)
                    step(dve.tensor_scalar(xstat[:, 1, :], xstat[:, 1, :], 1e-12, None, ALU.max))
                    step(dve.reciprocal(xstat[:, 2, :], xstat[:, 1, :]))
                dve.wait_ge(logits_done, 1)
                if kind == "cos":
                    step(dve.tensor_copy(both[:, :, :], bank[0:S, 0:B * LW].rearrange("s (b l) -> s b l", l=LW)))
                    step(dve.tensor_tensor(logits[:, :, :], both[:, :, 0:E], wide(xstat[:, 2, :].unsqueeze(2)), ALU.mult))
                    step(dve.tensor_tensor(logits[:, :, :], logits[:, :, :], both[:, :, E:LW], ALU.add))
                elif bias is not None:
                    step(dve.tensor_tensor(logits[:, :, :], bank[0:S, 0:B * E].rearrange("s (b l) -> s b l", l=E),
                                           bias_bc[:, :].unsqueeze(1).to_broadcast([S, B, E]), ALU.add))
                else:
                    step(dve.tensor_copy(logits[:, :, :], bank[0:S, 0:B * E].rearrange("s (b l) -> s b l", l=E)))
                for t in range(B):
                    ins = dve.max(best[:, t, :], logits[:, t, :])
                step(ins)
                if kind == "cos":
                    step(dve.tensor_tensor(hot[:, :, :], logits[:, :, :], wide(best[:, :, 1:2]), ALU.is_ge))
                else:
                    for t in range(B):
                        ins = dve.max_index(where[:, t, :], best[:, t, :], logits[:, t, :])
                    step(ins)
                    step(dve.tensor_copy(wheref[:, :, :], where[:, :, :]))
                    lane = iota8[0:S, :].unsqueeze(1).to_broadcast([S, B, E])
                    step(dve.tensor_tensor(hot1[:, :, :], lane, wide(wheref[:, :, 0:1]), ALU.is_equal))
                    if kind == "two":
                        step(dve.tensor_tensor(hot2[:, :, :], lane, wide(wheref[:, :, 1:2]), ALU.is_equal))
                        step(dve.tensor_tensor(hot[:, :, :], hot1[:, :, :], hot2[:, :, :], ALU.add))
                    else:
                        step(dve.tensor_copy(hot[:, :, :], hot1[:, :, :]))
                out = gates[:, :, :].rearrange("s e b -> s b e")
                if kind == "one":
                    dve.tensor_copy(out, hot[:, :, :]).then_inc(gates_done, 1)
                else:
                    dve.tensor_tensor(ex[:, :, :], logits[:, :, :], wide(best[:, :, 0:1]), ALU.subtract).then_inc(sub_done, 1)
                    dve.wait_ge(exp_done, 1)
                    if kind != "prob":
                        step(dve.tensor_tensor(ex[:, :, :], ex[:, :, :], hot[:, :, :], ALU.mult))
                    step(dve.tensor_reduce(total[:, :], ex[:, :, :], AX.X, ALU.add))
                    step(dve.reciprocal(total[:, :], total[:, :]))
                    dve.tensor_tensor(out, (hot if kind == "prob" else ex)[:, :, :], wide(total[:, :].unsqueeze(2)),
                                      ALU.mult).then_inc(gates_done, 1)
                if weights is not None:
                    dve.wait_ge(gates_done, 1)
                    for n, w in enumerate(weights):
                        step(dve.tensor_tensor(ex[:, :, :], out, (hot1, hot2)[n][:, :, :], ALU.mult))
                        step(dve.tensor_reduce(w[:, :], ex[:, :, :], AX.X, ALU.add))
                base = B if kind == "cos" else 0
                for t in range(B):
                    dve.wait_ge(out_done, base + t + 1)
                    dve.tensor_tensor(X[:, t, :], ob[t % 2][0:S, 0:D], X[:, t, :], ALU.add).then_inc(x_done, 1)
                dve.wait_ge(x_done, B)


def ffn_phase(nc, tag, X, XT, gates, W1, b1, W2, F, func):
    FC = F // 128
    NH = 2
    HR = 4
    with ExitStack() as st:
        m = Mem(nc, st, tag)
        w1 = m.sb("w1", [128, 2, DC, F])
        w2 = m.sb("w2", [128, 2, FC, D])
        b1s = m.sb("b1s", [128, 2, FC])
        h = m.sb("h", [128, NH, FC, GW])
        h_bank = [m.bank(f"h{i}") for i in range(HR)]
        o_bank = [m.bank(f"o{i}") for i in range(GT)]
        w_in = [m.sem("w_in0"), m.sem("w_in1")]
        h_done, h_evac, o_done, x_done = (m.sem(n) for n in ("h_done", "h_evac", "o_done", "x_done"))
        SG = 2 * G

        def turns(eng, body):
            body(0)
            with eng.Fori(1, E // 2) as i:
                body(i)

        with nc.Block() as block:
            @block.sync
            def _(sp):
                def load(i, u):
                    e = i * 2 + u
                    sp.dma_start(w1[:, u, :, :], W1[e].rearrange("(c p) f -> p c f", p=128)).then_inc(w_in[u], 16)
                    sp.dma_start(w2[:, u, :, :], W2[e].rearrange("(c p) f -> p c f", p=128)).then_inc(w_in[u], 16)
                    sp.dma_start(b1s[:, u, :], b1[e]).then_inc(w_in[u], 16)
                load(0, 0)
                load(0, 1)
                with sp.Fori(1, E // 2) as i:
                    for u in range(2):
                        sp.wait_ge(o_done, (i - 1) * SG * GT + (u + 1) * G * GT)
                        load(i, u)

            def peeled(i):
                return isinstance(i, int)

            @block.tensor
            def _(pe):
                def hidden(i, s):
                    u, g = divmod(s, G)
                    if g == 0:
                        pe.wait_ge(w_in[u], 48 * (i + 1))
                    for f in range(FC):
                        n = s * FC + f
                        if not (peeled(i) and n < HR):
                            pe.wait_ge(h_evac, i * SG * FC + n - HR + 1)
                        for c in range(DC):
                            mm = pe.matmul(h_bank[n % HR][:, 0:GW], w1[:, u, c, f * 128:(f + 1) * 128],
                                           XT[:, c, g * GW:(g + 1) * GW], start=c == 0, stop=c == DC - 1)
                        mm.then_inc(h_done, 1)

                def output(i, s):
                    u, g = divmod(s, G)
                    pe.wait_ge(h_evac, (i * SG + s + 1) * FC)
                    for t in range(GT):
                        if not (peeled(i) and s == 0):
                            pe.wait_ge(x_done, (i * SG + s - 1) * GT + t + 1)
                        for f in range(FC):
                            mm = pe.matmul(o_bank[t][0:S, 0:D], h[:, s % NH, f, t * S:(t + 1) * S], w2[:, u, f, :],
                                           start=f == 0, stop=f == FC - 1)
                        mm.then_inc(o_done, 1)

                def body(i):
                    for s in range(SG):
                        hidden(i, s)
                        if s > 0:
                            output(i, s - 1)
                        elif not peeled(i):
                            output_prev(i)

                def output_prev(i):
                    s = SG - 1
                    u, g = divmod(s, G)
                    pe.wait_ge(h_evac, i * SG * FC)
                    for t in range(GT):
                        pe.wait_ge(x_done, (i * SG - 2) * GT + t + 1)
                        for f in range(FC):
                            mm = pe.matmul(o_bank[t][0:S, 0:D], h[:, s % NH, f, t * S:(t + 1) * S], w2[:, u, f, :],
                                           start=f == 0, stop=f == FC - 1)
                        mm.then_inc(o_done, 1)

                turns(pe, body)
                output_prev(E // 2)

            @block.scalar
            def _(act):
                def body(i):
                    for s in range(SG):
                        u, g = divmod(s, G)
                        if not (peeled(i) and s < NH):
                            act.wait_ge(o_done, (i * SG + s - NH + 1) * GT)
                        for f in range(FC):
                            n = s * FC + f
                            act.wait_ge(h_done, i * SG * FC + n + 1)
                            act.activation(h[:, s % NH, f, :], h_bank[n % HR][:, 0:GW], func,
                                           bias=b1s[:, u, f:f + 1]).then_inc(h_evac, 1)
                act.wait_ge(w_in[0], 48)
                turns(act, body)

            @block.vector
            def _(dve):
                def body(i):
                    for s in range(SG):
                        u, g = divmod(s, G)
                        for t in range(GT):
                            b = g * GT + t
                            dve.wait_ge(o_done, (i * SG + s) * GT + t + 1)
                            if not (peeled(i) and s < G):
                                dve.wait_ge(x_done, (i * SG + s - G) * GT + t + 1)
                            dve.scalar_tensor_tensor(out=X[:, b, :], in0=o_bank[t][0:S, 0:D],
                                                     scalar=gates[:, :, :].rearrange("s e b -> s (e b)")[:, bass.ds((i * 2 + u) * B + b, 1)],
                                                     in1=X[:, b, :], op0=ALU.mult, op1=ALU.add).then_inc(x_done, 1)
                turns(dve, body)
                dve.wait_ge(x_done, E * B)


def dispatch_phase(nc, tag, xn, hots, slots, tile_expert, xg, TS):
    K = len(hots)
    JMAX = B * S // TS
    with ExitStack() as st:
        m = Mem(nc, st, tag)
        before = m.sb("before", [S, S])
        ones = m.sb("ones", [S, S])
        hot = m.sb("hot", [S, B, E])
        tot = m.sb("tot", [S, B, E])
        cum = m.sb("cum", [S, B + 1, E])
        edges = m.sb("edges", [S, JMAX])
        index = m.sb("index", [S, NT])
        filled = m.sb("filled", [S, E, JMAX])
        tiles = m.sb("tiles", [S, E])
        start = m.sb("start", [S, E + 1])
        start_row = m.sb("start_row", [S, E])
        passed = m.sb("passed", [S, NT, E])
        expert = m.sb("expert", [S, NT])
        row = m.sb("row", [S, B, E])
        picked = m.sb("picked", [S, B, E])
        slotf = m.sb("slotf", [S, B])
        prefix_bank, total_bank = m.bank("prefix_ps"), m.bank("total_ps")
        made, tri, hot_done, counted, link, slots_done, sent = (
            m.sem(n) for n in ("made", "tri", "hot_done", "counted", "link", "slots_done", "sent"))
        with nc.Block() as block:
            @block.gpsimd
            def _(pool):
                pool.memset(before[:, :], 1.0).then_inc(tri, 1)
                pool.memset(ones[:, :], 1.0).then_inc(made, 1)
                pool.iota(edges[:, :], pattern=[[TS, JMAX]], base=0, channel_multiplier=0,
                          allow_small_or_imprecise_dtypes=True).then_inc(made, 1)
                pool.iota(index[:, :], pattern=[[1, NT]], base=0, channel_multiplier=0,
                          allow_small_or_imprecise_dtypes=True).then_inc(made, 1)
                pool.wait_ge(tri, 1)
                pool.affine_select(out=before[:, :], in_=before[:, :], compare_op=ALU.is_gt, fill=0.0, base=0,
                                   pattern=[[1, S]], channel_multiplier=-1).then_inc(made, 1)
                for k in range(K):
                    pool.wait_ge(slots_done, k + 1)
                    for b in range(B):
                        pool.indirect_dma_start(
                            out=xg[:, :], out_offset=bass.IndirectOffsetOnAxis(ap=slots[k][:, b:b + 1], axis=0),
                            in_=xn[:, b, :], in_offset=None).then_inc(sent, 16)
                pool.wait_ge(sent, 16 * K * B)

            @block.tensor
            def _(pe):
                pe.wait_ge(made, 4)
                pe.wait_ge(hot_done, 1)
                pe.matmul(prefix_bank[0:S, 0:B * E], before[:, :], hot[:, :, :].rearrange("s b e -> s (b e)"),
                          start=True, stop=True).then_inc(counted, 1)
                pe.matmul(total_bank[0:S, 0:B * E], ones[:, :], hot[:, :, :].rearrange("s b e -> s (b e)"),
                          start=True, stop=True).then_inc(counted, 1)

            @block.vector
            def _(dve):
                count = [0]

                def step(ins):
                    count[0] += 1
                    ins.then_inc(link, 1)
                    dve.wait_ge(link, count[0])

                if K == 1:
                    dve.tensor_copy(hot[:, :, :], hots[0][:, :, :]).then_inc(hot_done, 1)
                else:
                    dve.tensor_tensor(hot[:, :, :], hots[0][:, :, :], hots[1][:, :, :], ALU.add).then_inc(hot_done, 1)
                dve.memset(start[:, 0:1], 0.0)
                step(dve.memset(cum[:, 0, :], 0.0))
                dve.wait_ge(counted, 2)
                step(dve.tensor_copy(tot[:, :, :], total_bank[0:S, 0:B * E].rearrange("s (b e) -> s b e", e=E)))
                for b in range(B):
                    step(dve.tensor_tensor(cum[:, b + 1, :], cum[:, b, :], tot[:, b, :], ALU.add))
                dve.wait_ge(made, 4)
                step(dve.tensor_tensor(filled[:, :, :], cum[:, B, :].unsqueeze(2).to_broadcast([S, E, JMAX]),
                                       edges[:, :].unsqueeze(1).to_broadcast([S, E, JMAX]), ALU.is_gt))
                step(dve.tensor_reduce(tiles[:, :], filled[:, :, :], AX.X, ALU.add))
                for e in range(E):
                    step(dve.tensor_tensor(start[:, e + 1:e + 2], start[:, e:e + 1], tiles[:, e:e + 1], ALU.add))
                step(dve.tensor_scalar(start_row[:, :], start[:, 0:E], float(TS), None, ALU.mult))
                step(dve.tensor_tensor(row[:, :, :], prefix_bank[0:S, 0:B * E].rearrange("s (b e) -> s b e", e=E),
                                       cum[:, 0:B, :], ALU.add))
                step(dve.tensor_tensor(row[:, :, :], row[:, :, :],
                                       start_row[:, :].unsqueeze(1).to_broadcast([S, B, E]), ALU.add))
                for k in range(K):
                    step(dve.tensor_tensor(picked[:, :, :], row[:, :, :], hots[k][:, :, :], ALU.mult))
                    step(dve.tensor_reduce(slotf[:, :], picked[:, :, :], AX.X, ALU.add))
                    dve.tensor_copy(slots[k][:, :], slotf[:, :]).then_inc(slots_done, 1)
                    dve.wait_ge(slots_done, k + 1)
                step(dve.tensor_tensor(passed[:, :, :], index[:, :].unsqueeze(2).to_broadcast([S, NT, E]),
                                       start[:, 1:E + 1].unsqueeze(1).to_broadcast([S, NT, E]), ALU.is_ge))
                step(dve.tensor_reduce(expert[:, :], passed[:, :, :], AX.X, ALU.add))
                step(dve.tensor_scalar(expert[:, :], expert[:, :], float(E - 1), None, ALU.min))
                step(dve.tensor_copy(tile_expert[:, :], expert[0:1, :]))


def experts_phase(nc, tag, xg, yg, tile_expert, ident, W1, b1, W2, F, func, TS):
    FC, MT, R = F // 128, TS // 128, 3
    TURNS = NT // R
    with ExitStack() as st:
        m = Mem(nc, st, tag)
        w1 = m.sb("w1", [128, R, DC, F])
        w2 = m.sb("w2", [128, R, FC, D])
        b1s = m.sb("b1s", [128, R, FC])
        xs = m.sb("xs", [128, R, MT, D])
        xT = m.sb("xT", [128, R, DC, TS])
        h = m.sb("h", [128, R, FC, TS])
        y = m.sb("y", [128, R, MT, D])
        t_bank = m.bank("t")
        h_bank = [m.bank(f"h{i}") for i in range(R)]
        o_bank = [m.bank(f"o{i}") for i in range(R)]
        w1_in = [m.sem(f"w1_in{i}") for i in range(R)]
        w2_in = [m.sem(f"w2_in{i}") for i in range(R)]
        xs_in = [m.sem(f"xs_in{i}") for i in range(R)]
        stored = [m.sem(f"stored{i}") for i in range(R)]
        turned, xT_done, h_done, h_evac, o_done, y_done = (
            m.sem(n) for n in ("turned", "xT", "h_done", "h_evac", "o_done", "y"))
        xg_t = xg.rearrange("(j p) d -> p j d", p=128)
        yg_t = yg.rearrange("(j p) d -> p j d", p=128)

        with nc.Block() as block:
            @block.sync
            def _(sp):
                def load(i, s):
                    j = i * R + s
                    wait_for(sp, turned, j - R + 1)
                    sp.dma_start(xs[:, s, :, :], xg_t[:, bass.ds(j * MT, MT), :]).then_inc(xs_in[s], 16)
                    e = sp.value_load(tile_expert[0:1, bass.ds(j, 1)], min_val=0, max_val=E - 1)
                    wait_for(sp, h_evac, (j - R + 1) * FC)
                    sp.dma_start(w1[:, s, :, :], W1[bass.ds(e, 1)].rearrange("o (c p) f -> p (o c) f", p=128)).then_inc(w1_in[s], 16)
                    sp.dma_start(b1s[:, s, :], b1[bass.ds(e, 1)].rearrange("o p f -> p (o f)")).then_inc(w1_in[s], 16)
                    wait_for(sp, o_done, (j - R + 1) * MT)
                    sp.dma_start(w2[:, s, :, :], W2[bass.ds(e, 1)].rearrange("o (c p) f -> p (o c) f", p=128)).then_inc(w2_in[s], 16)
                for s in range(R):
                    load(0, s)
                with sp.Fori(1, TURNS) as i:
                    for s in range(R):
                        load(i, s)

            @block.gpsimd
            def _(pool):
                with pool.Fori(0, TURNS) as i:
                    for s in range(R):
                        pool.wait_ge(y_done, (i * R + s + 1) * MT)
                        pool.dma_start(yg_t[:, bass.ds((i * R + s) * MT, MT), :], y[:, s, :, :]).then_inc(stored[s], 16)
                for s in range(R):
                    pool.wait_ge(stored[s], 16 * TURNS)

            def in_order(eng, turn, hidden, output):
                turn(0, 0)
                for i in (0, 1, TURNS - 1):
                    def body(i):
                        for s in range(R):
                            if s + 1 < R:
                                turn(i, s + 1)
                            elif not isinstance(i, int) or i < TURNS - 1:
                                turn(i + 1, 0)
                            hidden(i, s)
                            if s > 0:
                                output(i, s - 1)
                            elif not isinstance(i, int) or i > 0:
                                output(i - 1, R - 1)
                    if i == 1:
                        with eng.Fori(1, TURNS - 1) as k:
                            body(k)
                    else:
                        body(i)
                output(TURNS - 1, R - 1)

            @block.tensor
            def _(pe):
                def turn(i, s):
                    pe.wait_ge(xs_in[s], 16 * (i + 1))
                    wait_for(pe, xT_done, i * R + s)
                    for c in range(DC):
                        for t in range(MT):
                            mm = pe.transpose(t_bank[:, c * TS + t * 128:c * TS + (t + 1) * 128],
                                              xs[:, s, t, c * 128:(c + 1) * 128], ident[:, :])
                    mm.then_inc(turned, 1)

                def hidden(i, s):
                    pe.wait_ge(w1_in[s], 32 * (i + 1))
                    pe.wait_ge(xT_done, i * R + s + 1)
                    for f in range(FC):
                        n = s * FC + f
                        wait_for(pe, h_evac, i * R * FC + n - R + 1)
                        for c in range(DC):
                            mm = pe.matmul(h_bank[n % R][:, 0:TS], w1[:, s, c, f * 128:(f + 1) * 128],
                                           xT[:, s, c, :], start=c == 0, stop=c == DC - 1)
                        mm.then_inc(h_done, 1)

                def output(i, s):
                    pe.wait_ge(w2_in[s], 16 * (i + 1))
                    pe.wait_ge(h_evac, (i * R + s + 1) * FC)
                    for t in range(MT):
                        n = s * MT + t
                        wait_for(pe, y_done, i * R * MT + n - R + 1)
                        for f in range(FC):
                            mm = pe.matmul(o_bank[n % R][:, 0:D], h[:, s, f, t * 128:(t + 1) * 128], w2[:, s, f, :],
                                           start=f == 0, stop=f == FC - 1)
                        mm.then_inc(o_done, 1)

                in_order(pe, turn, hidden, output)

            @block.scalar
            def _(act):
                def body(i):
                    for s in range(R):
                        wait_for(act, o_done, (i * R + s - R + 1) * MT)
                        act.wait_ge(w1_in[s], 32 * (i + 1))
                        for f in range(FC):
                            n = s * FC + f
                            act.wait_ge(h_done, i * R * FC + n + 1)
                            act.activation(h[:, s, f, :], h_bank[n % R][:, 0:TS], func,
                                           bias=b1s[:, s, f:f + 1]).then_inc(h_evac, 1)
                body(0)
                with act.Fori(1, TURNS) as i:
                    body(i)

            @block.vector
            def _(dve):
                def turn(i, s):
                    dve.wait_ge(turned, i * R + s + 1)
                    wait_for(dve, h_done, (i * R + s - R + 1) * FC)
                    dve.tensor_copy(xT[:, s, :, :], t_bank[:, 0:DC * TS].rearrange("p (c t) -> p c t", c=DC)).then_inc(xT_done, 1)

                def output(i, s):
                    wait_for(dve, stored[s], 16 * i)
                    for t in range(MT):
                        dve.wait_ge(o_done, (i * R + s) * MT + t + 1)
                        dve.tensor_copy(y[:, s, t, :], o_bank[(s * MT + t) % R][:, 0:D]).then_inc(y_done, 1)

                in_order(dve, turn, lambda i, s: None, output)


def combine_phase(nc, tag, X, yg, slots, weights):
    K = len(slots)
    with ExitStack() as st:
        m = Mem(nc, st, tag)
        got = m.sb("got", [S, K * B, D])
        fetched = [m.sem(f"fetched{i}") for i in range(8)]
        x_done = m.sem("x_done")
        with nc.Block() as block:
            @block.gpsimd
            def _(pool):
                for n in range(K * B):
                    k, b = divmod(n, B)
                    pool.indirect_dma_start(
                        out=got[:, n, :], out_offset=None, in_=yg[:, :],
                        in_offset=bass.IndirectOffsetOnAxis(ap=slots[k][:, b:b + 1], axis=0)).then_inc(fetched[n % 8], 16)
                    if n >= 7:
                        pool.wait_ge(fetched[(n - 7) % 8], 16 * ((n - 7) // 8 + 1))

            @block.vector
            def _(dve):
                for n in range(K * B):
                    k, b = divmod(n, B)
                    dve.wait_ge(fetched[n % 8], 16 * (n // 8 + 1))
                    if k > 0:
                        dve.wait_ge(x_done, (k - 1) * B + b + 1)
                    dve.scalar_tensor_tensor(out=X[:, b, :], in0=got[:, n, :], scalar=weights[k][:, b:b + 1],
                                             in1=X[:, b, :], op0=ALU.mult, op1=ALU.add).then_inc(x_done, 1)
                dve.wait_ge(x_done, K * B)


def store_phase(nc, out, X):
    with ExitStack() as st:
        m = Mem(nc, st, "store")
        stored = m.sem("stored")
        with nc.Block() as block:
            @block.sync
            def _(sp):
                sp.dma_start(out.rearrange("b s d -> s b d"), X[:, :, :]).then_inc(stored, 16)
                sp.wait_ge(stored, 16)


def build(nc, a, out, stop=8):
    with ExitStack() as st:
        m = Mem(nc, st, "all")
        X = m.sb("X", [S, B, D])
        XT = m.sb("XT", [128, DC, B * S])
        gates = m.sb("gates", [S, E, B])
        ident = m.sb("ident", [128, 128])
        iota8 = m.sb("iota8", [128, E])
        load_phase(nc, a["x"], X, ident, iota8)
        xg = nc.dram_tensor("rows", (NT * 256, D), F32, kind="Internal").ap()
        yg = nc.dram_tensor("expert_rows", (NT * 256, D), F32, kind="Internal").ap()
        clear_rows_phase(nc, xg)

        def sparse_ffn(t, kind, W1, b1, W2, b2, F, func, Wr, bias=None, add_xn=False, rw1=None, rb1=None):
            K, TS = (2, 256) if kind == "two" else (1, 128)
            with ExitStack() as st2:
                m2 = Mem(nc, st2, f"s{t}")
                slots = [m2.sb(f"slots{k}", [S, B], U32) for k in range(K)]
                weights = [m2.sb(f"weights{k}", [S, B]) for k in range(K)]
                tile_expert = m2.sb("tile_expert", [1, NT], U32)
                rows, rows_out = xg[0:NT * TS, :], yg[0:NT * TS, :]
                with ExitStack() as st3:
                    m3 = Mem(nc, st3, f"d{t}")
                    xn = m3.sb("xn", [S, B, D])
                    hots = [m3.sb(f"hots{k}", [S, B, E]) for k in range(K)]
                    layernorm_phase(nc, f"n{t}", X, XT, ident, add_xn=add_xn, xn=xn)
                    router_phase(nc, f"r{t}", X, XT, gates, ident, iota8, kind, b2, Wr=Wr, bias=bias,
                                 rw1=rw1, rb1=rb1, hots=hots, weights=weights)
                    dispatch_phase(nc, f"p{t}", xn, hots, slots, tile_expert, rows, TS)
                experts_phase(nc, f"f{t}", rows, rows_out, tile_expert, ident, W1, b1, W2, F, func, TS)
                combine_phase(nc, f"c{t}", X, rows_out, slots, weights)

        def sub0():
            layernorm_phase(nc, "n0", X, XT, ident, bias=a["L0_xattn_bc"])
            attention_phase(nc, "a0", X, XT, ident, a["ctxT"], a["L0_WqT"], a["L0_WkT"], a["L0_WcT"],
                            bq=a["L0_bq"], bk=a["L0_bk"], ctx=a["ctx_1024"], hd=16)

        def sub1():
            sparse_ffn(1, "prob", a["L0_ffn_W1"], a["L0_b1"], a["L0_ffn_W2"], a["L0_ffn_b2"], 1024, ACT.Gelu,
                       a["L0_ffn_Wr"])

        def sub2():
            layernorm_phase(nc, "n2", X, XT, ident)
            linear_attention_phase(nc, "a2", X, XT, a["ctxT"], a["L1_WqT"], a["L1_WkT"], a["L1_projT"],
                                   a["L1_Wv"], a["L1_Wo"])

        def sub3():
            layernorm_phase(nc, "n3", X, XT, ident)
            router_phase(nc, "r3", X, XT, gates, ident, iota8, "cos", a["L1_ffn_b2"], Wr=a["L1_wrT"],
                         cent=a["L1_ffn_centroids"])
            ffn_phase(nc, "f3", X, XT, gates, a["L1_ffn_w1"], a["L1_b1"], a["L1_ffn_w2"], 128, ACT.Gelu)

        def sub4():
            layernorm_phase(nc, "n4", X, XT, ident, bias=a["L2_xattn_bo"])
            attention_phase(nc, "a4", X, XT, ident, a["ctxT"], a["L2_xattn_Wq"], a["L2_xattn_Wk"],
                            a["L2_xattn_Wo"], Wv=a["L2_xattn_Wv"], hd=64,
                            mask=a["mask_BxSxS2_bk1"], mask_kind="per_query")

        def sub5():
            sparse_ffn(5, "two", a["L2_ffn_ew1"], a["L2_b1"], a["L2_ffn_ew2"], a["L2_ffn_eb2"], 512, ACT.Silu,
                       a["L2_ffn_rw2"], bias=a["L2_ffn_rb2"], add_xn=True, rw1=a["L2_ffn_rw1"], rb1=a["L2_rb1"])

        def sub6():
            layernorm_phase(nc, "n6", X, XT, ident, bias=a["L3_xattn_bo"])
            attention_phase(nc, "a6", X, XT, ident, a["ctxT"], a["L3_xattn_Wq"], a["L3_xattn_Wk"],
                            a["L3_xattn_Wo"], bq=a["L3_bq"], bk=a["L3_bk"], Wv=a["L3_xattn_Wv"],
                            bv=a["L3_xattn_bv"], hd=16, mask=a["mask_Bx1xS2_ik0"], mask_kind="per_key")

        def sub7():
            sparse_ffn(7, "one", a["L3_ffn_W1"], a["L3_b1"], a["L3_ffn_W2"], a["L3_ffn_b2"], 256, ACT.Gelu,
                       a["L3_ffn_Wg"], bias=a["L3_ffn_bg"])

        first_sub, stop = stop if isinstance(stop, tuple) else (0, stop)
        for sub in (sub0, sub1, sub2, sub3, sub4, sub5, sub6, sub7)[first_sub:stop]:
            sub()
        store_phase(nc, out, X)


def layout(inputs):
    a = {n: np.asarray(v) for n, v in inputs.items()}

    def columns(v):
        return v.reshape(-1, 128).T

    a["ctxT"] = a["ctx_1024"].transpose(0, 2, 1)
    for n in ("q", "k", "c"):
        a[f"L0_W{n}T"] = a.pop(f"L0_xattn_W{n}").T
    for n in ("q", "k"):
        a[f"L0_b{n}"] = columns(a.pop(f"L0_xattn_b{n}"))
        a[f"L3_b{n}"] = columns(a.pop(f"L3_xattn_b{n}"))
        a[f"L1_W{n}T"] = a.pop(f"L1_xattn_W{n}").transpose(1, 2, 0).reshape(1024, D)
    a["L2_rb1"] = columns(a.pop("L2_ffn_rb1"))
    a["L1_projT"] = a.pop("L1_xattn_proj").T
    a["L1_Wv"] = a.pop("L1_xattn_Wv").reshape(D, 1024)
    a["L1_Wo"] = a.pop("L1_xattn_Wo").reshape(1024, D)
    a["L1_wrT"] = a.pop("L1_ffn_w_route").T
    for layer, name in (("L0", "L0_ffn_b1"), ("L1", "L1_ffn_b1"), ("L2", "L2_ffn_eb1"), ("L3", "L3_ffn_b1")):
        b = a.pop(name)
        a[f"{layer}_b1"] = b.reshape(E, -1, 128).transpose(0, 2, 1)
    return {n: np.ascontiguousarray(v) for n, v in a.items()}


def declare(nc, arrays, stop=8):
    a = {n: nc.dram_tensor(f"in_{n}", v.shape, mybir.dt.from_np(v.dtype), kind="ExternalInput").ap()
         for n, v in arrays.items()}
    out = nc.dram_tensor("out", (B, S, D), F32, kind="ExternalOutput").ap()
    build(nc, a, out, stop)


def kernel(**inputs):
    import concourse.bacc as bacc
    from concourse.bass_utils import run_bass_kernel_spmd

    arrays = layout(inputs)
    nc = bacc.Bacc("TRN2", target_bir_lowering=False, num_devices=1)
    declare(nc, arrays)
    r = run_bass_kernel_spmd(nc, [{f"in_{n}": v for n, v in arrays.items()}], core_ids=[0])
    return r.results[0]["out"]
```

```python
from contextlib import ExitStack

import numpy as np
import concourse.bass as bass
from concourse import mybir

F32 = mybir.dt.float32
F16 = mybir.dt.float16
U32 = mybir.dt.uint32
ALU = mybir.AluOpType
ACT = mybir.ActivationFunctionType
AX = mybir.AxisListType

B, S, D = 16, 112, 256
SK, KT, KP = 375, 3, 125
DC = D // 128
H = 16
E = 8
GT = 4
G = B // GT
ZR = 7
GW = GT * S
NT = 21
LN_EPS = 1e-5
HI, LO = 0, 1
PARTS = ((LO, HI), (HI, LO), (HI, HI))
WS = 64.0
BIG = 1e30


class Mem:

    def __init__(self, nc, stack, tag):
        self.nc, self.stack, self.tag = nc, stack, tag
        self.sems = []
        stack.callback(self.clear)

    def clear(self):
        if self.sems:
            self.nc.clear_and_free_semaphores(self.sems)
            self.nc.all_engine_barrier()

    def sb(self, name, shape, dt=F32):
        return self.stack.enter_context(self.nc.sbuf_tensor(f"{self.tag}_{name}", shape, dt))

    def bank(self, name):
        return self.stack.enter_context(self.nc.psum_tensor(f"{self.tag}_{name}", [128, 512], F32))

    def sem(self, name):
        self.sems.append(self.nc.alloc_semaphore(f"{self.tag}_{name}"))
        return self.sems[-1]


def wait_for(eng, sem, value):
    if not isinstance(value, int) or value > 0:
        eng.wait_ge(sem, value)


def chunked(w):
    return w.rearrange("(c p) m -> p c m", p=128)


def load_phase(nc, x, X, ident, iota8, zero, zeroed, cleared, xg):
    with ExitStack() as st:
        m = Mem(nc, st, "load")
        x_in, blank, made = m.sem("x_in"), m.sem("blank"), m.sem("made")
        with nc.Block() as block:
            @block.vector
            def _(dve):
                dve.memset(zero[:, :], 0.0).then_inc(zeroed, 1)

            @block.sync
            def _(sp):
                sp.dma_start(X[:, :, :], x.rearrange("b s d -> s b d")).then_inc(x_in, 16)
                sp.wait_ge(x_in, 16)
                sp.wait_ge(zeroed, 1)
                for i in range(xg.shape[0] // 128 // ZR):
                    sp.dma_start(xg.rearrange("(i p j) d -> i p (j d)", p=128, j=ZR)[i], zero[:, :]).then_inc(cleared, 16)

            @block.gpsimd
            def _(pool):
                pool.memset(ident[:, :], 0.0).then_inc(blank, 1)
                pool.wait_ge(blank, 1)
                pool.affine_select(out=ident[:, :], in_=ident[:, :], compare_op=ALU.not_equal, fill=1.0,
                                   base=0, pattern=[[-1, 128]], channel_multiplier=1).then_inc(made, 1)
                pool.iota(iota8[:, :], pattern=[[1, E]], base=0, channel_multiplier=0,
                          allow_small_or_imprecise_dtypes=True).then_inc(made, 1)


def layernorm_phase(nc, tag, X, XT, ident, xn=None, fetch=None, prepare=None):
    HB = B // 2
    with ExitStack() as st:
        m = Mem(nc, st, tag)
        stats = m.sb("stats", [S, B, 6])
        mean_var = m.sb("mean_var", [S, B, 2])
        eps = m.sb("eps", [S, 1])
        warm = m.sb("warm", [S, 1])
        std = m.sb("std", [S, B])
        rstd = m.sb("rstd", [S, B])
        xn = m.sb("xn", [S, B, D]) if xn is None else xn
        banks = [m.bank(f"b{i}") for i in range(8)]
        stats_done, mv_done, std_done, rstd_done = (m.sem(n) for n in ("stats", "mv", "std", "rstd"))
        xn_done, turned, evacuated, eps_done = (m.sem(n) for n in ("xn", "turned", "evac", "eps"))
        with nc.Block() as block:
            if fetch is not None:
                @block.sync
                def _(sp):
                    fetch(sp)

            if prepare is not None:
                @block.gpsimd
                def _(pool):
                    prepare(pool)

            @block.vector
            def _(dve):
                def statistics(i):
                    for b in range(i * HB, (i + 1) * HB):
                        dve.bn_stats(stats[:, b, :], X[:, b, :]).then_inc(stats_done, 1)
                    dve.wait_ge(stats_done, (i + 1) * HB)
                    for b in range(i * HB, (i + 1) * HB):
                        dve.bn_aggr(mean_var[:, b, :], stats[:, b, :]).then_inc(mv_done, 1)

                def invert(i):
                    dve.wait_ge(std_done, i + 1)
                    dve.reciprocal(rstd[:, i * HB:(i + 1) * HB], std[:, i * HB:(i + 1) * HB]).then_inc(rstd_done, 1)

                def normalise(i):
                    dve.wait_ge(rstd_done, i + 1)
                    for b in range(i * HB, (i + 1) * HB):
                        dve.tensor_scalar(xn[:, b, :], X[:, b, :], mean_var[:, b, 0:1], rstd[:, b:b + 1],
                                          ALU.subtract, ALU.mult).then_inc(xn_done, 1)

                dve.memset(eps[:, :], LN_EPS).then_inc(eps_done, 1)
                statistics(0)
                statistics(1)
                invert(0)
                normalise(0)
                invert(1)
                normalise(1)

            @block.scalar
            def _(act):
                act.wait_ge(eps_done, 1)
                act.activation(warm[:, :], eps[:, :], ACT.Sqrt)
                for i in range(2):
                    act.wait_ge(mv_done, (i + 1) * HB)
                    act.activation(std[:, i * HB:(i + 1) * HB], mean_var[:, i * HB:(i + 1) * HB, 1], ACT.Sqrt,
                                   bias=eps[:, 0:1]).then_inc(std_done, 1)
                for g in range(G):
                    for c in range(DC):
                        act.wait_ge(turned, g * DC + c + 1)
                        act.copy(XT[:, c, g * GW:(g + 1) * GW], banks[g * DC + c][:, 0:GW]).then_inc(evacuated, 1)
                act.wait_ge(evacuated, G * DC)

            @block.tensor
            def _(pe):
                for g in range(G):
                    for c in range(DC):
                        for t in range(GT):
                            if c == 0:
                                pe.wait_ge(xn_done, g * GT + t + 1)
                            mm = pe.transpose(banks[g * DC + c][:, t * S:(t + 1) * S],
                                              xn[:, g * GT + t, c * 128:(c + 1) * 128], ident[0:S, 0:S])
                        mm.then_inc(turned, 1)


def attention_phase(nc, tag, X, XT, ident, ctxT, Wq, Wk, Wo, bo, bq=None, bk=None, Wv=None, bv=None,
                    ctx=None, scratch=None, hd=16, mask=None, mask_kind=None):
    C = H * hd // 128

    step = 32 if hd == 16 else 64
    HB = 128 // step
    NB = H // HB
    VW = H * hd
    VN = min(VW, 512)
    kv = [("q", c, 0) for c in range(C)] + [("k", c, 0) for c in range(C)]
    if Wv is not None:
        kv += [("v", j, n) for j in range(KT) for n in range(VW // VN)]
    NP = len(kv)
    scale = -float(hd) ** -0.5
    QK = 2 * C
    if hd == 16:
        NPASS, KH = 1, H // 2
        q_slots = [(0, 64 * r + 16 * i, r, 2, (HI, LO, HI)[i]) for r in range(2) for i in range(3)]
        k_slots = [(0, 64 * r + 16 * i, r, 2, (HI, HI, LO)[i]) for r in range(2) for i in range(3)]
    else:
        NPASS, KH = 2, H
        q_slots = [(n, 64 * i, 0, 1, (HI, LO)[n]) for n in range(2) for i in range(2)]
        k_slots = [(0, 64 * i, 0, 1, (HI, LO)[i]) for i in range(2)]
    NSLOT = len(q_slots) + len(k_slots)
    split = hd == 64
    with ExitStack() as st:
        m = Mem(nc, st, tag)
        wq = m.sb("wq", [128, DC, H * hd])
        wk = m.sb("wk", [128, DC, H * hd])
        wv = m.sb("wv", [128, DC, VW]) if Wv is not None else None
        wo = m.sb("wo", [128, NB, D])
        bqT = m.sb("bqT", [128, C]) if bq is not None else None
        bkT = m.sb("bkT", [128, C]) if bk is not None else None
        bv_bc = m.sb("bv_bc", [128, VW]) if bv is not None else None
        bo_bc = m.sb("bo_bc", [S, D])
        kc = m.sb("kc", [128, 2, DC, SK])
        if split:
            kc16 = m.sb("kc16", [128, 2, 2, DC, SK], F16)
            wk16 = m.sb("wk16", [128, 2, DC, H * hd], F16)
            wv16 = m.sb("wv16", [128, 2, DC, VW], F16)
        q = m.sb("q", [128, 2, NPASS, H, S], F16)
        k = m.sb("k", [128, 2, KH, SK], F16)
        q_dram, k_dram = scratch
        v = m.sb("v", [KP, 2, KT, VW])
        least = m.sb("least", [S, 2, H])
        total = m.sb("total", [S, 2, H])
        inv = m.sb("inv", [S, 2, H])
        if mask is not None:
            mask_raw = m.sb("mask_raw", [S, 2, SK], mask.dtype)
            mask_add = m.sb("mask_add", [S, 2, SK])
            masked = m.sb("masked", [S, 2, SK])
        weights_in, zeroed = m.sem("weights_in"), m.sem("zeroed")
        stack_in = [m.sem("stack_in0"), m.sem("stack_in1")]
        parts_made, parts_out, bias_scaled = (m.sem(n) for n in ("parts_made", "parts_out", "bias_scaled"))
        kc_in = [m.sem("kc_in0"), m.sem("kc_in1")]
        v_in = [m.sem("v_in0"), m.sem("v_in1")]
        mask_in = [m.sem("mask_in0"), m.sem("mask_in1")]
        mask_made = m.sem("mask_made")
        w_hi, w_split, kc_hi, kc_split = (m.sem(n) for n in ("w_hi", "w_split", "kc_hi", "kc_split"))
        projected, evacuated = m.sem("projected"), m.sem("evacuated")
        scored, least_done, exp_done, inv_done, P_done = (
            m.sem(n) for n in ("scored", "least", "exp", "inv", "P_done"))
        turned, PT_done, av_done, y_done, out_done, x_done = (
            m.sem(n) for n in ("turned", "PT_done", "av", "y", "out", "x_done"))
        sp_waited, pool_waited, dve_waited, biased = m.sem("sp_waited"), m.sem("pool_waited"), m.sem("dve_waited"), m.sem("biased")
        half = NB // 2
        n_weights = 4 + (Wv is not None) + (bq is not None) + (bk is not None) + (bv is not None)
        if hd == 16:
            n_weights += 3

        def bodies(eng, body):
            body(0, 0)
            with eng.Fori(0, (B - 4) // 2) as i:
                body(i * 2 + 1, 1)
                body(i * 2 + 2, 0)
            for b in range(B - 3, B):
                body(b, b % 2)

        first = lambda b: isinstance(b, int) and b == 0
        last = lambda b: isinstance(b, int) and b == B - 1

        PER = 2 if hd == 64 else 1
        QK_STEP, OUT_STEP = (H - QK // PER, 6) if hd == 64 else (10, 6)

        def units(b, h):
            n = QK + h - 1
            if QK <= n < NP and not last(b):
                return [(b + 1, n)]
            n = PER * (h - QK_STEP)
            if 0 <= n < QK and not (isinstance(b, int) and b >= B - 2):
                return [(b + 2, n + i) for i in range(PER)]
            return []

        def load_keys(sp, b, u):
            sp.dma_start(kc[:, u, :, :], ctxT[b].rearrange("(c p) s -> p c s", p=128)).then_inc(kc_in[u], 16)

        def load_rest(sp, b, u):
            if ctx is not None:
                if not (isinstance(b, int) and b < 2):
                    sp.wait_ge(av_done, H * (b - 1))
                sp.dma_start(v[:, u, :, :], ctx[b].rearrange("(j p) d -> p j d", p=KP)).then_inc(v_in[u], 16)
            if mask is not None:
                src = mask[b] if mask_kind == "per_query" else mask[b].to_broadcast([S, SK])
                sp.dma_start(mask_raw[:, u, :], src).then_inc(mask_in[u], 16)

        def fetch(sp):
            sp.dma_start(bo_bc[:, :], bo.unsqueeze(0).to_broadcast([S, D])).then_inc(weights_in, 16)
            sp.dma_start(wq[:, :, :], chunked(Wq)).then_inc(weights_in, 16)
            sp.dma_start(wk[:, :, :], chunked(Wk)).then_inc(weights_in, 16)
            if hd == 16:
                for a in range(4):
                    sp.wait_ge(zeroed, 1)
                    sp.dma_start(wo[32 * a:32 * a + 16, :, :],
                                 Wo.rearrange("(n a d) m -> a d n m", a=4, d=16)[a]).then_inc(weights_in, 16)
            else:
                sp.dma_start(wo[:, :, :], chunked(Wo)).then_inc(weights_in, 16)
            if Wv is not None:
                sp.dma_start(wv[:, :, :], chunked(Wv)).then_inc(weights_in, 16)
            if bq is not None:
                sp.dma_start(bqT[:, :], bq).then_inc(weights_in, 16)
            if bk is not None:
                sp.dma_start(bkT[:, :], bk).then_inc(weights_in, 16)
            if bv is not None:
                sp.dma_start(bv_bc[:, :], bv.unsqueeze(0).to_broadcast([128, VW])).then_inc(weights_in, 16)
            for b in range(2):
                load_keys(sp, b, b)
                load_rest(sp, b, b)

        def prepare(pool):
            if hd == 16:
                pool.memset(wo[:, :, :], 0.0).then_inc(zeroed, 1)
                pool.memset(q[:, :, :, :, :], 0.0).then_inc(zeroed, 1)
                pool.memset(k[:, :, :, :], 0.0).then_inc(zeroed, 1)

        layernorm_phase(nc, tag + "n", X, XT, ident, fetch=fetch, prepare=prepare)
        P = m.sb("P", [S, 4, SK])
        PT = m.sb("PT", [KP, 2, KT, S])
        yT = m.sb("yT", [128, 2, NB, S])
        raw = m.sb("raw", [128, 2, SK])
        q_parts = m.sb("q_parts", [128, 2, C, S], F16)
        k_parts = m.sb("k_parts", [128, 2, C, SK], F16)
        s_bank = [m.bank("s0"), m.bank("s1")]
        t_bank = [m.bank("t0"), m.bank("t1")]
        y_bank = [m.bank("y0"), m.bank("y1")]
        p_bank = [m.bank("p0"), m.bank("p1")]

        with nc.Block() as block:
            @block.sync
            def _(sp):
                def stack(b, u):
                    if not (isinstance(b, int) and b < 2):
                        sp.wait_ge(stack_in[u], 16 * NSLOT * (b // 2) if isinstance(b, int) else (b - u) * (8 * NSLOT))
                        sp.sem_inc(sp_waited, 1)
                    sp.wait_ge(parts_made, QK * (b + 1))
                    rows = lambda d: d[u].rearrange("n (c p) s -> p n c s", p=128)
                    for part in range(2):
                        sp.dma_start(rows(q_dram)[:, part], q_parts[:, part, :, :]).then_inc(parts_out, 16)
                        sp.dma_start(rows(k_dram)[:, part], k_parts[:, part, :, :]).then_inc(parts_out, 16)
                    sp.wait_ge(parts_out, (b + 1) * 64)
                    sp.sem_inc(sp_waited, 1)
                    if not (isinstance(b, int) and b < 2):
                        sp.wait_ge(scored, H * (b - 1))
                    elif hd == 16:
                        sp.wait_ge(zeroed, 3)
                    for dram, out, slots in ((q_dram, q, q_slots), (k_dram, k, k_slots)):
                        heads = dram[u].rearrange("n (h d) s -> n d h s", d=hd)
                        for n, p0, h0, by, part in slots:
                            if out is q:
                                dst = q[p0:p0 + hd, u, n, h0::by, :]
                            else:
                                dst = k[p0:p0 + hd, u, :, :]
                            sp.dma_start(dst, heads[part][:, h0::by, :]).then_inc(stack_in[u], 16)

                def body(b, u):
                    if split:
                        sp.wait_ge(kc_split, b - 1)
                    else:
                        sp.wait_ge(projected, NP * (b - 1))
                    sp.sem_inc(sp_waited, 1)
                    load_keys(sp, b, u)
                    stack(b - 1, 1 - u)
                    if mask is not None:
                        sp.wait_ge(mask_made, b - 1)
                        sp.sem_inc(sp_waited, 1)
                    load_rest(sp, b, u)

                stack(0, 0)
                body(2, 0)
                body(3, 1)
                with sp.Fori(2, B // 2) as i:
                    body(i * 2, 0)
                    body(i * 2 + 1, 1)
                stack(B - 1, 1)

            @block.gpsimd
            def _(pool):
                def part(b, n):
                    kind, c, _ = kv[n]
                    width, parts = (S, q_parts) if kind == "q" else (SK, k_parts)
                    pool.wait_ge(evacuated, NP * b + n + 1)
                    pool.tensor_tensor(parts[:, LO, c, :], raw[:, n % 2, 0:width], parts[:, HI, c, :],
                                       ALU.subtract).then_inc(parts_made, 1)

                def scale_P(b, u, h):
                    pool.wait_ge(inv_done, H * b + h + 1)
                    pool.sem_inc(pool_waited, 1)
                    pool.tensor_scalar(P[:, h % 4, :], P[:, h % 4, :], inv[:, u, h:h + 1], 1.0,
                                       ALU.mult, ALU.mult).then_inc(P_done, 1)

                def low(b, u):
                    pool.wait_ge(kc_hi, b + 1)
                    pool.tensor_tensor(kc16[:, u, LO, :, :], kc[:, u, :, :], kc16[:, u, HI, :, :],
                                       ALU.subtract).then_inc(kc_split, 1)

                def body(b, u):
                    for h in range(H):
                        if h == QK_STEP - 2 and split and not (isinstance(b, int) and b >= B - 2):
                            low(b + 2, u)
                        if h == 12:
                            pool.tensor_tensor(X[:, b, :], X[:, b, :], bo_bc[:, :], ALU.add).then_inc(biased, 1)
                        if h < H - 2:
                            scale_P(b, u, h + 2)
                        elif not last(b):
                            scale_P(b + 1, 1 - u, h + 2 - H)
                        if h > 0:
                            for b2, n in units(b, h - 1):
                                if n < QK:
                                    part(b2, n)
                        elif not first(b):
                            for b2, n in units(b - 1, H - 1):
                                if n < QK:
                                    part(b2, n)

                pool.wait_ge(weights_in, 16 * n_weights)
                if split:
                    low(0, 0)
                if bq is not None:
                    pool.tensor_scalar(bqT[:, :], bqT[:, :], scale, None, ALU.mult).then_inc(bias_scaled, 1)
                for n in range(QK):
                    part(0, n)
                if split:
                    low(1, 1)
                for n in range(QK):
                    part(1, n)
                scale_P(0, 0, 0)
                scale_P(0, 0, 1)
                bodies(pool, body)

            @block.scalar
            def _(act):
                def evacuate(b, u, n):
                    kind, c, w = kv[n]
                    act.wait_ge(projected, NP * b + n + 1)
                    src = p_bank[n % 2]
                    if kind != "v":
                        if not (first(b) and n < 2):
                            act.wait_ge(parts_made, QK * b + n - 1)
                        width, by = (S, scale) if kind == "q" else (SK, 1.0 / WS if split else 1.0)
                        bias = bqT if kind == "q" else bkT
                        if n == 0 and not first(b):
                            act.wait_ge(parts_out, b * 64)
                        parts = q_parts if kind == "q" else k_parts
                        for dst in (parts[:, HI, c, :], raw[:, n % 2, 0:width]):
                            if bias is not None:
                                mv = act.activation(dst, src[:, 0:width], ACT.Identity, bias=bias[:, c:c + 1], scale=by)
                            else:
                                mv = act.mul(dst, src[:, 0:width], by)
                        mv.then_inc(evacuated, 1)
                    elif bv is None:
                        if not (isinstance(b, int) and b < 2):
                            act.wait_ge(av_done, H * (b - 1))
                        act.mul(v[:, u, c, w * VN:(w + 1) * VN], src[0:KP, 0:VN], 1.0 / WS).then_inc(evacuated, 1)

                def high(b, u):
                    act.wait_ge(kc_in[u], 16 * (b // 2) + 16 if isinstance(b, int) else (b - u) * 8 + 16)
                    if not (isinstance(b, int) and b < 2):
                        act.wait_ge(projected, NP * (b - 1))
                    act.copy(kc16[:, u, HI, :, :], kc[:, u, :, :]).then_inc(kc_hi, 1)

                def exp(b, u, h):
                    act.wait_ge(least_done, H * b + h + 1)
                    if not (first(b) and h < 4):
                        act.wait_ge(turned, H * b + h - 3)
                    src = s_bank[h % 2][0:S, 0:SK] if mask is None else masked[:, h % 2, :]
                    act.activation(P[:, h % 4, :], src, ACT.Exp, bias=least[:, u, h:h + 1], scale=-1.0,
                                   accum_out=total[:, u, h:h + 1]).then_inc(exp_done, 1)

                def take_y(b, u, hf):
                    act.wait_ge(av_done, H * b + 8 * hf + 8)
                    if not (first(b) or (isinstance(b, int) and b == 1)) and hf == 0:
                        act.wait_ge(out_done, b - 1)
                    act.copy(yT[:, u, hf * half:(hf + 1) * half, :],
                             y_bank[hf][:, 0:half * S].rearrange("p (n s) -> p n s", n=half)).then_inc(y_done, 1)

                def body(b, u):
                    for h in range(H):
                        if h == QK_STEP - 2 and split and not (isinstance(b, int) and b >= B - 2):
                            high(b + 2, u)
                        if h < H - 3:
                            exp(b, u, h + 3)
                        elif not last(b):
                            exp(b + 1, 1 - u, h + 3 - H)
                        for b2, n in units(b, h):
                            if not (kv[n][0] == "v" and bv is not None):
                                evacuate(b2, 1 - u if n >= QK else u, n)
                        if h == 1 and not first(b):
                            take_y(b - 1, 1 - u, 1)
                        if h == 9:
                            take_y(b, u, 0)

                if bq is not None:
                    act.wait_ge(bias_scaled, 1)
                act.wait_ge(weights_in, 16 * n_weights)
                if split:
                    high(0, 0)
                    act.mul(wk16[:, HI, :, :], wk[:, :, :], WS).then_inc(w_hi, 1)
                    act.mul(wv16[:, HI, :, :], wv[:, :, :], WS).then_inc(w_hi, 1)
                for n in range(NP):
                    if not (kv[n][0] == "v" and bv is not None):
                        evacuate(0, 0, n)
                if split:
                    high(1, 1)
                for n in range(QK):
                    evacuate(1, 1, n)
                for h in range(3):
                    exp(0, 0, h)
                bodies(act, body)
                take_y(B - 1, 1, 1)

            @block.vector
            def _(dve):
                def make_mask(b, u):
                    dve.wait_ge(mask_in[u], 16 * (b // 2) + 16 if isinstance(b, int) else (b - u) * 8 + 16)
                    if mask_kind == "per_query":
                        dve.tensor_scalar(mask_add[:, u, :], mask_raw[:, u, :], BIG, None, ALU.mult).then_inc(mask_made, 1)
                    else:
                        dve.tensor_scalar(mask_add[:, u, :], mask_raw[:, u, :], 0, BIG, ALU.is_equal,
                                          ALU.mult).then_inc(mask_made, 1)

                def value_bias(b, u, n):
                    _, j, w = kv[n]
                    dve.wait_ge(projected, NP * b + n + 1)
                    if not (isinstance(b, int) and b < 2):
                        dve.wait_ge(av_done, H * (b - 1))
                    dve.tensor_tensor(v[:, u, j, w * VN:(w + 1) * VN], p_bank[n % 2][0:KP, 0:VN],
                                      bv_bc[0:KP, w * VN:(w + 1) * VN], ALU.add).then_inc(evacuated, 1)

                def least_of(b, u, h):
                    dve.wait_ge(scored, H * b + h + 1)
                    if mask is None:
                        dve.tensor_reduce(least[:, u, h:h + 1], s_bank[h % 2][0:S, 0:SK], AX.X,
                                          ALU.min).then_inc(least_done, 1)
                        return
                    if h == 0:
                        dve.wait_ge(mask_made, b + 1)
                    if not (first(b) and h < 2):
                        dve.wait_ge(exp_done, H * b + h - 1)
                    dve.sem_inc(dve_waited, 1)
                    dve.tensor_tensor_reduce(masked[:, h % 2, :], s_bank[h % 2][0:S, 0:SK], mask_add[:, u, :], 1.0,
                                             3e38, ALU.add, ALU.min, least[:, u, h:h + 1]).then_inc(least_done, 1)

                def invert(b, u, h):
                    dve.wait_ge(exp_done, H * b + h + 1)
                    dve.reciprocal(inv[:, u, h:h + 1], total[:, u, h:h + 1]).then_inc(inv_done, 1)

                def take_PT(b, u, h):
                    dve.wait_ge(turned, H * b + h + 1)
                    if not (first(b) and h < 2):
                        dve.wait_ge(av_done, H * b + h - 1)
                    dve.tensor_copy(PT[:, h % 2, :, :],
                                    t_bank[h % 2][0:KP, 0:KT * S].rearrange("p (j s) -> p j s", j=KT)).then_inc(PT_done, 1)

                def add_out(b, u):
                    dve.wait_ge(out_done, b + 1)
                    dve.wait_ge(biased, b + 1)
                    dve.tensor_tensor(X[:, b, :], p_bank[1][0:S, 0:D], X[:, b, :], ALU.add).then_inc(x_done, 1)

                def body(b, u):
                    for h in range(H):
                        if mask is not None and h == 2 and not last(b):
                            make_mask(b + 1, 1 - u)
                        if h < H - 3:
                            least_of(b, u, h + 3)
                        elif not last(b):
                            least_of(b + 1, 1 - u, h + 3 - H)
                        if h < H - 2:
                            invert(b, u, h + 2)
                        elif not last(b):
                            invert(b + 1, 1 - u, h + 2 - H)
                        for b2, n in units(b, h):
                            if kv[n][0] == "v" and bv is not None:
                                value_bias(b2, 1 - u, n)
                        take_PT(b, u, h)
                        if h == OUT_STEP + 1 and not first(b):
                            add_out(b - 1, 1 - u)

                dve.memset(y_bank[0][:, :], 0.0).then_inc(x_done, 1)
                dve.memset(y_bank[1][:, :], 0.0).then_inc(x_done, 1)
                if split:
                    dve.wait_ge(weights_in, 16 * n_weights)
                    for n, (w, w16) in enumerate(((wk, wk16), (wv, wv16))):
                        dve.wait_ge(w_hi, n + 1)
                        dve.scalar_tensor_tensor(w16[:, LO, :, :], w[:, :, :], WS, w16[:, HI, :, :], ALU.mult,
                                                 ALU.subtract).then_inc(w_split, 1)
                if mask is not None:
                    make_mask(0, 0)
                for n in range(NP):
                    if kv[n][0] == "v" and bv is not None:
                        value_bias(0, 0, n)
                for h in range(3):
                    least_of(0, 0, h)
                invert(0, 0, 0)
                invert(0, 0, 1)
                bodies(dve, body)
                add_out(B - 1, 1)
                dve.wait_ge(x_done, 2 + B)

            @block.tensor
            def _(pe):
                def project(b, u, n):
                    kind, c, w = kv[n]
                    out = p_bank[n % 2]
                    if n == 0:
                        pe.wait_ge(kc_in[u], 16 * (b // 2) + 16 if isinstance(b, int) else (b - u) * 8 + 16)
                        if not first(b):
                            pe.wait_ge(evacuated, NP * b)
                        if not first(b) and not (isinstance(b, int) and b == 1):
                            pe.wait_ge(x_done, b)
                    elif kind == "v" and bv is not None and kv[n - 1][0] == "k":
                        pe.wait_ge(evacuated, NP * b + n)
                    elif n >= 2:
                        pe.wait_ge(evacuated, NP * b + n - 1)
                    if split and kind != "q":
                        pe.wait_ge(w_split, 1 + (kind == "v"))
                        pe.wait_ge(kc_split, b + 1)
                        n_mm = 0
                        for x, z in PARTS:
                            for i in range(DC):
                                flags = dict(start=n_mm == 0, stop=n_mm == len(PARTS) * DC - 1)
                                if kind == "k":
                                    mm = pe.matmul(out[:, 0:SK], wk16[:, z, i, c * 128:(c + 1) * 128],
                                                   kc16[:, u, x, i, :], **flags)
                                else:
                                    mm = pe.matmul(out[0:KP, 0:VN], kc16[:, u, x, i, c * KP:(c + 1) * KP],
                                                   wv16[:, z, i, w * VN:(w + 1) * VN], **flags)
                                n_mm += 1
                        mm.then_inc(projected, 1)
                        return
                    for i in range(DC):
                        if kind == "q":
                            mm = pe.matmul(out[:, 0:S], wq[:, i, c * 128:(c + 1) * 128],
                                           XT[:, i, bass.ds(b * S, S)], start=i == 0, stop=i == DC - 1)
                        elif kind == "k":
                            mm = pe.matmul(out[:, 0:SK], wk[:, i, c * 128:(c + 1) * 128], kc[:, u, i, :],
                                           start=i == 0, stop=i == DC - 1)
                        else:
                            mm = pe.matmul(out[0:KP, 0:VN], kc[:, u, i, c * KP:(c + 1) * KP],
                                           wv[:, i, w * VN:(w + 1) * VN], start=i == 0, stop=i == DC - 1)
                    mm.then_inc(projected, 1)

                def score(b, u, h):
                    if h == 0:
                        pe.wait_ge(stack_in[u], 16 * NSLOT * (b // 2 + 1) if isinstance(b, int) else (b - u + 2) * (8 * NSLOT))
                    if not (first(b) and h < 2):
                        pe.wait_ge(exp_done if mask is None else least_done, H * b + h - 1)
                    for n in range(NPASS):
                        mm = pe.matmul(s_bank[h % 2][0:S, 0:SK], q[:, u, NPASS - 1 - n, h, :], k[:, u, h * KH // H, :],
                                       start=n == 0, stop=n == NPASS - 1)
                    mm.then_inc(scored, 1)

                def turn(b, u, h):
                    pe.wait_ge(P_done, H * b + h + 1)
                    if not (first(b) and h < 2):
                        pe.wait_ge(PT_done, H * b + h - 1)
                    for j in range(KT):
                        mm = pe.transpose(t_bank[h % 2][0:KP, j * S:(j + 1) * S],
                                          P[:, h % 4, j * KP:(j + 1) * KP], ident[0:S, 0:S])
                    mm.then_inc(turned, 1)

                def weigh(b, u, h):
                    pe.wait_ge(PT_done, H * b + h + 1)
                    if h == 0:
                        pe.wait_ge(evacuated, NP * (b + 1))
                    if h == 0 and ctx is not None:
                        pe.wait_ge(v_in[u], 16 * (b // 2) + 16 if isinstance(b, int) else (b - u) * 8 + 16)
                    if h % 8 == 0 and not first(b):
                        pe.wait_ge(y_done, 2 * b - 1 + h // 8)
                    p0, blk = step * (h % HB), (h % 8) // HB
                    for j in range(KT):
                        mm = pe.matmul(y_bank[h // 8][p0:p0 + hd, blk * S:(blk + 1) * S],
                                       v[:, u, j, h * hd:(h + 1) * hd], PT[:, h % 2, j, :],
                                       start=j == 0, stop=j == KT - 1)
                    mm.then_inc(av_done, 1)

                def out_product(b, u):
                    pe.wait_ge(y_done, 2 * b + 2)
                    if last(b):
                        pe.wait_ge(x_done, 2 + B - 1)
                    else:
                        pe.wait_ge(evacuated, NP * B if isinstance(b, int) and b == B - 2 else NP * (b + 3))
                    for n in range(NB):
                        mm = pe.matmul(p_bank[1][0:S, 0:D], yT[:, u, n, :], wo[:, n, :], start=n == 0, stop=n == NB - 1)
                    mm.then_inc(out_done, 1)

                def body(b, u):
                    for h in range(H):
                        if h < H - 3:
                            score(b, u, h + 3)
                        elif not last(b):
                            score(b + 1, 1 - u, h + 3 - H)
                        todo = [(b2, 1 - u if n >= QK else u, n) for b2, n in units(b, h)]
                        if todo:
                            project(*todo.pop(0))
                        turn(b, u, h)
                        if h > 0:
                            weigh(b, u, h - 1)
                        elif not first(b):
                            weigh(b - 1, 1 - u, H - 1)
                        for unit in todo:
                            project(*unit)
                        if h == OUT_STEP and not first(b):
                            out_product(b - 1, 1 - u)

                pe.wait_ge(weights_in, 16 * n_weights)
                pe.wait_ge(x_done, 2)
                for n in range(NP):
                    project(0, 0, n)
                for n in range(QK):
                    project(1, 1, n)
                for h in range(3):
                    score(0, 0, h)
                bodies(pe, body)
                weigh(B - 1, 1, H - 1)
                out_product(B - 1, 1)


def linear_attention_phase(nc, tag, X, XT, ident, ctxT, WqT, WkT, projT, Wv, Wo):
    DH, M, EPS = 64, 128, 1e-3
    RATIO = 1.0 / float(np.sqrt(M))
    NPAIR = H // 2
    KN = H * M // 512
    VN = H * DH // 512
    VC = DH + 1
    units = [("k", j, n) for j in range(KT) for n in range(KN)] + \
            [("v", j, n) for j in range(KT) for n in range(VN)] + [("q", g, 0) for g in range(H // 4)]
    NU, NK, NV = len(units), KT * KN, KT * VN
    with ExitStack() as st:
        m = Mem(nc, st, tag)
        wkf = m.sb("wkf", [128, 2, DC, H * M], F16)
        wv16 = m.sb("wv16", [128, 2, DC, H * DH], F16)
        wqf = m.sb("wqf", [128, 2, DC, H * M], F16)
        XT16 = m.sb("XT16", [128, 2, DC, B * S], F16)
        wv = m.sb("wv", [128, DC, H * DH])
        wo = m.sb("wo", [128, NPAIR, D])
        kc = m.sb("kc", [128, 2, DC, SK])
        kc16 = m.sb("kc16", [128, 2, 2, DC, SK], F16)
        kvs = m.sb("kvs", [128, H, VC])
        rden = m.sb("rden", [128, 4 * S])
        attT = m.sb("attT", [128, NPAIR, S])
        fold_in, proj_zero, proj_in, folded, fold_evac = (
            m.sem(n) for n in ("fold_in", "proj_zero", "proj_in", "folded", "fold_evac"))
        x_hi, x_split = m.sem("x_hi"), m.sem("x_split")
        weights_in, fold_low, wv_split = m.sem("weights_in"), m.sem("fold_low"), m.sem("wv_split")
        kc_hi, kc_split = m.sem("kc_hi"), m.sem("kc_split")
        k_hi, k_low, v_low = m.sem("k_hi"), m.sem("k_low"), m.sem("v_low")
        kc_in = [m.sem("kc_in0"), m.sem("kc_in1")]
        ones_made, unit_done, k_evac, v_evac, q_evac = (
            m.sem(n) for n in ("ones", "unit", "k_evac", "v_evac", "q_evac"))
        kvs_done, kvs_evac, nd_done, rden_done, att_done, out_done, x_done = (
            m.sem(n) for n in ("kvs_done", "kvs_evac", "nd", "rden", "att", "out", "x_done"))

        with ExitStack() as st2:
            m2 = Mem(nc, st2, tag + "_fold")
            wT = m2.sb("wT", [128, 2, NPAIR, D])
            pp = m2.sb("pp", [128, 2 * M])

            def fetch(sp):
                sp.dma_start(wT[:, 0, :, :], chunked(WkT)).then_inc(fold_in, 16)
                sp.dma_start(wT[:, 1, :, :], chunked(WqT)).then_inc(fold_in, 16)
                sp.wait_ge(proj_zero, 1)
                sp.dma_start(pp[0:DH, 0:M], projT).then_inc(proj_in, 16)
                sp.dma_start(pp[DH:2 * DH, M:2 * M], projT).then_inc(proj_in, 16)
                sp.dma_start(wv[:, :, :], chunked(Wv)).then_inc(weights_in, 16)
                sp.dma_start(wo[:, :, :], chunked(Wo)).then_inc(weights_in, 16)
                sp.dma_start(kc[:, 0, :, :], ctxT[0].rearrange("(c p) s -> p c s", p=128)).then_inc(kc_in[0], 16)
                sp.dma_start(kc[:, 1, :, :], ctxT[1].rearrange("(c p) s -> p c s", p=128)).then_inc(kc_in[1], 16)

            def prepare(pool):
                pool.memset(pp[:, :], 0.0).then_inc(proj_zero, 1)

            layernorm_phase(nc, tag + "n", X, XT, ident, fetch=fetch, prepare=prepare)
            u_bank = [m.bank(f"u{i}") for i in range(4)]
            kvs_bank = [m.bank("kvs0"), m.bank("kvs1")]
            num_bank, den_bank = m.bank("num"), m.bank("den")
            with nc.Block() as block:
                @block.gpsimd
                def _(pool):
                    pool.wait_ge(x_hi, 1)
                    pool.tensor_tensor(XT16[:, LO, :, :], XT[:, :, :], XT16[:, HI, :, :], ALU.subtract).then_inc(x_split, 1)

                @block.tensor
                def _(pe):
                    pe.wait_ge(fold_in, 32)
                    pe.wait_ge(proj_in, 32)
                    n = 0
                    for w in range(2):
                        for pr in range(NPAIR):
                            for c in range(DC):
                                if n >= 4:
                                    pe.wait_ge(fold_evac, n - 3)
                                    pe.wait_ge(fold_low, n - 3)
                                pe.matmul(u_bank[n % 4][:, 0:2 * M], wT[:, w, pr, c * 128:(c + 1) * 128], pp[:, :],
                                          start=True, stop=True).then_inc(folded, 1)
                                n += 1

                @block.scalar
                def _(act):
                    act.copy(XT16[:, HI, :, :], XT[:, :, :]).then_inc(x_hi, 1)
                    n = 0
                    for w in range(2):
                        for pr in range(NPAIR):
                            for c in range(DC):
                                act.wait_ge(folded, n + 1)
                                cols = slice(pr * 2 * M, (pr + 1) * 2 * M)
                                act.mul((wkf, wqf)[w][:, HI, c, cols], u_bank[n % 4][:, 0:2 * M],
                                        RATIO * WS).then_inc(fold_evac, 1)
                                n += 1
                    act.wait_ge(weights_in, 32)
                    act.mul(wv16[:, HI, :, :], wv[:, :, :], WS).then_inc(fold_evac, 1)
                    act.wait_ge(fold_evac, n + 1)

                @block.vector
                def _(dve):
                    n = 0
                    for wf in (wkf, wqf):
                        for pr in range(NPAIR):
                            for c in range(DC):
                                dve.wait_ge(fold_evac, n + 1)
                                cols = slice(pr * 2 * M, (pr + 1) * 2 * M)
                                dve.scalar_tensor_tensor(wf[:, LO, c, cols], u_bank[n % 4][:, 0:2 * M], RATIO * WS,
                                                         wf[:, HI, c, cols], ALU.mult, ALU.subtract).then_inc(fold_low, 1)
                                n += 1
                    dve.wait_ge(fold_evac, n + 1)
                    dve.scalar_tensor_tensor(wv16[:, LO, :, :], wv[:, :, :], WS, wv16[:, HI, :, :], ALU.mult,
                                             ALU.subtract).then_inc(wv_split, 1)

        kp = m.sb("kp", [KP, 4, 512])
        kp16 = m.sb("kp16", [KP, 2, KT, H * M], F16)
        v16 = m.sb("v16", [KP, 2, KT, H, VC], F16)
        qp = m.sb("qp", [128, 2, H, S])

        def bodies(eng, body):
            body(0, 0)
            with eng.Fori(0, (B - 2) // 2) as i:
                body(i * 2 + 1, 1)
                body(i * 2 + 2, 0)
            body(B - 1, 1)

        first = lambda b: isinstance(b, int) and b == 0
        last = lambda b: isinstance(b, int) and b == B - 1

        with nc.Block() as block:
            @block.sync
            def _(sp):
                def body(b, u):
                    sp.wait_ge(kc_split, b - 1)
                    sp.dma_start(kc[:, u, :, :], ctxT[b].rearrange("(c p) s -> p c s", p=128)).then_inc(kc_in[u], 16)
                with sp.Fori(1, B // 2) as i:
                    body(i * 2, 0)
                    body(i * 2 + 1, 1)

            @block.gpsimd
            def _(pool):
                pool.memset(v16[:, HI, :, :, DH:VC], 1.0).then_inc(ones_made, 1)
                pool.memset(v16[:, LO, :, :, DH:VC], 0.0).then_inc(ones_made, 1)

                def low(b, u):
                    pool.wait_ge(kc_hi, b + 1)
                    pool.tensor_tensor(kc16[:, u, LO, :, :], kc[:, u, :, :], kc16[:, u, HI, :, :],
                                       ALU.subtract).then_inc(kc_split, 1)

                def feature_low(b, u, n):
                    _, j, w = units[n]
                    pool.wait_ge(k_hi, NK * b + n + 1)
                    pool.tensor_tensor(kp16[:, LO, j, w * 512:(w + 1) * 512], kp[:, n % 4, :],
                                       kp16[:, HI, j, w * 512:(w + 1) * 512],
                                       ALU.subtract).then_inc(k_low, 1)

                def body(b, u):
                    for n in range(NK):
                        feature_low(b, u, n)
                    if not last(b):
                        low(b + 1, 1 - u)

                low(0, 0)
                bodies(pool, body)

            @block.scalar
            def _(act):
                def high(b, u):
                    act.wait_ge(kc_in[u], 16 * (b // 2) + 16 if isinstance(b, int) else (b - u) * 8 + 16)
                    if not (isinstance(b, int) and b < 2):
                        act.wait_ge(unit_done, NU * (b - 2) + NK + NV)
                    act.copy(kc16[:, u, HI, :, :], kc[:, u, :, :]).then_inc(kc_hi, 1)

                def body(b, u):
                    if not last(b):
                        high(b + 1, 1 - u)
                    for n in range(NK):
                        _, j, w = units[n]
                        act.wait_ge(k_evac, NK * b + n + 1)
                        if n == 0 and not first(b):
                            act.wait_ge(kvs_done, 4 * b)
                        act.copy(kp16[:, HI, j, w * 512:(w + 1) * 512], kp[:, n % 4, :]).then_inc(k_hi, 1)
                    for n in range(NK, NK + NV):
                        _, j, w = units[n]
                        act.wait_ge(unit_done, NU * b + n + 1)
                        act.mul(v16[:, HI, j, w * 8:(w + 1) * 8, 0:DH],
                                u_bank[(u * NU + n) % 4][0:KP, 0:512].rearrange("p (h d) -> p h d", d=DH),
                                1.0 / WS).then_inc(v_evac, 1)
                    for g in range(H // 4):
                        act.wait_ge(kvs_done, 4 * b + g + 1)
                        act.copy(kvs[:, 4 * g:4 * g + 4, :],
                                 kvs_bank[g % 2][:, 0:4 * VC].rearrange("p (h d) -> p h d", d=VC)).then_inc(kvs_evac, 1)
                high(0, 0)
                bodies(act, body)

            @block.vector
            def _(dve):
                def take(b, u, n, dst, rows, cols, sem, ws=1.0):
                    if sem is k_evac and not (first(b) and n < 4):
                        dve.wait_ge(k_low, NK * b + n - 3)
                    dve.wait_ge(unit_done, NU * b + n + 1)
                    dve.tensor_scalar(dst, u_bank[(u * NU + n) % 4][0:rows, 0:cols], 0.0, EPS * ws, ALU.max,
                                      ALU.add).then_inc(sem, 1)

                def divide(b, u, hf):
                    dve.wait_ge(nd_done, 2 * b + hf + 1)
                    if not (first(b) and hf == 0):
                        dve.wait_ge(att_done, 2 * b + hf)
                    dve.reciprocal(rden[:, :], den_bank[:, 0:4 * S]).then_inc(rden_done, 1)
                    dve.wait_ge(rden_done, 2 * b + hf + 1)
                    dve.tensor_tensor(attT[:, 4 * hf:4 * hf + 4, :], num_bank[:, 0:4 * S].rearrange("p (n s) -> p n s", s=S),
                                      rden[:, :].rearrange("p (n s) -> p n s", s=S), ALU.mult).then_inc(att_done, 1)

                def add_out(b):
                    dve.wait_ge(out_done, b + 1)
                    dve.tensor_tensor(X[:, b, :], num_bank[0:S, 0:D], X[:, b, :], ALU.add).then_inc(x_done, 1)

                def body(b, u):
                    for n in range(NK):
                        _, j, w = units[n]
                        if n == NK // 2 and not first(b):
                            divide(b - 1, 1 - u, 0)
                        take(b, u, n, kp[:, n % 4, :], KP, 512, k_evac, WS)
                    if not first(b):
                        divide(b - 1, 1 - u, 1)
                    for n in range(NK, NK + NV):
                        _, j, w = units[n]
                        dve.wait_ge(v_evac, NV * b + n - NK + 1)
                        dve.scalar_tensor_tensor(v16[:, LO, j, w * 8:(w + 1) * 8, 0:DH],
                                                 u_bank[(u * NU + n) % 4][0:KP, 0:512].rearrange("p (h d) -> p h d", d=DH),
                                                 1.0 / WS, v16[:, HI, j, w * 8:(w + 1) * 8, 0:DH], ALU.mult,
                                                 ALU.subtract).then_inc(v_low, 1)
                    if not first(b):
                        add_out(b - 1)
                    for g in range(H // 4):
                        take(b, u, NK + NV + g, qp[:, u, 4 * g:4 * g + 4, :].rearrange("p n s -> p (n s)"),
                             128, 4 * S, q_evac, WS)
                bodies(dve, body)
                divide(B - 1, 1, 0)
                divide(B - 1, 1, 1)
                add_out(B - 1)
                dve.wait_ge(x_done, B)

            @block.tensor
            def _(pe):
                def evacuated(b, n):
                    if n < 0:
                        b, n = b - 1, n + NU
                    kind = units[n][0]
                    if kind == "k":
                        pe.wait_ge(k_evac, NK * b + n + 1)
                    elif kind == "v":
                        pe.wait_ge(v_low, NV * b + n - NK + 1)
                    else:
                        pe.wait_ge(q_evac, (H // 4) * b + n - NK - NV + 1)

                def unit(b, u, n):
                    kind, j, w = units[n]
                    if n == 0:
                        pe.wait_ge(kc_split, b + 1)
                    if not (first(b) and n < 4):
                        evacuated(b, n - 4)
                    out = u_bank[(u * NU + n) % 4]
                    if kind == "q":
                        for hh in range(4):
                            h = 4 * j + hh
                            n_mm = 0
                            for a, z in PARTS:
                                for c in range(DC):
                                    mm = pe.matmul(out[:, hh * S:(hh + 1) * S], wqf[:, z, c, h * M:(h + 1) * M],
                                                   XT16[:, a, c, bass.ds(b * S, S)], start=n_mm == 0,
                                                   stop=n_mm == len(PARTS) * DC - 1)
                                    n_mm += 1
                    else:
                        wt = wkf if kind == "k" else wv16
                        n_mm = 0
                        for a, z in PARTS:
                            for c in range(DC):
                                mm = pe.matmul(out[0:KP, 0:512], kc16[:, u, a, c, j * KP:(j + 1) * KP],
                                               wt[:, z, c, w * 512:(w + 1) * 512], start=n_mm == 0,
                                               stop=n_mm == len(PARTS) * DC - 1)
                                n_mm += 1
                    mm.then_inc(unit_done, 1)

                def sum_keys(b, u):
                    pe.wait_ge(k_low, NK * (b + 1))
                    pe.wait_ge(v_low, NV * (b + 1))
                    for g in range(H // 4):
                        if g >= 2:
                            pe.wait_ge(kvs_evac, 4 * b + g - 1)
                        elif not first(b):
                            pe.wait_ge(kvs_evac, 4 * b + g - 1)
                        for hh in range(4):
                            h = 4 * g + hh
                            n_mm = 0
                            for a, z in PARTS:
                                for j in range(KT):
                                    mm = pe.matmul(kvs_bank[g % 2][:, hh * VC:(hh + 1) * VC],
                                                   kp16[:, a, j, h * M:(h + 1) * M], v16[:, z, j, h, :],
                                                   start=n_mm == 0, stop=n_mm == len(PARTS) * KT - 1)
                                    n_mm += 1
                        mm.then_inc(kvs_done, 1)

                def num_den(b, u, hf):
                    pe.wait_ge(kvs_evac, 4 * b + 2 * hf + 2)
                    pe.wait_ge(q_evac, 4 * b + 2 * hf + 2)
                    if not first(b) or hf == 1:
                        pe.wait_ge(att_done, 2 * b + hf)
                    if hf == 0 and not first(b):
                        pe.wait_ge(x_done, b)
                    for pr in range(4):
                        for which in range(2):
                            for side in range(2):
                                h = 8 * hf + 2 * pr + side
                                lhs = kvs[:, h, 0:DH] if which == 0 else kvs[:, h, DH:VC].to_broadcast([128, DH])
                                mm = pe.matmul((num_bank, den_bank)[which][side * DH:(side + 1) * DH, pr * S:(pr + 1) * S],
                                               lhs, qp[:, u, h, :], start=True, stop=True)
                    mm.then_inc(nd_done, 1)

                def out_product(b):
                    pe.wait_ge(att_done, 2 * b + 2)
                    for n in range(NPAIR):
                        mm = pe.matmul(num_bank[0:S, 0:D], attT[:, n, :], wo[:, n, :], start=n == 0, stop=n == NPAIR - 1)
                    mm.then_inc(out_done, 1)

                def body(b, u):
                    for n in range(NK):
                        if n == NK // 2 and not first(b):
                            num_den(b - 1, 1 - u, 0)
                        unit(b, u, n)
                    if not first(b):
                        num_den(b - 1, 1 - u, 1)
                    for n in range(NK, NK + NV):
                        unit(b, u, n)
                    if not first(b):
                        out_product(b - 1)
                    for n in range(NK + NV, NU):
                        unit(b, u, n)
                    sum_keys(b, u)

                pe.wait_ge(weights_in, 32)
                pe.wait_ge(wv_split, 1)
                pe.wait_ge(fold_low, 2 * NPAIR * DC)
                pe.wait_ge(x_split, 1)
                pe.wait_ge(ones_made, 2)
                bodies(pe, body)
                num_den(B - 1, 1, 0)
                num_den(B - 1, 1, 1)
                out_product(B - 1)


def router_phase(nc, tag, X, XT, gates, ident, iota8, kind, b2, Wr=None, bias=None, cent=None,
                 rw1=None, rb1=None, hots=None, weights=None, xn=None, add_xn=False):
    LW = 2 * E if kind == "cos" else E
    with ExitStack() as st:
        m = Mem(nc, st, tag)
        wr = m.sb("wr", [128, DC, LW])
        if weights is None:
            b2s = m.sb("b2s", [E, D])
        logits = m.sb("logits", [S, B, E])
        lt = m.sb("lt", [128, GW])
        best = m.sb("best", [S, B, 8])
        where = m.sb("where", [S, B, 8], U32)
        wheref = m.sb("wheref", [S, B, 8])
        hot = m.sb("hot", [S, B, E])
        hot1 = m.sb("hot1", [S, B, E]) if hots is None else hots[0]
        hot2 = m.sb("hot2", [S, B, E]) if hots is None or kind != "two" else hots[1]
        ex = m.sb("ex", [S, B, E])
        total = m.sb("total", [S, B])
        gT = m.sb("gT", [E, B, S])
        weights_in, added, logits_done, link, exp_done, sub_done, gates_done = (
            m.sem(n) for n in ("weights_in", "added", "logits", "link", "exp", "sub", "gates"))
        gt_turned, gt_evac, out_done, x_done = (m.sem(n) for n in ("gt", "gt_evac", "out", "x_done"))
        c_sq, c_norm, c_scaled, c_turned, c_in, x_sq, x_norm = (
            m.sem(n) for n in ("c_sq", "c_norm", "c_scaled", "c_turned", "c_in", "x_sq", "x_norm"))
        hid, hid_evac = m.sem("hid"), m.sem("hid_evac")
        n_in = 2 if weights is None else 1
        if bias is not None:
            bias_bc = m.sb("bias_bc", [S, E])
            n_in += 1
        if kind == "cos":
            cn = m.sb("cn", [E, D])
            cjunk = m.sb("cjunk", [E, D])
            cstat = m.sb("cstat", [E, 3])
            xjunk = m.sb("xjunk", [S, 2, D])
            xstat = m.sb("xstat", [S, 3, B])
            both = m.sb("both", [S, B, LW])
            n_in += 1
        if kind == "two":
            w1 = m.sb("w1", [128, DC, D])
            b1 = m.sb("b1", [128, DC])
            hidden = m.sb("hidden", [128, DC, B * S])
            n_in += 2

        def fetch(sp):
            if weights is None:
                sp.dma_start(b2s[:, :], b2).then_inc(weights_in, 16)
            sp.dma_start(wr[:, :, LW - E:LW], chunked(Wr)).then_inc(weights_in, 16)
            if bias is not None:
                sp.dma_start(bias_bc[:, :], bias.unsqueeze(0).to_broadcast([S, E])).then_inc(weights_in, 16)
            if kind == "cos":
                sp.dma_start(cn[:, :], cent).then_inc(weights_in, 16)
            if kind == "two":
                sp.dma_start(w1[:, :, :], chunked(rw1)).then_inc(weights_in, 16)
                sp.dma_start(b1[:, :], rb1).then_inc(weights_in, 16)

        layernorm_phase(nc, tag + "n", X, XT, ident, xn=xn, fetch=fetch)
        bank = m.bank("logits_ps")
        gt_bank = [m.bank(f"gt{i}") for i in range(4)]
        ob = [m.bank(f"ob{i}") for i in range(2)]
        extra = m.bank("extra")
        lt_bank = gt_bank[0] if kind == "cos" else extra
        lt_zeroed, lt_done, lt_out = m.sem("lt_zeroed"), m.sem("lt_done"), m.sem("lt_out")
        with nc.Block() as block:
            if add_xn:
                @block.gpsimd
                def _(pool):
                    for t in range(B):
                        pool.tensor_tensor(X[:, t, :], X[:, t, :], xn[:, t, :], ALU.add).then_inc(added, 1)
                    pool.wait_ge(added, B)

            @block.tensor
            def _(pe):
                pe.wait_ge(weights_in, 16 * n_in)
                if kind == "cos":
                    pe.wait_ge(c_scaled, 1)
                    for c in range(DC):
                        mm = pe.transpose(extra[:, c * E:(c + 1) * E], cn[:, c * 128:(c + 1) * 128], ident[0:E, 0:E])
                    mm.then_inc(c_turned, 1)
                    pe.wait_ge(c_in, 1)
                    for t in range(B):
                        if t >= 2:
                            pe.wait_ge(x_sq, t - 1)
                        for c in range(DC):
                            mm = pe.transpose(ob[t % 2][0:S, c * 128:(c + 1) * 128], XT[:, c, t * S:(t + 1) * S], ident[:, :])
                        mm.then_inc(out_done, 1)
                src = XT
                if kind == "two":
                    src = hidden
                    n = 0
                    for g in range(G):
                        for f in range(DC):
                            if n >= 4:
                                pe.wait_ge(hid_evac, n - 3)
                            for c in range(DC):
                                mm = pe.matmul(gt_bank[n % 4][:, 0:GW], w1[:, c, f * 128:(f + 1) * 128],
                                               XT[:, c, g * GW:(g + 1) * GW], start=c == 0, stop=c == DC - 1)
                            mm.then_inc(hid, 1)
                            n += 1
                    pe.wait_ge(hid_evac, n)
                pe.wait_ge(lt_zeroed, 1)
                for c in range(DC):
                    for g in range(G):
                        mm = pe.matmul(lt_bank[32 * g:32 * g + LW, 0:GW], wr[:, c, :], src[:, c, g * GW:(g + 1) * GW],
                                       start=c == 0, stop=c == DC - 1)
                mm.then_inc(lt_done, 1)
                pe.wait_ge(lt_out, 1)
                for t in range(GT):
                    mm = pe.transpose(bank[0:S, t * 128:(t + 1) * 128], lt[:, t * S:(t + 1) * S], ident[:, :])
                mm.then_inc(logits_done, 1)
                if weights is not None:
                    return
                pe.wait_ge(gates_done, 1)
                for g in range(G):
                    for t in range(GT):
                        mm = pe.transpose(gt_bank[g][0:E, t * S:(t + 1) * S], gates[:, :, g * GT + t], ident[0:S, 0:S])
                    mm.then_inc(gt_turned, 1)
                if kind == "cos":
                    pe.wait_ge(x_sq, B)
                for t in range(B):
                    if t % GT == 0:
                        pe.wait_ge(gt_evac, t // GT + 1)
                    if t >= 2:
                        pe.wait_ge(x_done, t - 1)
                    pe.matmul(ob[t % 2][0:S, 0:D], gT[:, t, :], b2s[:, :], start=True, stop=True).then_inc(out_done, 1)

            @block.scalar
            def _(act):
                if kind == "cos":
                    act.wait_ge(c_sq, 1)
                    act.activation(cstat[:, 1:2], cstat[:, 0:1], ACT.Sqrt).then_inc(c_norm, 1)
                    act.wait_ge(c_turned, 1)
                    act.copy(wr[:, :, 0:E], extra[:, 0:DC * E].rearrange("p (c e) -> p c e", e=E)).then_inc(c_in, 1)
                    for t in range(B):
                        act.wait_ge(out_done, t + 1)
                        act.activation(xjunk[:, t % 2, :], ob[t % 2][0:S, 0:D], ACT.Square,
                                       accum_out=xstat[:, 0, t:t + 1]).then_inc(x_sq, 1)
                    act.wait_ge(lt_done, 1)
                    act.copy(lt[:, :], lt_bank[:, 0:GW]).then_inc(lt_out, 1)
                    act.wait_ge(x_sq, B)
                    act.activation(xstat[:, 1, :], xstat[:, 0, :], ACT.Sqrt).then_inc(x_norm, 1)
                if kind == "two":
                    act.wait_ge(weights_in, 16 * n_in)
                    for n in range(G * DC):
                        g, f = divmod(n, DC)
                        act.wait_ge(hid, n + 1)
                        act.activation(hidden[:, f, g * GW:(g + 1) * GW], gt_bank[n % 4][:, 0:GW], ACT.Silu,
                                       bias=b1[:, f:f + 1]).then_inc(hid_evac, 1)
                if kind != "one":
                    act.wait_ge(sub_done, 1)
                    act.activation(ex[:, :, :], ex[:, :, :], ACT.Exp).then_inc(exp_done, 1)
                for g in range(G if weights is None else 0):
                    act.wait_ge(gt_turned, g + 1)
                    act.copy(gT[:, g * GT:(g + 1) * GT, :],
                             gt_bank[g][0:E, 0:GW].rearrange("p (t s) -> p t s", t=GT)).then_inc(gt_evac, 1)

            @block.vector
            def _(dve):
                count = [0]

                def step(ins):
                    count[0] += 1
                    ins.then_inc(link, 1)
                    dve.wait_ge(link, count[0])

                def wide(a):
                    return a.to_broadcast([S, B, E])

                dve.memset(lt_bank[:, :], 0.0).then_inc(lt_zeroed, 1)
                dve.wait_ge(weights_in, 16 * n_in)
                if kind == "cos":
                    dve.tensor_tensor_reduce(cjunk[:, :], cn[:, :], cn[:, :], 1.0, 0.0, ALU.mult, ALU.add,
                                             cstat[:, 0:1]).then_inc(c_sq, 1)
                    dve.wait_ge(c_norm, 1)
                    step(dve.tensor_scalar(cstat[:, 1:2], cstat[:, 1:2], 1e-12, None, ALU.max))
                    step(dve.reciprocal(cstat[:, 2:3], cstat[:, 1:2]))
                    dve.tensor_scalar(cn[:, :], cn[:, :], cstat[:, 2:3], None, ALU.mult).then_inc(c_scaled, 1)
                    dve.wait_ge(x_norm, 1)
                    step(dve.tensor_scalar(xstat[:, 1, :], xstat[:, 1, :], 1e-12, None, ALU.max))
                    step(dve.reciprocal(xstat[:, 2, :], xstat[:, 1, :]))
                if kind != "cos":
                    dve.wait_ge(lt_done, 1)
                    dve.tensor_copy(lt[:, :], lt_bank[:, 0:GW]).then_inc(lt_out, 1)
                dve.wait_ge(logits_done, 1)
                tokens = bank[0:S, :].rearrange("s (t g l) -> s g t l", t=GT, l=32)
                grouped = lambda x: x.rearrange("s (g t) l -> s g t l", t=GT)
                if kind == "cos":
                    step(dve.tensor_copy(grouped(both[:, :, :]), tokens[:, :, :, 0:LW]))
                    step(dve.tensor_tensor(logits[:, :, :], both[:, :, 0:E], wide(xstat[:, 2, :].unsqueeze(2)), ALU.mult))
                    step(dve.tensor_tensor(logits[:, :, :], logits[:, :, :], both[:, :, E:LW], ALU.add))
                elif bias is not None:
                    step(dve.tensor_tensor(grouped(logits[:, :, :]), tokens[:, :, :, 0:E],
                                           bias_bc[:, :].unsqueeze(1).unsqueeze(1).to_broadcast([S, G, GT, E]), ALU.add))
                else:
                    step(dve.tensor_copy(grouped(logits[:, :, :]), tokens[:, :, :, 0:E]))
                for t in range(B):
                    ins = dve.max(best[:, t, :], logits[:, t, :])
                step(ins)
                if kind == "cos":
                    step(dve.tensor_tensor(hot[:, :, :], logits[:, :, :], wide(best[:, :, 1:2]), ALU.is_ge))
                else:
                    for t in range(B):
                        ins = dve.max_index(where[:, t, :], best[:, t, :], logits[:, t, :])
                    step(ins)
                    step(dve.tensor_copy(wheref[:, :, :], where[:, :, :]))
                    lane = iota8[0:S, :].unsqueeze(1).to_broadcast([S, B, E])
                    step(dve.tensor_tensor(hot1[:, :, :], lane, wide(wheref[:, :, 0:1]), ALU.is_equal))
                    if kind == "two":
                        step(dve.tensor_tensor(hot2[:, :, :], lane, wide(wheref[:, :, 1:2]), ALU.is_equal))
                        step(dve.tensor_tensor(hot[:, :, :], hot1[:, :, :], hot2[:, :, :], ALU.add))
                    else:
                        step(dve.tensor_copy(hot[:, :, :], hot1[:, :, :]))
                out = gates[:, :, :].rearrange("s e b -> s b e")
                if kind == "one":
                    dve.tensor_copy(out, hot[:, :, :]).then_inc(gates_done, 1)
                else:
                    dve.tensor_tensor(ex[:, :, :], logits[:, :, :], wide(best[:, :, 0:1]), ALU.subtract).then_inc(sub_done, 1)
                    dve.wait_ge(exp_done, 1)
                    if kind != "prob":
                        step(dve.tensor_tensor(ex[:, :, :], ex[:, :, :], hot[:, :, :], ALU.mult))
                    step(dve.tensor_reduce(total[:, :], ex[:, :, :], AX.X, ALU.add))
                    step(dve.reciprocal(total[:, :], total[:, :]))
                    dve.tensor_tensor(out, (hot if kind == "prob" else ex)[:, :, :], wide(total[:, :].unsqueeze(2)),
                                      ALU.mult).then_inc(gates_done, 1)
                if weights is not None:
                    dve.wait_ge(gates_done, 1)
                    for n, w in enumerate(weights):
                        step(dve.tensor_tensor(ex[:, :, :], out, (hot1, hot2)[n][:, :, :], ALU.mult))
                        step(dve.tensor_reduce(w[:, :], ex[:, :, :], AX.X, ALU.add))
                    return
                base = B if kind == "cos" else 0
                for t in range(B):
                    dve.wait_ge(out_done, base + t + 1)
                    dve.tensor_tensor(X[:, t, :], ob[t % 2][0:S, 0:D], X[:, t, :], ALU.add).then_inc(x_done, 1)
                dve.wait_ge(x_done, B)


def ffn_phase(nc, tag, X, XT, gates, W1, b1, W2, F, func):
    FC = F // 128
    NH = 2
    HR = 4
    with ExitStack() as st:
        m = Mem(nc, st, tag)
        w1 = m.sb("w1", [128, 2, DC, F])
        w2 = m.sb("w2", [128, 2, FC, D])
        b1s = m.sb("b1s", [128, 2, FC])
        h = m.sb("h", [128, NH, FC, GW])
        h_bank = [m.bank(f"h{i}") for i in range(HR)]
        o_bank = [m.bank(f"o{i}") for i in range(GT)]
        w_in = [m.sem("w_in0"), m.sem("w_in1")]
        h_done, h_evac, o_done, x_done = (m.sem(n) for n in ("h_done", "h_evac", "o_done", "x_done"))
        SG = 2 * G

        def turns(eng, body):
            body(0)
            with eng.Fori(1, E // 2) as i:
                body(i)

        with nc.Block() as block:
            @block.sync
            def _(sp):
                def load(i, u):
                    e = i * 2 + u
                    sp.dma_start(w1[:, u, :, :], W1[e].rearrange("(c p) f -> p c f", p=128)).then_inc(w_in[u], 16)
                    sp.dma_start(w2[:, u, :, :], W2[e].rearrange("(c p) f -> p c f", p=128)).then_inc(w_in[u], 16)
                    sp.dma_start(b1s[:, u, :], b1[e]).then_inc(w_in[u], 16)
                load(0, 0)
                load(0, 1)
                with sp.Fori(1, E // 2) as i:
                    for u in range(2):
                        sp.wait_ge(o_done, (i - 1) * SG * GT + (u + 1) * G * GT)
                        load(i, u)

            def peeled(i):
                return isinstance(i, int)

            @block.tensor
            def _(pe):
                def hidden(i, s):
                    u, g = divmod(s, G)
                    if g == 0:
                        pe.wait_ge(w_in[u], 48 * (i + 1))
                    for f in range(FC):
                        n = s * FC + f
                        if not (peeled(i) and n < HR):
                            pe.wait_ge(h_evac, i * SG * FC + n - HR + 1)
                        for c in range(DC):
                            mm = pe.matmul(h_bank[n % HR][:, 0:GW], w1[:, u, c, f * 128:(f + 1) * 128],
                                           XT[:, c, g * GW:(g + 1) * GW], start=c == 0, stop=c == DC - 1)
                        mm.then_inc(h_done, 1)

                def output(i, s):
                    u, g = divmod(s, G)
                    pe.wait_ge(h_evac, (i * SG + s + 1) * FC)
                    for t in range(GT):
                        if not (peeled(i) and s == 0):
                            pe.wait_ge(x_done, (i * SG + s - 1) * GT + t + 1)
                        for f in range(FC):
                            mm = pe.matmul(o_bank[t][0:S, 0:D], h[:, s % NH, f, t * S:(t + 1) * S], w2[:, u, f, :],
                                           start=f == 0, stop=f == FC - 1)
                        mm.then_inc(o_done, 1)

                def body(i):
                    for s in range(SG):
                        hidden(i, s)
                        if s > 0:
                            output(i, s - 1)
                        elif not peeled(i):
                            output_prev(i)

                def output_prev(i):
                    s = SG - 1
                    u, g = divmod(s, G)
                    pe.wait_ge(h_evac, i * SG * FC)
                    for t in range(GT):
                        pe.wait_ge(x_done, (i * SG - 2) * GT + t + 1)
                        for f in range(FC):
                            mm = pe.matmul(o_bank[t][0:S, 0:D], h[:, s % NH, f, t * S:(t + 1) * S], w2[:, u, f, :],
                                           start=f == 0, stop=f == FC - 1)
                        mm.then_inc(o_done, 1)

                turns(pe, body)
                output_prev(E // 2)

            @block.scalar
            def _(act):
                def body(i):
                    for s in range(SG):
                        u, g = divmod(s, G)
                        if not (peeled(i) and s < NH):
                            act.wait_ge(o_done, (i * SG + s - NH + 1) * GT)
                        for f in range(FC):
                            n = s * FC + f
                            act.wait_ge(h_done, i * SG * FC + n + 1)
                            act.activation(h[:, s % NH, f, :], h_bank[n % HR][:, 0:GW], func,
                                           bias=b1s[:, u, f:f + 1]).then_inc(h_evac, 1)
                act.wait_ge(w_in[0], 48)
                turns(act, body)

            @block.vector
            def _(dve):
                def body(i):
                    for s in range(SG):
                        u, g = divmod(s, G)
                        for t in range(GT):
                            b = g * GT + t
                            dve.wait_ge(o_done, (i * SG + s) * GT + t + 1)
                            if not (peeled(i) and s < G):
                                dve.wait_ge(x_done, (i * SG + s - G) * GT + t + 1)
                            dve.scalar_tensor_tensor(out=X[:, b, :], in0=o_bank[t][0:S, 0:D],
                                                     scalar=gates[:, :, :].rearrange("s e b -> s (e b)")[:, bass.ds((i * 2 + u) * B + b, 1)],
                                                     in1=X[:, b, :], op0=ALU.mult, op1=ALU.add).then_inc(x_done, 1)
                turns(dve, body)
                dve.wait_ge(x_done, E * B)


def dispatch_phase(nc, tag, X, gates, b2, ident, xn, hots, slots, tile_expert, xg, cleared, TS):
    K = len(hots)
    JMAX = B * S // TS
    with ExitStack() as st:
        m = Mem(nc, st, tag)
        before = m.sb("before", [S, S])
        ones = m.sb("ones", [S, S])
        hot = m.sb("hot", [S, B, E])
        tot = m.sb("tot", [S, B, E])
        cum = m.sb("cum", [S, B + 1, E])
        edges = m.sb("edges", [S, JMAX])
        index = m.sb("index", [S, NT])
        filled = m.sb("filled", [S, E, JMAX])
        tiles = m.sb("tiles", [S, E])
        start = m.sb("start", [S, E + 1])
        start_row = m.sb("start_row", [S, E])
        passed = m.sb("passed", [S, NT, E])
        expert = m.sb("expert", [S, NT])
        row = m.sb("row", [S, B, E])
        picked = m.sb("picked", [S, B, E])
        slotf = m.sb("slotf", [S, B])
        prefix_bank, total_bank = m.bank("prefix_ps"), m.bank("total_ps")
        b2s = m.sb("b2s", [E, D])
        gT = m.sb("gT", [E, B, S])
        gt_bank = [m.bank(f"gt{i}") for i in range(G)]
        ob = [m.bank(f"ob{i}") for i in range(2)]
        b2_in, gt_turned, gt_evac, out_done, x_done = (m.sem(n) for n in ("b2_in", "gt", "gt_evac", "out", "x_done"))
        made, tri, hot_done, counted, link, slots_done, sent = (
            m.sem(n) for n in ("made", "tri", "hot_done", "counted", "link", "slots_done", "sent"))
        with nc.Block() as block:
            @block.sync
            def _(sp):
                sp.dma_start(b2s[:, :], b2).then_inc(b2_in, 16)

            @block.scalar
            def _(act):
                for g in range(G):
                    act.wait_ge(gt_turned, g + 1)
                    act.copy(gT[:, g * GT:(g + 1) * GT, :],
                             gt_bank[g][0:E, 0:GW].rearrange("p (t s) -> p t s", t=GT)).then_inc(gt_evac, 1)

            @block.gpsimd
            def _(pool):
                pool.memset(before[:, :], 1.0).then_inc(tri, 1)
                pool.memset(ones[:, :], 1.0).then_inc(made, 1)
                pool.iota(edges[:, :], pattern=[[TS, JMAX]], base=0, channel_multiplier=0,
                          allow_small_or_imprecise_dtypes=True).then_inc(made, 1)
                pool.iota(index[:, :], pattern=[[1, NT]], base=0, channel_multiplier=0,
                          allow_small_or_imprecise_dtypes=True).then_inc(made, 1)
                pool.wait_ge(tri, 1)
                pool.affine_select(out=before[:, :], in_=before[:, :], compare_op=ALU.is_gt, fill=0.0, base=0,
                                   pattern=[[1, S]], channel_multiplier=-1).then_inc(made, 1)
                pool.wait_ge(cleared, 16 * (NT * 256 // 128 // ZR))
                for k in range(K):
                    pool.wait_ge(slots_done, k + 1)
                    for b in range(B):
                        pool.indirect_dma_start(
                            out=xg[:, :], out_offset=bass.IndirectOffsetOnAxis(ap=slots[k][:, b:b + 1], axis=0),
                            in_=xn[:, b, :], in_offset=None).then_inc(sent, 16)
                pool.wait_ge(sent, 16 * K * B)

            @block.tensor
            def _(pe):
                pe.wait_ge(made, 4)
                pe.wait_ge(hot_done, 1)
                pe.matmul(prefix_bank[0:S, 0:B * E], before[:, :], hot[:, :, :].rearrange("s b e -> s (b e)"),
                          start=True, stop=True).then_inc(counted, 1)
                pe.matmul(total_bank[0:S, 0:B * E], ones[:, :], hot[:, :, :].rearrange("s b e -> s (b e)"),
                          start=True, stop=True).then_inc(counted, 1)
                for g in range(G):
                    for t in range(GT):
                        mm = pe.transpose(gt_bank[g][0:E, t * S:(t + 1) * S], gates[:, :, g * GT + t], ident[0:S, 0:S])
                    mm.then_inc(gt_turned, 1)
                pe.wait_ge(b2_in, 16)
                for t in range(B):
                    if t % GT == 0:
                        pe.wait_ge(gt_evac, t // GT + 1)
                    if t >= 2:
                        pe.wait_ge(x_done, t - 1)
                    pe.matmul(ob[t % 2][0:S, 0:D], gT[:, t, :], b2s[:, :], start=True, stop=True).then_inc(out_done, 1)

            @block.vector
            def _(dve):
                count = [0]

                def step(ins):
                    count[0] += 1
                    ins.then_inc(link, 1)
                    dve.wait_ge(link, count[0])

                if K == 1:
                    dve.tensor_copy(hot[:, :, :], hots[0][:, :, :]).then_inc(hot_done, 1)
                else:
                    dve.tensor_tensor(hot[:, :, :], hots[0][:, :, :], hots[1][:, :, :], ALU.add).then_inc(hot_done, 1)
                dve.memset(start[:, 0:1], 0.0)
                step(dve.memset(cum[:, 0, :], 0.0))
                dve.wait_ge(counted, 2)
                step(dve.tensor_copy(tot[:, :, :], total_bank[0:S, 0:B * E].rearrange("s (b e) -> s b e", e=E)))
                for b in range(B):
                    step(dve.tensor_tensor(cum[:, b + 1, :], cum[:, b, :], tot[:, b, :], ALU.add))
                dve.wait_ge(made, 4)
                step(dve.tensor_tensor(filled[:, :, :], cum[:, B, :].unsqueeze(2).to_broadcast([S, E, JMAX]),
                                       edges[:, :].unsqueeze(1).to_broadcast([S, E, JMAX]), ALU.is_gt))
                step(dve.tensor_reduce(tiles[:, :], filled[:, :, :], AX.X, ALU.add))
                for e in range(E):
                    step(dve.tensor_tensor(start[:, e + 1:e + 2], start[:, e:e + 1], tiles[:, e:e + 1], ALU.add))
                step(dve.tensor_scalar(start_row[:, :], start[:, 0:E], float(TS), None, ALU.mult))
                step(dve.tensor_tensor(row[:, :, :], prefix_bank[0:S, 0:B * E].rearrange("s (b e) -> s b e", e=E),
                                       cum[:, 0:B, :], ALU.add))
                step(dve.tensor_tensor(row[:, :, :], row[:, :, :],
                                       start_row[:, :].unsqueeze(1).to_broadcast([S, B, E]), ALU.add))
                for k in range(K):
                    step(dve.tensor_tensor(picked[:, :, :], row[:, :, :], hots[k][:, :, :], ALU.mult))
                    step(dve.tensor_reduce(slotf[:, :], picked[:, :, :], AX.X, ALU.add))
                    dve.tensor_copy(slots[k][:, :], slotf[:, :]).then_inc(slots_done, 1)
                    dve.wait_ge(slots_done, k + 1)
                step(dve.tensor_tensor(passed[:, :, :], index[:, :].unsqueeze(2).to_broadcast([S, NT, E]),
                                       start[:, 1:E + 1].unsqueeze(1).to_broadcast([S, NT, E]), ALU.is_ge))
                step(dve.tensor_reduce(expert[:, :], passed[:, :, :], AX.X, ALU.add))
                step(dve.tensor_scalar(expert[:, :], expert[:, :], float(E - 1), None, ALU.min))
                step(dve.tensor_copy(tile_expert[:, :], expert[0:1, :]))
                for t in range(B):
                    dve.wait_ge(out_done, t + 1)
                    dve.tensor_tensor(X[:, t, :], ob[t % 2][0:S, 0:D], X[:, t, :], ALU.add).then_inc(x_done, 1)
                dve.wait_ge(x_done, B)


def experts_phase(nc, tag, xg, yg, tile_expert, ident, W1, b1, W2, F, func, TS):
    FC, MT, R = F // 128, TS // 128, 3
    TURNS = NT // R
    with ExitStack() as st:
        m = Mem(nc, st, tag)
        w1 = m.sb("w1", [128, R, DC, F])
        w2 = m.sb("w2", [128, R, FC, D])
        b1s = m.sb("b1s", [128, R, FC])
        xs = m.sb("xs", [128, R, MT, D])
        xT = m.sb("xT", [128, R, DC, TS])
        h = m.sb("h", [128, R, FC, TS])
        y = m.sb("y", [128, R, MT, D])
        t_bank = m.bank("t")
        h_bank = [m.bank(f"h{i}") for i in range(R)]
        o_bank = [m.bank(f"o{i}") for i in range(R)]
        w1_in = [m.sem(f"w1_in{i}") for i in range(R)]
        w2_in = [m.sem(f"w2_in{i}") for i in range(R)]
        xs_in = [m.sem(f"xs_in{i}") for i in range(R)]
        stored = [m.sem(f"stored{i}") for i in range(R)]
        turned, xT_done, h_done, h_evac, o_done, y_done = (
            m.sem(n) for n in ("turned", "xT", "h_done", "h_evac", "o_done", "y"))
        xg_t = xg.rearrange("(j p) d -> p j d", p=128)
        yg_t = yg.rearrange("(j p) d -> p j d", p=128)

        with nc.Block() as block:
            @block.sync
            def _(sp):
                def load(i, s):
                    j = i * R + s
                    wait_for(sp, turned, j - R + 1)
                    sp.dma_start(xs[:, s, :, :], xg_t[:, bass.ds(j * MT, MT), :]).then_inc(xs_in[s], 16)
                    e = sp.value_load(tile_expert[0:1, bass.ds(j, 1)], min_val=0, max_val=E - 1)
                    wait_for(sp, h_evac, (j - R + 1) * FC)
                    sp.dma_start(w1[:, s, :, :], W1[bass.ds(e, 1)].rearrange("o (c p) f -> p (o c) f", p=128)).then_inc(w1_in[s], 16)
                    sp.dma_start(b1s[:, s, :], b1[bass.ds(e, 1)].rearrange("o p f -> p (o f)")).then_inc(w1_in[s], 16)
                    wait_for(sp, o_done, (j - R + 1) * MT)
                    sp.dma_start(w2[:, s, :, :], W2[bass.ds(e, 1)].rearrange("o (c p) f -> p (o c) f", p=128)).then_inc(w2_in[s], 16)
                for s in range(R):
                    load(0, s)
                with sp.Fori(1, TURNS) as i:
                    for s in range(R):
                        load(i, s)

            @block.gpsimd
            def _(pool):
                with pool.Fori(0, TURNS) as i:
                    for s in range(R):
                        pool.wait_ge(y_done, (i * R + s + 1) * MT)
                        pool.dma_start(yg_t[:, bass.ds((i * R + s) * MT, MT), :], y[:, s, :, :]).then_inc(stored[s], 16)
                for s in range(R):
                    pool.wait_ge(stored[s], 16 * TURNS)

            def in_order(eng, turn, hidden, output):
                turn(0, 0)
                for i in (0, 1, TURNS - 1):
                    def body(i):
                        for s in range(R):
                            if s + 1 < R:
                                turn(i, s + 1)
                            elif not isinstance(i, int) or i < TURNS - 1:
                                turn(i + 1, 0)
                            hidden(i, s)
                            if s > 0:
                                output(i, s - 1)
                            elif not isinstance(i, int) or i > 0:
                                output(i - 1, R - 1)
                    if i == 1:
                        with eng.Fori(1, TURNS - 1) as k:
                            body(k)
                    else:
                        body(i)
                output(TURNS - 1, R - 1)

            @block.tensor
            def _(pe):
                def turn(i, s):
                    pe.wait_ge(xs_in[s], 16 * (i + 1))
                    wait_for(pe, xT_done, i * R + s)
                    for c in range(DC):
                        for t in range(MT):
                            mm = pe.transpose(t_bank[:, c * TS + t * 128:c * TS + (t + 1) * 128],
                                              xs[:, s, t, c * 128:(c + 1) * 128], ident[:, :])
                    mm.then_inc(turned, 1)

                def hidden(i, s):
                    pe.wait_ge(w1_in[s], 32 * (i + 1))
                    pe.wait_ge(xT_done, i * R + s + 1)
                    for f in range(FC):
                        n = s * FC + f
                        wait_for(pe, h_evac, i * R * FC + n - R + 1)
                        for c in range(DC):
                            mm = pe.matmul(h_bank[n % R][:, 0:TS], w1[:, s, c, f * 128:(f + 1) * 128],
                                           xT[:, s, c, :], start=c == 0, stop=c == DC - 1)
                        mm.then_inc(h_done, 1)

                def output(i, s):
                    pe.wait_ge(w2_in[s], 16 * (i + 1))
                    pe.wait_ge(h_evac, (i * R + s + 1) * FC)
                    for t in range(MT):
                        n = s * MT + t
                        wait_for(pe, y_done, i * R * MT + n - R + 1)
                        for f in range(FC):
                            mm = pe.matmul(o_bank[n % R][:, 0:D], h[:, s, f, t * 128:(t + 1) * 128], w2[:, s, f, :],
                                           start=f == 0, stop=f == FC - 1)
                        mm.then_inc(o_done, 1)

                in_order(pe, turn, hidden, output)

            @block.scalar
            def _(act):
                def body(i):
                    for s in range(R):
                        wait_for(act, o_done, (i * R + s - R + 1) * MT)
                        act.wait_ge(w1_in[s], 32 * (i + 1))
                        for f in range(FC):
                            n = s * FC + f
                            act.wait_ge(h_done, i * R * FC + n + 1)
                            act.activation(h[:, s, f, :], h_bank[n % R][:, 0:TS], func,
                                           bias=b1s[:, s, f:f + 1]).then_inc(h_evac, 1)
                body(0)
                with act.Fori(1, TURNS) as i:
                    body(i)

            @block.vector
            def _(dve):
                def turn(i, s):
                    dve.wait_ge(turned, i * R + s + 1)
                    wait_for(dve, h_done, (i * R + s - R + 1) * FC)
                    dve.tensor_copy(xT[:, s, :, :], t_bank[:, 0:DC * TS].rearrange("p (c t) -> p c t", c=DC)).then_inc(xT_done, 1)

                def output(i, s):
                    wait_for(dve, stored[s], 16 * i)
                    for t in range(MT):
                        dve.wait_ge(o_done, (i * R + s) * MT + t + 1)
                        dve.tensor_copy(y[:, s, t, :], o_bank[(s * MT + t) % R][:, 0:D]).then_inc(y_done, 1)

                in_order(dve, turn, lambda i, s: None, output)


def combine_phase(nc, tag, X, yg, slots, weights):
    K = len(slots)
    with ExitStack() as st:
        m = Mem(nc, st, tag)
        got = m.sb("got", [S, K * B, D])
        fetched = [m.sem(f"fetched{i}") for i in range(8)]
        x_done = m.sem("x_done")
        with nc.Block() as block:
            @block.gpsimd
            def _(pool):
                for n in range(K * B):
                    k, b = divmod(n, B)
                    pool.indirect_dma_start(
                        out=got[:, n, :], out_offset=None, in_=yg[:, :],
                        in_offset=bass.IndirectOffsetOnAxis(ap=slots[k][:, b:b + 1], axis=0)).then_inc(fetched[n % 8], 16)
                    if n >= 7:
                        pool.wait_ge(fetched[(n - 7) % 8], 16 * ((n - 7) // 8 + 1))

            @block.vector
            def _(dve):
                for n in range(K * B):
                    k, b = divmod(n, B)
                    dve.wait_ge(fetched[n % 8], 16 * (n // 8 + 1))
                    if k > 0:
                        dve.wait_ge(x_done, (k - 1) * B + b + 1)
                    dve.scalar_tensor_tensor(out=X[:, b, :], in0=got[:, n, :], scalar=weights[k][:, b:b + 1],
                                             in1=X[:, b, :], op0=ALU.mult, op1=ALU.add).then_inc(x_done, 1)
                dve.wait_ge(x_done, K * B)


def store_phase(nc, out, X, cleared):
    with ExitStack() as st:
        m = Mem(nc, st, "store")
        stored = m.sem("stored")
        with nc.Block() as block:
            @block.sync
            def _(sp):
                sp.dma_start(out.rearrange("b s d -> s b d"), X[:, :, :]).then_inc(stored, 16)
                sp.wait_ge(stored, 16)
                sp.wait_ge(cleared, 16 * (NT * 256 // 128 // ZR))


def build(nc, a, out, stop=8):
    with ExitStack() as st:
        m = Mem(nc, st, "all")
        X = m.sb("X", [S, B, D])
        XT = m.sb("XT", [128, DC, B * S])
        gates = m.sb("gates", [S, E, B])
        ident = m.sb("ident", [128, 128])
        iota8 = m.sb("iota8", [128, E])
        xg = nc.dram_tensor("rows", (NT * 256, D), F32, kind="Internal").ap()
        yg = nc.dram_tensor("expert_rows", (NT * 256, D), F32, kind="Internal").ap()
        zero, zeroed, cleared = m.sb("zero", [128, ZR * D]), m.sem("zeroed"), m.sem("cleared")
        load_phase(nc, a["x"], X, ident, iota8, zero, zeroed, cleared, xg)

        def scratch(hd):
            return [nc.dram_tensor(f"{n}_parts{hd}", (2, 2, H * hd, w), F16, kind="Internal").ap()
                    for n, w in (("q", S), ("k", SK))]

        scratch16, scratch64 = scratch(16), scratch(64)

        def sparse_ffn(t, kind, W1, b1, W2, b2, F, func, Wr, bias=None, add_xn=False, rw1=None, rb1=None):
            K, TS = (2, 256) if kind == "two" else (1, 128)
            with ExitStack() as st2:
                m2 = Mem(nc, st2, f"s{t}")
                slots = [m2.sb(f"slots{k}", [S, B], U32) for k in range(K)]
                weights = [m2.sb(f"weights{k}", [S, B]) for k in range(K)]
                tile_expert = m2.sb("tile_expert", [1, NT], U32)
                rows, rows_out = xg[0:NT * TS, :], yg[0:NT * TS, :]
                with ExitStack() as st3:
                    m3 = Mem(nc, st3, f"d{t}")
                    xn = m3.sb("xn", [S, B, D])
                    hots = [m3.sb(f"hots{k}", [S, B, E]) for k in range(K)]
                    router_phase(nc, f"r{t}", X, XT, gates, ident, iota8, kind, b2, Wr=Wr, bias=bias,
                                 rw1=rw1, rb1=rb1, hots=hots, weights=weights, xn=xn, add_xn=add_xn)
                    dispatch_phase(nc, f"p{t}", X, gates, b2, ident, xn, hots, slots, tile_expert, rows, cleared, TS)
                experts_phase(nc, f"f{t}", rows, rows_out, tile_expert, ident, W1, b1, W2, F, func, TS)
                combine_phase(nc, f"c{t}", X, rows_out, slots, weights)

        def sub0():
            attention_phase(nc, "a0", X, XT, ident, a["ctxT"], a["L0_WqT"], a["L0_WkT"], a["L0_WcT"], a["L0_xattn_bc"],
                            bq=a["L0_bq"], bk=a["L0_bk"], ctx=a["ctx_1024"], scratch=scratch16, hd=16)

        def sub1():
            sparse_ffn(1, "prob", a["L0_ffn_W1"], a["L0_b1"], a["L0_ffn_W2"], a["L0_ffn_b2"], 1024, ACT.Gelu,
                       a["L0_ffn_Wr"])

        def sub2():
            linear_attention_phase(nc, "a2", X, XT, ident, a["ctxT"], a["L1_WqT"], a["L1_WkT"], a["L1_projT"],
                                   a["L1_Wv"], a["L1_Wo"])

        def sub3():
            router_phase(nc, "r3", X, XT, gates, ident, iota8, "cos", a["L1_ffn_b2"], Wr=a["L1_wrT"],
                         cent=a["L1_ffn_centroids"])
            ffn_phase(nc, "f3", X, XT, gates, a["L1_ffn_w1"], a["L1_b1"], a["L1_ffn_w2"], 128, ACT.Gelu)

        def sub4():
            attention_phase(nc, "a4", X, XT, ident, a["ctxT"], a["L2_xattn_Wq"], a["L2_xattn_Wk"],
                            a["L2_xattn_Wo"], a["L2_xattn_bo"], Wv=a["L2_xattn_Wv"], scratch=scratch64, hd=64,
                            mask=a["mask_BxSxS2_bk1"], mask_kind="per_query")

        def sub5():
            sparse_ffn(5, "two", a["L2_ffn_ew1"], a["L2_b1"], a["L2_ffn_ew2"], a["L2_ffn_eb2"], 512, ACT.Silu,
                       a["L2_ffn_rw2"], bias=a["L2_ffn_rb2"], add_xn=True, rw1=a["L2_ffn_rw1"], rb1=a["L2_rb1"])

        def sub6():
            attention_phase(nc, "a6", X, XT, ident, a["ctxT"], a["L3_xattn_Wq"], a["L3_xattn_Wk"],
                            a["L3_xattn_Wo"], a["L3_xattn_bo"], bq=a["L3_bq"], bk=a["L3_bk"], Wv=a["L3_xattn_Wv"],
                            bv=a["L3_xattn_bv"], scratch=scratch16, hd=16, mask=a["mask_Bx1xS2_ik0"], mask_kind="per_key")

        def sub7():
            sparse_ffn(7, "one", a["L3_ffn_W1"], a["L3_b1"], a["L3_ffn_W2"], a["L3_ffn_b2"], 256, ACT.Gelu,
                       a["L3_ffn_Wg"], bias=a["L3_ffn_bg"])

        first_sub, stop = stop if isinstance(stop, tuple) else (0, stop)
        for sub in (sub0, sub1, sub2, sub3, sub4, sub5, sub6, sub7)[first_sub:stop]:
            sub()
        store_phase(nc, out, X, cleared)


def layout(inputs):
    a = {n: np.asarray(v) for n, v in inputs.items()}

    def columns(v):
        return v.reshape(-1, 128).T

    a["ctxT"] = a["ctx_1024"].transpose(0, 2, 1)
    for n in ("q", "k", "c"):
        a[f"L0_W{n}T"] = a.pop(f"L0_xattn_W{n}").T
    for n in ("q", "k"):
        a[f"L0_b{n}"] = columns(a.pop(f"L0_xattn_b{n}"))
        a[f"L3_b{n}"] = columns(a.pop(f"L3_xattn_b{n}"))
        a[f"L1_W{n}T"] = a.pop(f"L1_xattn_W{n}").transpose(1, 2, 0).reshape(1024, D)
    a["L2_rb1"] = columns(a.pop("L2_ffn_rb1"))
    a["L1_projT"] = a.pop("L1_xattn_proj").T
    a["L1_Wv"] = a.pop("L1_xattn_Wv").reshape(D, 1024)
    a["L1_Wo"] = a.pop("L1_xattn_Wo").reshape(1024, D)
    a["L1_wrT"] = a.pop("L1_ffn_w_route").T
    for layer, name in (("L0", "L0_ffn_b1"), ("L1", "L1_ffn_b1"), ("L2", "L2_ffn_eb1"), ("L3", "L3_ffn_b1")):
        b = a.pop(name)
        a[f"{layer}_b1"] = b.reshape(E, -1, 128).transpose(0, 2, 1)
    return {n: np.ascontiguousarray(v) for n, v in a.items()}


def declare(nc, arrays, stop=8):
    a = {n: nc.dram_tensor(f"in_{n}", v.shape, mybir.dt.from_np(v.dtype), kind="ExternalInput").ap()
         for n, v in arrays.items()}
    out = nc.dram_tensor("out", (B, S, D), F32, kind="ExternalOutput").ap()
    build(nc, a, out, stop)


def kernel(**inputs):
    import concourse.bacc as bacc
    from concourse.bass_utils import run_bass_kernel_spmd

    arrays = layout(inputs)
    nc = bacc.Bacc("TRN2", target_bir_lowering=False, num_devices=1)
    declare(nc, arrays)
    r = run_bass_kernel_spmd(nc, [{f"in_{n}": v for n, v in arrays.items()}], core_ids=[0])
    return r.results[0]["out"]
```
